# Optimizing a Trainium2 kernel written in Bass

```python
import numpy as np
import jax
import jax.numpy as jnp

def _softmax(x, axis=-1):
    return jax.nn.softmax(x, axis=axis)

def _gelu(x):
    return jax.nn.gelu(x, approximate=True)

def _silu(x):
    return jax.nn.silu(x)

def _sigmoid(x):
    return jax.nn.sigmoid(x)

def _layernorm(x, axis=-1, eps=1e-05):
    m = jnp.mean(x, axis=axis, keepdims=True)
    v = jnp.var(x, axis=axis, keepdims=True)
    return (x - m) / jnp.sqrt(v + eps)

def _scatter_add(tgt, idx, src, axis=0):
    return tgt.at[idx].add(src)

def _segment_sum(src, seg, n):
    return jax.ops.segment_sum(src, seg, n)
kernel_name = 'mk_perceiver_d1_seqx_r4_0cb857'

def setup_inputs(seed: int=0):
    np.random.seed(seed)
    _w = jnp.asarray

    def _rec_inputs():
        import jax
        import jax.numpy as jnp
        _rk = jax.random.key(seed)
        x = 7.22e-05 + 1 * jax.random.normal(jax.random.fold_in(_rk, 1), (128, 32, 256), jnp.float32)
        _lenS = 32 - jax.random.randint(jax.random.fold_in(_rk, 7), (128,), 0, max(1, 32 // 4) + 1, jnp.int32)
        _lenS2 = 257 - jax.random.randint(jax.random.fold_in(_rk, 8), (128,), 0, max(1, 257 // 4) + 1, jnp.int32)
        _ctx_1024P = jax.random.normal(jax.random.fold_in(_rk, 11), (128, 16, 256), jnp.float32)
        _ctx_1024c = jax.random.dirichlet(jax.random.fold_in(_rk, 511), 0.3 * jnp.ones((16,), jnp.float32), (128, 257))
        _ctx_1024t = jnp.einsum('bsk,bkd->bsd', _ctx_1024c, _ctx_1024P)
        _ctx_1024t = _ctx_1024t * jax.lax.rsqrt(jnp.mean(jnp.square(_ctx_1024t)) + 1e-12) * 0.953939
        ctx_1024 = 4.13588e-05 + 0.999923 * (_ctx_1024t + 0.3 * jax.random.normal(jax.random.fold_in(_rk, 611), (128, 257, 256), jnp.float32))
        return (x, ctx_1024)
    x, ctx_1024 = _rec_inputs()

    def _L0_xattn_setup():
        import jax, jax.numpy as jnp
        import numpy as np
        EMBED_DIM = 256
        B, QL, KL = (4, 512, 512)
        key = jax.random.key(seed)
        k1, k2, k3, k4 = jax.random.split(key, 4)
        hidden_states = jax.random.normal(k1, (B, QL, EMBED_DIM), dtype=jnp.float32)
        decoder_hidden_states = jax.random.normal(k2, (B, KL, EMBED_DIM), dtype=jnp.float32)
        Wq = jax.random.normal(k3, (EMBED_DIM, EMBED_DIM), dtype=jnp.float32) * (1.0 / np.sqrt(EMBED_DIM))
        Wkv = jax.random.normal(k4, (EMBED_DIM, 2 * EMBED_DIM), dtype=jnp.float32) * (1.0 / np.sqrt(EMBED_DIM))
        return {'hidden_states': hidden_states, 'decoder_hidden_states': decoder_hidden_states, 'Wq': Wq, 'Wkv': Wkv}
    _L0_xattn_all = _L0_xattn_setup()
    _L0_xattn_in = {k: v for k, v in _L0_xattn_all.items() if k in ('Wq', 'Wkv')}
    del _L0_xattn_all

    def _L0_attn_setup():
        import jax, jax.numpy as jnp
        import numpy as np
        GAMMA = 0.96875
        key = jax.random.key(seed)
        kx, kq, kk, kv = jax.random.split(key, 4)
        B, T, D = (4, 512, 256)
        x = jax.random.normal(kx, (B, T, D), dtype=jnp.float32)
        Wq = jax.random.normal(kq, (D, D), dtype=jnp.float32) * (1.0 / np.sqrt(D))
        Wk = jax.random.normal(kk, (D, D), dtype=jnp.float32) * (1.0 / np.sqrt(D))
        Wv = jax.random.normal(kv, (D, D), dtype=jnp.float32) * (1.0 / np.sqrt(D))
        return {'x': x, 'Wq': Wq, 'Wk': Wk, 'Wv': Wv}
    _L0_attn_all = _L0_attn_setup()
    _L0_attn_in = {k: v for k, v in _L0_attn_all.items() if k in ('Wq', 'Wk', 'Wv')}
    del _L0_attn_all

    def _L0_ffn_setup():
        import jax, jax.numpy as jnp
        import numpy as np
        D_MODEL = 256
        D_FF = 1024
        N_ZONES = 8
        TOP_K = 3
        ROUTER_H = 64
        BATCH = 16
        SEQ = 512
        key = jax.random.key(seed)
        ks = jax.random.split(key, 8)
        s = lambda *dims: 1.0 / np.sqrt(dims[-2] if len(dims) > 1 else dims[-1])
        x = jax.random.normal(ks[0], (BATCH, SEQ, D_MODEL), dtype=jnp.float32)
        W1 = jax.random.normal(ks[1], (D_MODEL, ROUTER_H), dtype=jnp.float32) / np.sqrt(D_MODEL)
        b1 = jnp.zeros((ROUTER_H,), dtype=jnp.float32)
        W2 = jax.random.normal(ks[2], (ROUTER_H, N_ZONES), dtype=jnp.float32) / np.sqrt(ROUTER_H)
        b2 = jnp.zeros((N_ZONES,), dtype=jnp.float32)
        Wa = jax.random.normal(ks[3], (N_ZONES, D_MODEL, D_FF), dtype=jnp.float32) / np.sqrt(D_MODEL)
        Wb = jax.random.normal(ks[4], (N_ZONES, D_FF, D_MODEL), dtype=jnp.float32) / np.sqrt(D_FF)
        return {'x': x, 'W1': W1, 'b1': b1, 'W2': W2, 'b2': b2, 'Wa': Wa, 'Wb': Wb}
    _L0_ffn_all = _L0_ffn_setup()
    _L0_ffn_in = {k: v for k, v in _L0_ffn_all.items() if k in ('W1', 'b1', 'W2', 'b2', 'Wa', 'Wb')}
    del _L0_ffn_all
    return {'x': x, 'ctx_1024': ctx_1024, 'L0_xattn_Wq': _L0_xattn_in['Wq'], 'L0_xattn_Wkv': _L0_xattn_in['Wkv'], 'L0_attn_Wq': _L0_attn_in['Wq'], 'L0_attn_Wk': _L0_attn_in['Wk'], 'L0_attn_Wv': _L0_attn_in['Wv'], 'L0_ffn_W1': _L0_ffn_in['W1'], 'L0_ffn_b1': _L0_ffn_in['b1'], 'L0_ffn_W2': _L0_ffn_in['W2'], 'L0_ffn_b2': _L0_ffn_in['b2'], 'L0_ffn_Wa': _L0_ffn_in['Wa'], 'L0_ffn_Wb': _L0_ffn_in['Wb']}

def reference(x, ctx_1024, L0_xattn_Wq, L0_xattn_Wkv, L0_attn_Wq, L0_attn_Wk, L0_attn_Wv, L0_ffn_W1, L0_ffn_b1, L0_ffn_W2, L0_ffn_b2, L0_ffn_Wa, L0_ffn_Wb):
    import jax
    import jax.numpy as jnp

    def _L0_xattn_ref(hidden_states, decoder_hidden_states, Wq, Wkv):
        import jax, jax.numpy as jnp
        import numpy as np
        EMBED_DIM = 256
        B, QL, KL = (4, 512, 512)
        d = Wq.shape[0]
        scale = 1.0 / np.sqrt(d)
        query = hidden_states @ Wq
        kv = decoder_hidden_states @ Wkv
        key, value = jnp.split(kv, 2, axis=-1)
        scores = jnp.einsum('bqd,bkd->bqk', query, key) * scale
        w = jax.nn.softmax(scores, axis=-1)
        return jnp.einsum('bqk,bkd->bqd', w, value)

    def _L0_attn_ref(x, Wq, Wk, Wv):
        import jax, jax.numpy as jnp
        import numpy as np
        GAMMA = 0.96875
        B, T, _ = x.shape
        D = Wq.shape[1]
        Q = jnp.einsum('bti,id->btd', x, Wq)
        K = jnp.einsum('bti,id->btd', x, Wk)
        V = jnp.einsum('bti,id->btd', x, Wv)
        gamma = jnp.asarray(GAMMA, x.dtype)
        m = jnp.einsum('btd,bt->td', K, V.sum(axis=-1))

        def step(s, mt):
            s_new = gamma * s + mt
            return (s_new, s_new)
        _, states = jax.lax.scan(step, jnp.zeros((D,), x.dtype), m[1:])
        S = jnp.concatenate([states[:1], states], axis=0)
        S = S.reshape(-1, T).T
        return S[None, :, :] * Q

    def _L0_ffn_ref(x, W1, b1, W2, b2, Wa, Wb):
        import jax, jax.numpy as jnp
        import numpy as np
        D_MODEL = 256
        D_FF = 1024
        N_ZONES = 8
        TOP_K = 3
        ROUTER_H = 64
        BATCH = 16
        SEQ = 512
        pooled = x.mean(axis=1)
        h = jnp.tanh(pooled @ W1 + b1)
        logits = h @ W2 + b2
        probs = jax.nn.softmax(logits, axis=-1)
        top_p, top_i = jax.lax.top_k(probs, TOP_K)
        top_w = top_p / top_p.sum(axis=-1, keepdims=True)
        onehot = jax.nn.one_hot(top_i, N_ZONES, dtype=x.dtype)
        w = jnp.einsum('bk,bke->be', top_w, onehot)
        zone_outputs = jnp.zeros_like(x)
        for e in range(N_ZONES):
            z = jax.nn.gelu(x @ Wa[e]) @ Wb[e]
            zone_outputs = zone_outputs + z * w[:, e, None, None]
        return x + zone_outputs
    x = x + _L0_xattn_ref(_layernorm(x, axis=-1), ctx_1024, L0_xattn_Wq, L0_xattn_Wkv)
    x = x + _L0_attn_ref(_layernorm(x, axis=-1), L0_attn_Wq, L0_attn_Wk, L0_attn_Wv)
    x = x + _L0_ffn_ref(_layernorm(x, axis=-1), L0_ffn_W1, L0_ffn_b1, L0_ffn_W2, L0_ffn_b2, L0_ffn_Wa, L0_ffn_Wb)
    return x

_drawn_inputs = setup_inputs


def setup_inputs(seed=0):
    import zlib

    import numpy as np

    out = dict(_drawn_inputs(seed))
    spreads = {'L0_ffn_b1': (0.0, 2.0), 'L0_ffn_b2': (0.0, 2.0)}
    factors = {'L0_ffn_W1': 23.738, 'L0_ffn_W2': 23.265, 'L0_ffn_Wa': 26.295, 'L0_ffn_Wb': 21.697}
    for name, (base, spread) in spreads.items():
        noise = np.random.default_rng([zlib.crc32(name.encode()), seed]).standard_normal(out[name].shape)
        drawn = base * np.exp(spread * noise) if base else spread * noise
        out[name] = jnp.asarray(drawn.astype(out[name].dtype))
    for name, factor in factors.items():
        out[name] = (out[name] * factor).astype(out[name].dtype)
    return out
```

```python
from contextlib import ExitStack

import concourse.bass as bass
from concourse import mybir

F32 = mybir.dt.float32
I32 = mybir.dt.int32
ALU = mybir.AluOpType
ACT = mybir.ActivationFunctionType
AX = mybir.AxisListType
ds = bass.ds

P = 128
B, T, D = 128, 32, 256
KEYS = 257
DC = D // P
GB = P // T
NG = B // GB
NR = 4
EPS = 1e-5
SCALE = 1.0 / 16.0
GAMMA = 0.96875
E, TOP, HID, FF = 8, 3, 64, 1024
FC = FF // P
SLOTS = 16
TILES = (TOP * B + E * (SLOTS - 1)) // SLOTS
NSLOT = TILES * SLOTS
PAD = SLOTS * T


def wait_for(eng, sem, count):
    if isinstance(count, int) and count <= 0:
        return
    eng.wait_ge(sem, count)


def wait_alone(eng, sem, count, seen):
    if isinstance(count, int) and count <= 0:
        return
    eng.wait_ge(sem, count)
    eng.sem_inc(seen, 1)


def constants(nc, new, m):
    m.ident = new.sb("ident", [P, P])
    m.ones = new.sb("ones", [P, P])
    m.batch_mask = new.sb("batch_mask", [P, GB])
    m.time_mask = new.sb("time_mask", [P, T])
    m.minus_half = new.sb("minus_half", [P, 1])
    m.made = new.sem("made")
    m.seen, m.pool_seen = new.sem("seen"), new.sem("pool_seen")

    m.const_step = new.sem("const_step")
    n = [0]

    def build(pool):
        step = m.const_step

        def done(ins):
            n[0] += 1
            ins.then_inc(step, 1)
            pool.wait_ge(step, n[0])

        done(pool.memset(m.ident[:, :], 0.0))
        pool.affine_select(out=m.ident[:, :], in_=m.ident[:, :], compare_op=ALU.not_equal, fill=1.0,
                           base=0, pattern=[[-1, P]], channel_multiplier=1).then_inc(m.made, 1)
        pool.memset(m.ones[:, :], 1.0).then_inc(m.made, 1)
        done(pool.memset(m.minus_half[:, :], -0.5))
        done(pool.memset(m.batch_mask[:, :], 1.0))
        done(pool.affine_select(out=m.batch_mask[:, :], in_=m.batch_mask[:, :], compare_op=ALU.is_ge,
                                fill=0.0, base=0, pattern=[[-T, GB]], channel_multiplier=1))
        pool.affine_select(out=m.batch_mask[:, :], in_=m.batch_mask[:, :], compare_op=ALU.is_ge,
                           fill=0.0, base=T - 1, pattern=[[T, GB]], channel_multiplier=-1).then_inc(m.made, 1)
        done(pool.memset(m.time_mask[:, :], 0.0))
        for j in range(GB):
            last = pool.affine_select(out=m.time_mask[:, :], in_=m.time_mask[:, :], compare_op=ALU.not_equal,
                                      fill=1.0, base=-T * j, pattern=[[-1, T]], channel_multiplier=1)
            if j < GB - 1:
                done(last)
        last.then_inc(m.made, 1)

    m.build_constants = build
    m.const_steps = n
    m.all_made = 4


def attention(nc, new, m, psum, x, context, w):
    sb, sem = new.sb, new.sem
    ring = lambda name, shape, n=2: [sb(f"{name}{i}", shape) for i in range(n)]
    ident, x_all, ret_q = m.ident, m.x_all, m.ret_q

    ctx_rows = ring("ctx_rows", [P, GB, 2, D], NR)
    ctx_last = ring("ctx_last", [GB, D], NR)
    ctxT = ring("ctxT", [P, GB, DC, KEYS])
    xn = ring("xn", [P, D])
    xnT = ring("xnT_a", [P, DC, P])
    qT = ring("qT", [P, DC, P])
    probs = ring("probs", [P, KEYS])
    last_p = ring("last_p", [P, GB])
    pT = ring("pT", [P, 2, P])
    last_pT = ring("last_pT", [GB, P])
    pv = ring("pv", [P, D])
    pvT = ring("pvT", [P, DC, P])
    xn2 = ring("xn2", [P, D])
    xn2T = ring("xn2T", [P, DC, P])
    ev = ring("ev", [P, T])
    vprod, var_eps = sb("vprod", [P, D]), sb("var_eps", [P, 1])
    bn6a, bn2a, rstd_a = ring("bn6a", [P, 6]), ring("bn2a", [P, 2]), ring("rstd_a", [P, 1])
    bn6b, bn2b, rstd_b = ring("bn6b", [P, 6]), ring("bn2b", [P, 2]), ring("rstd_b", [P, 1])
    mx, nmx, rowsum, rinv, vs = (ring(n, [P, 1]) for n in ("mx", "nmx", "rowsum", "rinv", "vs"))
    x_wq, x_wkv = sb("x_wq", [P, DC, D]), sb("x_wkv", [P, DC, 2 * D])
    a_wq, a_wv = sb("a_wq", [P, DC, D]), sb("a_wv", [P, DC, D])
    w_T = ring("w_T", [P, 2, D], 3)
    qk = sb("qk", [P, DC, D])
    wv_sum = sb("wv_sum", [P, D])
    zero = sb("zero_a", [P, T])

    chunked = lambda bank, n: bank[:, 0:DC * n].rearrange("p (c n) -> p c n", c=DC)
    psC = psum[0:2]
    psT = chunked(psum[2], P)
    psX = chunked(psum[3], P)
    psS, psPV = psum[4][:, 0:KEYS], psum[4][:, 0:D]
    psP = psum[5]
    psL = psum[5][:, 3 * P:3 * P + DC * GB].rearrange("p (c b) -> p c b", c=DC)
    psY = psR = psum[6][:, 0:D]
    psU = psum[7][0:T, 0:D]

    w_in, x_first, x_rest = sem("w_in"), sem("x_first"), sem("x_rest")
    ctx_in = [sem(f"ctx_in{r}") for r in range(NR)]
    wT_done, wT_copied, w_product, w_product_copied = (
        sem(n) for n in ("wT_done", "wT_copied", "w_product", "w_product_copied"))
    seen, pool_seen = m.seen, m.pool_seen
    eps_a, eps_b = sem("eps_a"), sem("eps_b")
    st_a, ag_a, rs_a, st_b, ag_b, rs_b, mx_done, rinv_done, vs_done = (
        sem(n) for n in ("st_a", "ag_a", "rs_a", "st_b", "ag_b", "rs_b", "mx_done", "rinv_done", "vs_done"))
    xn_ready, xn_turned, xnT_ready, q_done, qT_ready = (
        sem(n) for n in ("xn_ready", "xn_turned", "xnT_ready", "q_done", "qT_ready"))
    ctx_turned = [sem(f"ctx_turned{j}") for j in range(GB)]
    ctxT_ready = [sem(f"ctxT_ready{j}") for j in range(GB)]
    last_turned, lastT_ready = sem("last_turned"), sem("lastT_ready")
    s_done, nmx_ready, p_ready, lp_ready, p_turned, pT_ready, lpT_ready = (
        sem(n) for n in ("s_done", "nmx_ready", "p_ready", "lp_ready", "p_turned", "pT_ready", "lpT_ready"))
    pv_done, pv_ready, pv_turned, pvT_ready, y_done, x2_ready = (
        sem(n) for n in ("pv_done", "pv_ready", "pv_turned", "pvT_ready", "y_done", "x2_ready"))
    xn2_ready, xn2_turned, xn2T_ready, r_done, r_copied, ev_ready, u_done = (
        sem(n) for n in ("xn2_ready", "xn2_turned", "xn2T_ready", "r_done", "r_copied", "ev_ready", "u_done"))
    m.psU = psU

    W_LOADS = 5
    X_CHUNKS = 8
    XC = NG // X_CHUNKS
    x_v = x.rearrange("(g p) d -> p g d", p=P)
    rows_v = context[:, 0:2 * P, :].rearrange("b (p c) d -> p b c d", c=2)
    last_v = context[:, 2 * P, :]

    def iterations(eng, step):
        for i in range(NR):
            step(i, i % NR, True, i >= 1, i >= 2)
        with eng.Fori(1, NG // NR) as k:
            for r in range(NR):
                step(k * NR + r, r, True, True, True)
        step(NG, 0, False, True, True)
        step(NG + 1, 1, False, False, True)

    with nc.Block() as block:

        @block.gpsimd
        def _(pool):
            m.build_constants(pool)
            pool.memset(zero[:, :], 0.0).then_inc(m.made, 1)

            def rstd_of(g, ag, rs, eps_added, bn2, rstd, ready):
                wait_for(pool, ready, g - 1)
                wait_alone(pool, ag, g + 1, pool_seen)
                pool.tensor_scalar(var_eps[:, :], bn2[:, 1:2], EPS, None, ALU.add).then_inc(eps_added, 1)
                wait_for(pool, eps_added, g + 1)
                pool.tensor_tensor(rstd[:, :], var_eps[:, :], m.minus_half[:, :], ALU.pow).then_inc(rs, 1)

            def step(i, r, front, mid, back):
                if front:
                    rstd_of(i, ag_a, rs_a, eps_a, bn2a[r % 2], rstd_a[r % 2], xn_ready)
                if back:
                    rstd_of(i - 2, ag_b, rs_b, eps_b, bn2b[r % 2], rstd_b[r % 2], xn2_ready)

            iterations(pool, step)

        @block.sync
        def _(sp):
            sp.dma_start(x_all[:, 0:XC * D].rearrange("p (g d) -> p g d", d=D), x_v[:, 0:XC, :]).then_inc(x_first, 16)
            for t, v in ((x_wq, w["x_wq"]), (x_wkv, w["x_wkv"]), (a_wv, w["a_wv"]), (a_wq, w["a_wq"]), (m.a_wk, w["a_wk"])):
                sp.dma_start(t[:, :, :], v.rearrange("(c p) n -> p c n", p=P)).then_inc(w_in, 16)

            def load(g, r):
                wait_for(sp, pv_done, g - (NR - 1))
                sp.dma_start(ctx_rows[r][:, :, :, :], rows_v[:, ds(g * GB, GB), :, :]).then_inc(ctx_in[r], 16)
                sp.dma_start(ctx_last[r][:, :], last_v[ds(g * GB, GB), :]).then_inc(ctx_in[r], 16)

            for g in range(NR):
                load(g, g)
            for j in range(1, X_CHUNKS):
                sp.dma_start(x_all[:, j * XC * D:(j + 1) * XC * D].rearrange("p (g d) -> p g d", d=D),
                             x_v[:, j * XC:(j + 1) * XC, :]).then_inc(x_rest, 16)
            with sp.Fori(1, NG // NR) as k:
                for r in range(NR):
                    load(k * NR + r, r)

        @block.tensor
        def _(pe):
            pe.wait_ge(m.made, m.all_made)
            pe.wait_ge(w_in, 16 * W_LOADS)
            for i, src in enumerate((x_wq, x_wkv, a_wv)):
                for kc in range(2):
                    for dc in range(DC):
                        o = kc * D + dc * P
                        last = pe.transpose(psum[i][:, o:o + P], src[:, dc, kc * P:kc * P + P], ident[:, :])
                last.then_inc(wT_done, 1)
            pe.wait_ge(wT_copied, 3)
            for dc in range(DC):
                for kc in range(2):
                    last = pe.matmul(psum[3][:, dc * D:(dc + 1) * D], w_T[0][:, kc, dc * P:(dc + 1) * P],
                                     w_T[1][:, kc, :], start=(kc == 0), stop=(kc == 1))
            last.then_inc(w_product, 1)
            for kc in range(2):
                last = pe.matmul(psum[4][:, 0:D], m.ones[:, :], w_T[2][:, kc, :], start=(kc == 0), stop=(kc == 1))
            last.then_inc(w_product, 1)
            pe.wait_ge(m.made, m.all_made + 1)
            pe.wait_ge(w_product_copied, 2)
            pe.matmul(psU, zero[:, :], wv_sum[:, :], start=True, stop=False, skip_group_check=True)

            def turn_context(g, r, p, js):
                for j in js:
                    if j == 0:
                        wait_for(pe, ctx_in[r], (g - r) * (32 // NR) + 32)
                    wait_for(pe, ctxT_ready[(j + 2) % GB], g + 1 if j >= 2 else g)
                    for dc in range(DC):
                        for c in range(2):
                            o = dc * 2 * P + c * P
                            last = pe.transpose(psC[j % 2][:, o:o + P], ctx_rows[r][:, j, c, dc * P:(dc + 1) * P],
                                                ident[:, :])
                    last.then_inc(ctx_turned[j], 1)

            def step(i, r, front, mid, back):
                f, c, b = i, i - 1, i - 2
                pf, pc, pb = r % 2, (r + 1) % 2, r % 2
                rc = (r + NR - 1) % NR
                if back:
                    wait_for(pe, pv_ready, b + 1)
                    wait_for(pe, xn2T_ready, b)
                    for dc in range(DC):
                        last = pe.transpose(psT[:, dc, :], pv[pb][:, dc * P:(dc + 1) * P], ident[:, :])
                    last.then_inc(pv_turned, 1)
                if front:
                    turn_context(f, r, pf, (0, 1))
                if mid:
                    for j in range(GB):
                        wait_for(pe, ctxT_ready[j], c + 1)
                    wait_for(pe, lastT_ready, c + 1)
                    wait_for(pe, qT_ready, c + 1)
                    wait_for(pe, pv_ready, c)
                    for dc in range(DC):
                        for j in range(GB):
                            last = pe.matmul(psS[j * T:(j + 1) * T, :], qT[pc][:, dc, j * T:(j + 1) * T],
                                             ctxT[pc][:, j, dc, :], start=(dc == 0), stop=(dc == DC - 1))
                    last.then_inc(s_done, 1)
                if back:
                    wait_for(pe, pvT_ready, b + 1)
                    wait_for(pe, r_copied, b)
                    for dc in range(DC):
                        last = pe.matmul(psY, pvT[pb][:, dc, :], x_wkv[:, dc, D:2 * D], start=(dc == 0),
                                         stop=(dc == DC - 1))
                    last.then_inc(y_done, 1)
                if front:
                    wait_for(pe, pT_ready, f - 1)
                    wait_for(pe, lpT_ready, f - 1)
                    turn_context(f, r, pf, (2, 3))
                    for dc in range(DC):
                        last = pe.transpose(psL[:, dc, :], ctx_last[r][:, dc * P:(dc + 1) * P], ident[0:GB, 0:GB])
                    last.then_inc(last_turned, 1)
                    wait_for(pe, xn_ready, f + 1)
                    wait_for(pe, qT_ready, f)
                    for dc in range(DC):
                        last = pe.transpose(psX[:, dc, :], xn[pf][:, dc * P:(dc + 1) * P], ident[:, :])
                    last.then_inc(xn_turned, 1)
                if mid:
                    wait_for(pe, p_ready, c + 1)
                    wait_for(pe, lp_ready, c + 1)
                    if front:
                        wait_for(pe, lastT_ready, f + 1)
                    for h in range(2):
                        pe.transpose(psP[:, h * P:(h + 1) * P], probs[pc][:, h * P:(h + 1) * P], ident[:, :])
                    pe.transpose(psP[0:GB, 2 * P:3 * P], last_p[pc][:, :], ident[:, :]).then_inc(p_turned, 1)
                if back:
                    wait_for(pe, xn2_ready, b + 1)
                    for dc in range(DC):
                        last = pe.transpose(psT[:, dc, :], xn2[pb][:, dc * P:(dc + 1) * P], ident[:, :])
                    last.then_inc(xn2_turned, 1)
                if front:
                    wait_for(pe, xnT_ready, f + 1)
                    for ec in range(DC):
                        for dc in range(DC):
                            last = pe.matmul(psX[:, ec, :], qk[:, dc, ec * P:(ec + 1) * P], xnT[pf][:, dc, :],
                                             start=(dc == 0), stop=(dc == DC - 1))
                    last.then_inc(q_done, 1)
                if mid:
                    wait_for(pe, pT_ready, c + 1)
                    wait_for(pe, lpT_ready, c + 1)
                    pe.matmul(psPV, last_pT[pc][:, :], ctx_last[rc][:, :], start=True, stop=False,
                              skip_group_check=True)
                    for h in range(2):
                        for j in range(GB):
                            last = pe.matmul(psPV[j * T:(j + 1) * T, :], pT[pc][:, h, j * T:(j + 1) * T],
                                             ctx_rows[rc][:, j, h, :], start=False, stop=(h == 1),
                                             skip_group_check=True)
                    last.then_inc(pv_done, 1)
                if back:
                    wait_for(pe, xn2T_ready, b + 1)
                    for dc in range(DC):
                        last = pe.matmul(psR, xn2T[pb][:, dc, :], a_wq[:, dc, :], start=(dc == 0), stop=(dc == DC - 1))
                    last.then_inc(r_done, 1)
                    wait_for(pe, ev_ready, b + 1)
                    pe.matmul(psU, ev[pb][:, :], xn2[pb][:, :], start=False, stop=(isinstance(i, int) and i == NG + 1),
                              skip_group_check=True).then_inc(u_done, 1)

            iterations(pe, step)

        @block.scalar
        def _(act):
            copy = lambda o, i: act.activation(o, i, ACT.Copy)
            for i in range(3):
                act.wait_ge(wT_done, i + 1)
                copy(w_T[i][:, :, :], psum[i][:, :].rearrange("p (c n) -> p c n", c=2)).then_inc(wT_copied, 1)
            act.wait_ge(w_product, 1)
            copy(qk[:, :, :], psum[3][:, :].rearrange("p (c n) -> p c n", c=DC)).then_inc(w_product_copied, 1)
            act.wait_ge(w_product, 2)
            copy(wv_sum[:, :], psum[4][:, 0:D]).then_inc(w_product_copied, 1)

            def context_copy(f, pf, j):
                wait_for(act, ctx_turned[j], f + 1)
                wait_for(act, s_done, f - 1)
                copy(ctxT[pf][:, j, :, 0:2 * P], psC[j % 2][:, :].rearrange("p (c n) -> p c n", c=DC)) \
                    .then_inc(ctxT_ready[j], 1)

            def step(i, r, front, mid, back):
                f, c, b = i, i - 1, i - 2
                pf, pc, pb = r % 2, (r + 1) % 2, r % 2
                if back:
                    wait_for(act, pv_turned, b + 1)
                    wait_for(act, y_done, b - 1)
                    copy(pvT[pb][:, :, :], psT).then_inc(pvT_ready, 1)
                if front:
                    context_copy(f, pf, 1)
                if mid:
                    wait_for(act, nmx_ready, c + 1)
                    wait_for(act, p_turned, c - 1)
                    wait_for(act, lp_ready, c - 1)
                    act.activation(probs[pc][:, :], psS, ACT.Exp, bias=nmx[pc][:, :], scale=SCALE,
                                   accum_out=rowsum[pc][:, :]).then_inc(p_ready, 1)
                if front:
                    context_copy(f, pf, 3)
                    wait_for(act, xn_turned, f + 1)
                    wait_for(act, q_done, f - 1)
                    copy(xnT[pf][:, :, :], psX).then_inc(xnT_ready, 1)
                if back:
                    wait_for(act, xn2_turned, b + 1)
                    wait_for(act, r_done, b - 1)
                    copy(xn2T[pb][:, :, :], psT).then_inc(xn2T_ready, 1)
                if front:
                    wait_for(act, q_done, f + 1)
                    wait_for(act, s_done, f - 1)
                    copy(qT[pf][:, :, :], psX).then_inc(qT_ready, 1)
                if mid:
                    wait_for(act, pv_done, c + 1)
                    wait_for(act, pv_turned, c - 1)
                    copy(pv[pc][:, :], psPV).then_inc(pv_ready, 1)
                if back:
                    wait_for(act, r_done, b + 1)
                    copy(ret_q[:, ds(b * D, D)], psR).then_inc(r_copied, 1)

            iterations(act, step)

        @block.vector
        def _(dve):
            dve.wait_ge(m.made, m.all_made)
            dve.wait_ge(w_product_copied, 2)
            dve.wait_ge(x_first, 16)

            def context_copy(f, pf, j):
                wait_for(dve, ctx_turned[j], f + 1)
                wait_for(dve, s_done, f - 1)
                dve.tensor_copy(ctxT[pf][:, j, :, 0:2 * P], psC[j % 2][:, :].rearrange("p (c n) -> p c n", c=DC)) \
                    .then_inc(ctxT_ready[j], 1)

            def moments(src, g, st, ag, rs, bn6, bn2):
                dve.bn_stats(bn6[:, :], src).then_inc(st, 1)
                wait_for(dve, rs, g - 1)
                wait_alone(dve, st, g + 1, seen)
                dve.bn_aggr(bn2[:, :], bn6[:, :]).then_inc(ag, 1)

            def normalise(src, g, ag, rs, bn2, rstd, dst, free, free_at, ready):
                wait_for(dve, rs, g + 1)
                wait_for(dve, ag, g + 1)
                wait_for(dve, free, free_at)
                dve.tensor_scalar(dst, src, bn2[:, 0:1], rstd[:, :], ALU.subtract, ALU.mult).then_inc(ready, 1)

            def step(i, r, front, mid, back):
                f, c, b = i, i - 1, i - 2
                pf, pc, pb = r % 2, (r + 1) % 2, r % 2
                if front:
                    context_copy(f, pf, 0)
                    moments(x_all[:, ds(f * D, D)], f, st_a, ag_a, rs_a, bn6a[pf], bn2a[pf])
                if mid:
                    wait_for(dve, s_done, c + 1)
                    dve.reduce_max(mx[pc][:, :], psS, AX.X).then_inc(mx_done, 1)
                    wait_for(dve, mx_done, c + 1)
                    wait_for(dve, p_ready, c - 1)
                    dve.tensor_scalar(nmx[pc][:, :], mx[pc][:, :], -SCALE, None, ALU.mult).then_inc(nmx_ready, 1)
                if front:
                    normalise(x_all[:, ds(f * D, D)], f, ag_a, rs_a, bn2a[pf], rstd_a[pf],
                              xn[pf][:, :], xn_turned, f - 1, xn_ready)
                if back:
                    wait_for(dve, y_done, b + 1)
                    wait_for(dve, rinv_done, b + 1)
                    xs = x_all[:, ds(b * D, D)]
                    dve.scalar_tensor_tensor(out=xs, in0=psY, scalar=rinv[pb][:, :], in1=xs, op0=ALU.mult,
                                             op1=ALU.add).then_inc(x2_ready, 1)
                    wait_alone(dve, x2_ready, b + 1, seen)
                    moments(x_all[:, ds(b * D, D)], b, st_b, ag_b, rs_b, bn6b[pb], bn2b[pb])
                if front:
                    context_copy(f, pf, 2)
                    wait_for(dve, last_turned, f + 1)
                    dve.tensor_copy(ctxT[pf][:, :, :, 2 * P:KEYS].rearrange("p b c o -> p c (b o)"), psL) \
                        .then_inc(lastT_ready, 1)
                if back:
                    normalise(x_all[:, ds(b * D, D)], b, ag_b, rs_b, bn2b[pb], rstd_b[pb],
                              xn2[pb][:, :], u_done, b - 1, xn2_ready)
                if mid:
                    wait_for(dve, p_ready, c + 1)
                    wait_for(dve, p_turned, c - 1)
                    dve.tensor_scalar(last_p[pc][:, :], m.batch_mask[:, :], probs[pc][:, 2 * P:KEYS], None,
                                      ALU.mult).then_inc(lp_ready, 1)
                    dve.reciprocal(rinv[pc][:, :], rowsum[pc][:, :]).then_inc(rinv_done, 1)
                if back:
                    wait_for(dve, xn2_ready, b + 1)
                    dve.tensor_tensor_reduce(out=vprod[:, :], in0=xn2[pb][:, :], in1=wv_sum[:, :], scale=1.0,
                                             scalar=0.0, op0=ALU.mult, op1=ALU.add,
                                             accum_out=vs[pb][:, :]).then_inc(vs_done, 1)
                if mid:
                    wait_for(dve, p_turned, c + 1)
                    wait_for(dve, pv_done, c - 1)
                    dve.tensor_copy(pT[pc][:, :, :], psP[:, 0:2 * P].rearrange("p (c n) -> p c n", c=2)) \
                        .then_inc(pT_ready, 1)
                    dve.tensor_copy(last_pT[pc][:, :], psP[0:GB, 2 * P:3 * P]).then_inc(lpT_ready, 1)
                if back:
                    wait_for(dve, vs_done, b + 1)
                    wait_for(dve, u_done, b - 1)
                    dve.tensor_scalar(ev[pb][:, :], m.time_mask[:, :], vs[pb][:, :], None, ALU.mult) \
                        .then_inc(ev_ready, 1)

            for i in range(NR):
                step(i, i % NR, True, i >= 1, i >= 2)
            dve.wait_ge(x_rest, 16 * (X_CHUNKS - 1))
            with dve.Fori(1, NG // NR) as k:
                for r in range(NR):
                    step(k * NR + r, r, True, True, True)
            step(NG, 0, False, True, True)
            step(NG + 1, 1, False, False, True)


def two_deep(eng, steps, tail, step):
    for i in range(4):
        step(i, i % 2)
    pairs = steps // 2
    with eng.Fori(2, pairs) as k:
        for r in range(2):
            step(k * 2 + r, r)
    for i in range(2 * pairs, steps + tail):
        step(i, i % 2)


def retention(nc, new, m, psum, kept):
    sb, sem = new.sb, new.sem
    C = 4
    NCH = NG // C
    W = C * D
    ident, x_all, ret_q, xnT = m.ident, m.x_all, m.ret_q, m.xnT
    u = sb("u", [T, D])
    uT = sb("uT", [P, DC, T])
    state = [sb(f"state{i}", [P, DC, T]) for i in range(2)]
    spread = sb("spread", [P, GB, GB, T])
    s_rows = sb("s_rows", [P, D])
    bn6 = [sb(f"bn6_{i}", [P, C, 6]) for i in range(2)]
    bn2 = [sb(f"bn2_{i}", [P, C, 2]) for i in range(2)]
    veps = sb("veps", [P, C])
    rstd = [sb(f"rstd_{i}", [P, C]) for i in range(2)]
    nmr = [sb(f"nmr_{i}", [P, C]) for i in range(2)]
    half4 = sb("half4", [P, C])
    xn3 = [sb(f"xn3_{i}", [P, C, D]) for i in range(2)]
    SPANS = [1, 2, 4, 8, 16]
    STEPS = len(SPANS) + 2
    final = state[len(SPANS) % 2]
    psT = psum[0:2]
    psM, psRows, m.psMean = psum[2], psum[3], psum[7]
    m.psMean_v = psum[7][:, 0:DC * B].rearrange("p (c b) -> p c b", c=DC)

    names = ("u_copied", "u_turned", "uT_copied", "m_done", "scan", "consts_made", "rows_done",
             "rows_copied", "q_scaled", "x3_done", "st_done", "ag_done", "veps_done", "rstd_done", "nmr_done",
             "xn_done", "mean_done", "kept_ready", "stored", "pads")
    s = {n: sem("r_" + n) for n in names}
    turned = [sem(f"r_turned{j}") for j in range(2)]
    copied = [sem(f"r_copied{j}") for j in range(2)]
    kept_v = kept.rearrange("(g p) d -> p g d", p=P)

    with nc.Block() as block:

        @block.sync
        def _(sp):
            with sp.Fori(0, NCH) as i:
                sp.wait_ge(s["kept_ready"], i + 1)
                sp.dma_start(kept_v[:, ds(i * C, C), :],
                             x_all[:, ds(i * W, W)].rearrange("p (g d) -> p g d", d=D)).then_inc(s["stored"], 16)
            sp.wait_ge(s["stored"], 16 * NCH)

        @block.gpsimd
        def _(pool):
            for b in range(GB):
                last = pool.tensor_copy(spread[:, :, b, :], ident[:, :].rearrange("p (q i) -> p q i", q=GB))
            last.then_inc(s["consts_made"], 1)
            pool.memset(half4[:, :], -0.5).then_inc(s["consts_made"], 1)
            pool.memset(xnT[:, :, B * T:], 0.0).then_inc(s["pads"], 1)
            pool.wait_ge(s["consts_made"], 2)
            pool.wait_ge(s["rows_copied"], 1)

            def step(i, r):
                if is_in(i, 0, NCH - 1):
                    qs = ret_q[:, ds(i * W, W)].rearrange("p (g d) -> p g d", d=D)
                    pool.tensor_tensor(qs, qs, s_rows[:, :].unsqueeze(1).to_broadcast([P, C, D]), ALU.mult) \
                        .then_inc(s["q_scaled"], 1)
                if is_in(i, 1, NCH):
                    j, rj = i - 1, 1 - r
                    wait_for(pool, s["nmr_done"], i - 2)
                    wait_for(pool, s["xn_done"], i - 2)
                    wait_for(pool, s["rstd_done"], i - 1)
                    wait_alone(pool, s["ag_done"], i, m.pool_seen)
                    pool.tensor_scalar(veps[:, :], bn2[rj][:, :, 1], EPS, None, ALU.add).then_inc(s["veps_done"], 1)
                    wait_for(pool, s["veps_done"], i)
                    pool.tensor_tensor(rstd[rj][:, :], veps[:, :], half4[:, :], ALU.pow).then_inc(s["rstd_done"], 1)
                if is_in(i, 2, NCH + 1):
                    xs = x_all[:, ds((i - 2) * W, W)]
                    wait_for(pool, s["xn_done"], i - 1)
                    pool.tensor_tensor(xs, xs, xn3[r][:, :, :].rearrange("p g d -> p (g d)"), ALU.add).then_inc(s["kept_ready"], 1)

            two_deep(pool, NCH, 2, step)

        @block.vector
        def _(dve):
            dve.tensor_copy(u[:, :], m.psU).then_inc(s["u_copied"], 1)
            dve.wait_ge(s["m_done"], 1)
            mT = psM[:, 0:DC * T].rearrange("p (c t) -> p c t", c=DC)
            dve.tensor_copy(state[0][:, :, :], mT).then_inc(s["scan"], 1)
            for n, span in enumerate(SPANS):
                a, b = state[n % 2], state[(n + 1) % 2]
                dve.wait_ge(s["scan"], n + 1)
                dve.tensor_copy(b[:, :, 0:1 + span], a[:, :, 0:1 + span])
                dve.scalar_tensor_tensor(out=b[:, :, 1 + span:], in0=a[:, :, 1:T - span], scalar=GAMMA ** span,
                                         in1=a[:, :, 1 + span:], op0=ALU.mult, op1=ALU.add).then_inc(s["scan"], 1)
            dve.wait_ge(s["scan"], STEPS - 1)
            dve.tensor_copy(final[:, :, 0:1], final[:, :, 1:2]).then_inc(s["scan"], 1)
            dve.wait_ge(s["rows_done"], 1)
            dve.tensor_copy(s_rows[:, :].rearrange("p (t c q) -> p q c t", c=DC, q=GB),
                            psRows[:, 0:D].rearrange("p (q c t) -> p q c t", q=GB, c=DC)).then_inc(s["rows_copied"], 1)

            def step(i, r):
                if is_in(i, 0, NCH - 1):
                    xs = x_all[:, ds(i * W, W)]
                    wait_for(dve, s["q_scaled"], i + 1)
                    dve.tensor_tensor(xs, xs, ret_q[:, ds(i * W, W)], ALU.add).then_inc(s["x3_done"], 1)
                    wait_for(dve, s["nmr_done"], i - 1)
                    wait_for(dve, s["rstd_done"], i - 1)
                    wait_alone(dve, s["x3_done"], i + 1, m.seen)
                    for g in range(C):
                        last = dve.bn_stats(bn6[r][:, g, :], x_all[:, ds(i * W + g * D, D)])
                    last.then_inc(s["st_done"], 1)
                    wait_alone(dve, s["st_done"], i + 1, m.seen)
                    for g in range(C):
                        last = dve.bn_aggr(bn2[r][:, g, :], bn6[r][:, g, :])
                    last.then_inc(s["ag_done"], 1)
                if is_in(i, 1, NCH):
                    rj = 1 - r
                    wait_for(dve, s["rstd_done"], i)
                    wait_for(dve, s["ag_done"], i)
                    wait_for(dve, s["xn_done"], i - 2)
                    dve.scalar_tensor_tensor(out=nmr[rj][:, :], in0=bn2[rj][:, :, 0], scalar=-1.0, in1=rstd[rj][:, :],
                                             op0=ALU.mult, op1=ALU.mult).then_inc(s["nmr_done"], 1)

            two_deep(dve, NCH, 1, step)

        @block.tensor
        def _(pe):
            pe.wait_ge(s["u_copied"], 1)
            for dc in range(DC):
                last = pe.transpose(psT[0][:, dc * T:(dc + 1) * T], u[:, dc * P:(dc + 1) * P], ident[0:T, 0:T])
            last.then_inc(s["u_turned"], 1)
            pe.wait_ge(s["uT_copied"], 1)
            for ec in range(DC):
                for dc in range(DC):
                    last = pe.matmul(psM[:, ec * T:(ec + 1) * T], m.a_wk[:, dc, ec * P:(ec + 1) * P], uT[:, dc, :],
                                     start=(dc == 0), stop=(dc == DC - 1))
            last.then_inc(s["m_done"], 1)
            pe.wait_ge(s["consts_made"], 1)
            pe.wait_ge(s["scan"], STEPS)
            for q in range(GB):
                last = pe.matmul(psRows[:, q * DC * T:(q + 1) * DC * T], spread[:, q, :, :].rearrange("p b i -> p (b i)"),
                                 final[:, :, :].rearrange("p c t -> p (c t)"), start=True, stop=True)
            last.then_inc(s["rows_done"], 1)

            def step(i, r):
                if is_in(i, 1, NCH):
                    j = 1 - r
                    for h in range(2):
                        wait_for(pe, copied[h], i - 1)
                        wait_for(pe, s["xn_done"], i)
                        for dc in range(DC):
                            for g in range(2):
                                o = (dc * 2 + g) * P
                                last = pe.transpose(psT[h][:, o:o + P], xn3[j][:, 2 * h + g, dc * P:(dc + 1) * P],
                                                    ident[:, :])
                        last.then_inc(turned[h], 1)
                    for dc in range(DC):
                        for g in range(C):
                            last = pe.matmul(m.psMean[:, ds((i - 1) * (C * GB) + dc * B + g * GB, GB)],
                                             xn3[j][:, g, dc * P:(dc + 1) * P], m.batch_mask[:, :],
                                             start=True, stop=True)
                    last.then_inc(s["mean_done"], 1)

            two_deep(pe, NCH, 1, step)

        @block.scalar
        def _(act):
            act.wait_ge(s["u_turned"], 1)
            act.activation(uT[:, :, :], psT[0][:, 0:DC * T].rearrange("p (c t) -> p c t", c=DC), ACT.Copy) \
                .then_inc(s["uT_copied"], 1)

            def step(i, r):
                if is_in(i, 1, NCH):
                    j = 1 - r
                    wait_for(act, s["nmr_done"], i)
                    wait_for(act, s["kept_ready"], i - 2)
                    wait_for(act, s["mean_done"], i - 2)
                    for g in range(C):
                        last = act.activation(xn3[j][:, g, :], x_all[:, ds((i - 1) * W + g * D, D)], ACT.Identity,
                                              bias=nmr[j][:, g:g + 1], scale=rstd[j][:, g:g + 1])
                    last.then_inc(s["xn_done"], 1)
                    for h in range(2):
                        wait_for(act, turned[h], i)
                        act.activation(xnT[:, :, ds((i - 1) * (C * P) + h * 2 * P, 2 * P)],
                                       psT[h][:, :].rearrange("p (c n) -> p c n", c=DC), ACT.Copy).then_inc(copied[h], 1)

            two_deep(act, NCH, 1, step)


def is_in(i, first, last):
    return not isinstance(i, int) or first <= i <= last


def router(nc, new, m, psum, w1, b1, w2, b2):
    sb, sem = new.sb, new.sem
    w1_sb, w2_sb = sb("w1_sb", [P, DC, HID]), sb("w2_sb", [HID, E])
    b1_sb, b2_sb = sb("b1_sb", [HID, 1]), sb("b2_sb", [1, E])
    mean, hid = sb("mean", [P, DC, B]), sb("hid", [HID, B])
    before = sb("before", [P, P])
    lower = sb("lower", [P, E, E])
    slot_no = sb("slot_no", [P, NSLOT])
    tile_no = sb("tile_no", [P, TILES])
    pad_col = sb("pad_col", [1, NSLOT])
    batch_col = sb("batch_col", [P, 1])
    full = sb("full", [P, E])
    small = lambda name: sb(name, [P, E])
    mx, nmx, total, inv = (sb(n, [P, 1]) for n in ("r_mx", "r_nmx", "r_total", "r_inv"))
    ex, probs, rank, picked, share, weight = (small("r_" + n) for n in ("ex", "probs", "rank", "picked", "share", "weight"))
    tiles, start, end, slot = (small("r_" + n) for n in ("tiles", "start", "end", "slot"))
    cmp, cmp2 = sb("cmp", [P, E, E]), sb("cmp2", [P, E, E])
    past = sb("past", [1, TILES, E])
    slot_k, weight_k = sb("slot_k", [P, TOP]), sb("weight_k", [P, TOP])
    pick_k = sb("pick_k", [P, E])
    scratch = sb("scratch", [P, E])
    hot = [sb(f"hot{k}", [P, NSLOT]) for k in range(TOP)]
    wide = [sb(f"wide{k}", [P, P]) for k in range(TOP)]
    row, row2 = sb("row", [1, NSLOT]), sb("row2", [1, NSLOT])
    texp = sb("texp", [1, TILES])

    psH, psLg, psPos, psCnt, psW, psCol = psum[0][0:HID, 0:B], psum[1][:, 0:E], psum[2][:, 0:E], psum[3][:, 0:E], \
        psum[4][:, 0:NSLOT], psum[5][0:1, 0:NSLOT]
    loaded, made, mean_copied, h_done, hid_ready, lg_done, nmx_ready, ex_ready, picked_ready, pos_done, \
        hot_ready, wide_ready, w_done, col_done, w_copied, v = (
            sem("o_" + n) for n in ("loaded", "made", "mean_copied", "h_done", "hid_ready", "lg_done", "nmx_ready",
                                    "ex_ready", "picked_ready", "pos_done", "hot_ready", "wide_ready", "w_done",
                                    "col_done", "w_copied", "steps"))

    with nc.Block() as block:

        @block.sync
        def _(sp):
            sp.dma_start(w1_sb[:, :, :], w1.rearrange("(c p) n -> p c n", p=P)).then_inc(loaded, 16)
            sp.dma_start(w2_sb[:, :], w2).then_inc(loaded, 16)
            sp.dma_start(b1_sb[:, :], b1.rearrange("(n a) -> n a", a=1)).then_inc(loaded, 16)
            sp.dma_start(b2_sb[:, :], b2.rearrange("(a n) -> a n", a=1)).then_inc(loaded, 16)

        @block.gpsimd
        def _(pool):
            n, step = m.const_steps, m.const_step

            def done(ins):
                n[0] += 1
                ins.then_inc(step, 1)
                pool.wait_ge(step, n[0])

            done(pool.memset(before[:, :], 1.0))
            done(pool.affine_select(out=before[:, :], in_=before[:, :], compare_op=ALU.is_ge, fill=0.0, base=-1,
                                    pattern=[[1, P]], channel_multiplier=-1))
            done(pool.memset(lower[:, :, :], 1.0))
            done(pool.affine_select(out=lower[:, :, :], in_=lower[:, :, :], compare_op=ALU.is_ge, fill=0.0, base=-1,
                                    pattern=[[1, E], [-1, E]], channel_multiplier=0))
            whole = dict(allow_small_or_imprecise_dtypes=True)
            pool.iota(slot_no[:, :], pattern=[[1, NSLOT]], base=0, channel_multiplier=0, **whole)
            pool.iota(tile_no[:, :], pattern=[[SLOTS, TILES]], base=0, channel_multiplier=0, **whole)
            pool.iota(pad_col[:, :].rearrange("p (i s) -> p i s", s=SLOTS), pattern=[[0, TILES], [T, SLOTS]],
                      base=B * T + 1, channel_multiplier=0, **whole)
            pool.iota(batch_col[:, :], pattern=[[0, 1]], base=1, channel_multiplier=T, **whole)
            done(pool.iota(full[:, :], pattern=[[SLOTS, E]], base=0, channel_multiplier=0, **whole))
            pool.sem_inc(made, 1)

        @block.tensor
        def _(pe):
            pe.wait_ge(loaded, 64)
            pe.wait_ge(mean_copied, 1)
            for dc in range(DC):
                last = pe.matmul(psH, w1_sb[:, dc, :], mean[:, dc, :], start=(dc == 0), stop=(dc == DC - 1))
            last.then_inc(h_done, 1)
            pe.wait_ge(hid_ready, 1)
            pe.matmul(psLg, hid[:, :], w2_sb[:, :], start=True, stop=False)
            pe.matmul(psLg, m.ones[0:1, :], b2_sb[:, :], start=False, stop=True).then_inc(lg_done, 1)
            pe.wait_ge(picked_ready, 1)
            pe.wait_ge(made, 1)
            pe.matmul(psPos, before[:, :], picked[:, :], start=True, stop=True)
            pe.matmul(psCnt, m.ones[:, :], picked[:, :], start=True, stop=True).then_inc(pos_done, 1)
            for k in range(TOP):
                pe.wait_ge(hot_ready, k + 1)
                pe.matmul(psCol, batch_col[:, :], hot[k][:, :], start=(k == 0), stop=(k == TOP - 1)) \
                    .then_inc(col_done, 1)
            for k in range(TOP):
                pe.wait_ge(wide_ready, k + 1)
                pe.matmul(psW, wide[k][:, :], hot[k][:, :], start=(k == 0), stop=(k == TOP - 1)).then_inc(w_done, 1)

        @block.scalar
        def _(act):
            act.activation(mean[:, :, :], m.psMean_v, ACT.Copy, scale=1.0 / T).then_inc(mean_copied, 1)
            act.wait_ge(loaded, 64)
            act.wait_ge(h_done, 1)
            act.activation(hid[:, :], psH, ACT.Tanh, bias=b1_sb[:, :]).then_inc(hid_ready, 1)
            act.wait_ge(nmx_ready, 1)
            act.activation(ex[:, :], psLg, ACT.Exp, bias=nmx[:, :], accum_out=total[:, :]).then_inc(ex_ready, 1)
            act.wait_ge(w_done, TOP)
            act.activation(m.slot_w[:, :], psW, ACT.Copy).then_inc(w_copied, 1)

        @block.vector
        def _(dve):
            n = [0]

            def done(ins):
                n[0] += 1
                ins.then_inc(v, 1)
                dve.wait_ge(v, n[0])

            by_j = lambda t: t[:, :].unsqueeze(1).to_broadcast([P, E, E])
            by_e = lambda t: t[:, :].unsqueeze(2).to_broadcast([P, E, E])
            dve.wait_ge(lg_done, 1)
            done(dve.reduce_max(mx[:, :], psLg, AX.X))
            dve.tensor_scalar(nmx[:, :], mx[:, :], -1.0, None, ALU.mult).then_inc(nmx_ready, 1)
            dve.wait_ge(ex_ready, 1)
            dve.wait_ge(made, 1)
            done(dve.reciprocal(inv[:, :], total[:, :]))
            done(dve.tensor_scalar(probs[:, :], ex[:, :], inv[:, :], None, ALU.mult))
            dve.tensor_tensor(cmp[:, :, :], by_j(probs), by_e(probs), ALU.is_gt)
            done(dve.tensor_tensor(cmp2[:, :, :], by_j(probs), by_e(probs), ALU.is_equal))
            done(dve.tensor_tensor(cmp2[:, :, :], cmp2[:, :, :], lower[:, :, :], ALU.mult))
            done(dve.tensor_tensor(cmp[:, :, :], cmp[:, :, :], cmp2[:, :, :], ALU.add))
            done(dve.reduce_sum(rank[:, :], cmp[:, :, :], AX.X))
            dve.tensor_scalar(picked[:, :], rank[:, :], float(TOP), None, ALU.is_lt).then_inc(picked_ready, 1)
            dve.wait_ge(picked_ready, 1)
            done(dve.tensor_tensor(share[:, :], probs[:, :], picked[:, :], ALU.mult))
            done(dve.reduce_sum(total[:, :], share[:, :], AX.X))
            done(dve.reciprocal(inv[:, :], total[:, :]))
            done(dve.tensor_scalar(weight[:, :], share[:, :], inv[:, :], None, ALU.mult))
            dve.wait_ge(pos_done, 1)
            done(dve.tensor_copy(scratch[:, :], psCnt))
            done(dve.tensor_tensor(cmp[:, :, :], by_e(scratch), by_j(full), ALU.is_gt))
            done(dve.reduce_sum(tiles[:, :], cmp[:, :, :], AX.X))
            done(dve.tensor_tensor(cmp[:, :, :], by_j(tiles), lower[:, :, :], ALU.mult))
            done(dve.reduce_sum(start[:, :], cmp[:, :, :], AX.X))
            done(dve.tensor_tensor(end[:, :], start[:, :], tiles[:, :], ALU.add))
            done(dve.tensor_scalar(end[:, :], end[:, :], float(SLOTS), None, ALU.mult))
            done(dve.scalar_tensor_tensor(out=slot[:, :], in0=start[:, :], scalar=float(SLOTS), in1=psPos,
                                          op0=ALU.mult, op1=ALU.add))
            for k in range(TOP):
                done(dve.tensor_scalar(pick_k[:, :], rank[:, :], float(k), None, ALU.is_equal))
                dve.tensor_tensor(scratch[:, :], pick_k[:, :], slot[:, :], ALU.mult)
                done(dve.tensor_tensor(share[:, :], pick_k[:, :], weight[:, :], ALU.mult))
                dve.reduce_sum(slot_k[:, k:k + 1], scratch[:, :], AX.X)
                done(dve.reduce_sum(weight_k[:, k:k + 1], share[:, :], AX.X))
                dve.tensor_scalar(hot[k][:, :], slot_no[:, :], slot_k[:, k:k + 1], None, ALU.is_equal) \
                    .then_inc(hot_ready, 1)
                dve.tensor_scalar(wide[k][:, :], m.ones[:, :], weight_k[:, k:k + 1], None, ALU.mult) \
                    .then_inc(wide_ready, 1)
            done(dve.tensor_tensor(past[:, :, :], tile_no[0:1, :].unsqueeze(2).to_broadcast([1, TILES, E]),
                                   end[0:1, :].unsqueeze(1).to_broadcast([1, TILES, E]), ALU.is_ge))
            done(dve.reduce_sum(texp[:, :], past[:, :, :], AX.X))
            dve.tensor_scalar(m.tile_expert[:, :], texp[:, :], float(E - 1), None, ALU.min)
            dve.wait_ge(col_done, TOP)
            done(dve.tensor_copy(row[:, :], psCol))
            done(dve.scalar_tensor_tensor(out=row2[:, :], in0=row[:, :], scalar=0.0, in1=pad_col[:, :],
                                          op0=ALU.is_equal, op1=ALU.mult))
            done(dve.scalar_tensor_tensor(out=m.slot_col[:, :], in0=row[:, :], scalar=-1.0, in1=row2[:, :],
                                          op0=ALU.add, op1=ALU.add))


def experts(nc, new, m, psum, wa, wb):
    sb, sem = new.sb, new.sem
    R = mybir.dt.float32r
    N = SLOTS * T
    raw_a, raw_b = sb("raw_a", [P, DC, FF]), sb("raw_b", [P, FC, D])
    pair = lambda name, shape, n: [[sb(f"{name}{h}{i}", shape, R) for h in ("hi", "lo")] for i in range(n)]
    wa_s, wb_s = pair("wa_", [P, DC, FF], 2), pair("wb_", [P, FC, D], 2)
    cols = sb("cols", [P, DC, N])
    x_s = pair("x_", [P, DC, N], 2)
    act_out = [sb(f"act_out{i}", [P, N]) for i in range(2)]
    h_s = pair("h_", [P, N], 4)
    psH = psum[0:4]
    psZ = [psum[4:6], psum[6:8]]
    TERMS = ((0, 0), (0, 1), (1, 0))

    w_in_a, w_in_b, w_hi, w_lo, cols_ready, x_hi, x_lo, added, acc_zero = (
        sem("e_" + n) for n in ("w_in_a", "w_in_b", "w_hi", "w_lo", "cols_ready", "x_hi", "x_lo", "added", "acc_zero"))
    up_done, gelu_done, h_lo, down_done = (
        [sem(f"e_{n}{c}") for c in range(FC)] for n in ("up_done", "gelu_done", "h_lo", "down_done"))
    h_hi = [sem(f"e_h_hi{c}") for c in range(2)]

    def run(eng, step):
        for i in range(-1, 2):
            step(i, i % 2)
        pairs = (TILES - 1) // 2
        with eng.Fori(1, pairs) as k:
            for r in range(2):
                step(k * 2 + r, r)
        for i in range(2 * pairs, TILES + 1):
            step(i, i % 2)

    def registers(eng_type, tile):
        _, v = nc.values_load_multi_w_load_instructions(
            m.slot_col[0:1, ds(tile * SLOTS, SLOTS)], engines=[eng_type], min_val=0, max_val=B * T + PAD - T)
        return v

    with nc.Block() as block:

        @block.sync
        def _(sp):
            def load(i):
                e = sp.value_load(m.tile_expert[0:1, ds(i, 1)], min_val=0, max_val=E - 1)
                wait_for(sp, w_lo, 2 * i - 1)
                sp.dma_start(raw_a[:, :, :], wa[ds(e, 1), :, :].rearrange("e (c p) f -> p (e c) f", p=P)) \
                    .then_inc(w_in_a, 16)
                wait_for(sp, w_lo, 2 * i)
                sp.dma_start(raw_b[:, :, :], wb[ds(e, 1), :, :].rearrange("e (c p) d -> p (e c) d", p=P)) \
                    .then_inc(w_in_b, 16)

            load(0)
            with sp.Fori(1, TILES) as i:
                load(i)

        @block.gpsimd
        def _(pool):
            pool.memset(m.acc[:, :, :], 0.0).then_inc(acc_zero, 1)

            def step(i, r):
                if is_in(i, -1, TILES - 2):
                    t, q = i + 1, 1 - r
                    v = registers(mybir.EngineType.Pool, t)
                    wait_for(pool, x_hi, t)
                    wait_for(pool, x_lo, t)
                    for j in range(SLOTS):
                        last = pool.tensor_copy(cols[:, :, j * T:(j + 1) * T], m.xnT[:, :, ds(v[j], T)])
                    last.then_inc(cols_ready, 1)
                    wait_for(pool, down_done[FC - 1], t - 1)
                    wait_for(pool, w_hi, 2 * t + 1)
                    pool.tensor_tensor(wa_s[q][1][:, :, :], raw_a[:, :, :], wa_s[q][0][:, :, :].bitcast(F32),
                                       ALU.subtract).then_inc(w_lo, 1)
                    wait_for(pool, w_hi, 2 * t + 2)
                    pool.tensor_tensor(wb_s[q][1][:, :, :], raw_b[:, :, :], wb_s[q][0][:, :, :].bitcast(F32),
                                       ALU.subtract).then_inc(w_lo, 1)

            run(pool, step)

        @block.scalar
        def _(act):
            def ready(t, q, part):
                if part == 0:
                    wait_for(act, cols_ready, t + 1)
                    act.activation(x_s[q][0][:, :, :], cols[:, :, :], ACT.Copy).then_inc(x_hi, 1)
                if part == 1:
                    wait_for(act, w_in_a, 16 * t + 16)
                    wait_for(act, down_done[FC - 1], t - 1)
                if part == 3:
                    wait_for(act, w_in_b, 16 * t + 16)
                for k, (dst, src) in enumerate(((wa_s[q][0], raw_a), (wb_s[q][0], raw_b))):
                    for half in range(2):
                        if part == 1 + 2 * k + half:
                            n = src.shape[1] // 2
                            last = act.activation(dst[:, half * n:(half + 1) * n, :], src[:, half * n:(half + 1) * n, :],
                                                  ACT.Copy)
                            if half == 1:
                                last.then_inc(w_hi, 1)

            def step(i, r):
                for fc in range(FC):
                    if is_in(i, 0, TILES - 1):
                        wait_for(act, up_done[fc], i + 1)
                        wait_for(act, h_lo[(fc - 2) % FC], i + 1 if fc >= 2 else i)
                        act.activation(act_out[fc % 2][:, :], psH[fc % 4][:, :], ACT.Gelu_apprx_tanh) \
                            .then_inc(gelu_done[fc], 1)
                    if is_in(i, -1, TILES - 2) and 2 <= fc:
                        ready(i + 1, 1 - r, fc - 2)

            run(act, step)

        @block.vector
        def _(dve):
            def combine(i, r, v, js):
                for j in js:
                    for dc in range(DC):
                        last = dve.scalar_tensor_tensor(
                            out=m.acc[:, dc, ds(v[j], T)], in0=psZ[r][dc][:, j * T:(j + 1) * T],
                            scalar=m.slot_w[:, ds(i * SLOTS + j, 1)], in1=m.acc[:, dc, ds(v[j], T)],
                            op0=ALU.mult, op1=ALU.add)
                return last

            def step(i, r):
                v = None
                for fc in range(FC):
                    if is_in(i, 0, TILES - 1):
                        g = act_out[fc % 2]
                        hi, lo = h_s[fc % 4]
                        wait_for(dve, gelu_done[fc], i + 1)
                        wait_for(dve, down_done[(fc - 4) % FC], i + 1 if fc >= 4 else i)
                        dve.tensor_copy(hi[:, :], g[:, :]).then_inc(h_hi[fc % 2], 1)
                        wait_for(dve, h_hi[fc % 2], i * (FC // 2) + fc // 2 + 1)
                        dve.tensor_tensor(lo[:, :], g[:, :], hi[:, :].bitcast(F32), ALU.subtract).then_inc(h_lo[fc], 1)
                    if is_in(i, 1, TILES) and fc == 2:
                        v = registers(mybir.EngineType.DVE, i - 1)
                        if isinstance(i, int) and i == 1:
                            dve.wait_ge(acc_zero, 1)
                        wait_for(dve, down_done[FC - 1], i)
                        wait_for(dve, added, i - 1)
                    if is_in(i, 1, TILES) and 3 <= fc < 7:
                        q = SLOTS // 4
                        last = combine(i - 1, 1 - r, v, range((fc - 3) * q, (fc - 2) * q))
                        if fc == 6:
                            last.then_inc(added, 1)
                    if is_in(i, -1, TILES - 2) and fc == 3:
                        q = 1 - r
                        wait_for(dve, x_hi, i + 2)
                        dve.tensor_tensor(x_s[q][1][:, :, :], cols[:, :, :], x_s[q][0][:, :, :].bitcast(F32),
                                          ALU.subtract).then_inc(x_lo, 1)

            run(dve, step)

        @block.tensor
        def _(pe):
            def up(i, r, fc):
                if fc == 0:
                    wait_for(pe, x_hi, i + 1)
                    wait_for(pe, x_lo, i + 1)
                    wait_for(pe, w_lo, 2 * i + 1)
                wait_for(pe, gelu_done[(fc - 4) % FC], i + 1 if fc >= 4 else i)
                n = 0
                for dc in range(DC):
                    for a, b in TERMS:
                        last = pe.matmul(psH[fc % 4][:, :], wa_s[r][a][:, dc, fc * P:(fc + 1) * P], x_s[r][b][:, dc, :],
                                         start=(n == 0), stop=(n == 2 * len(TERMS) - 1))
                        n += 1
                last.then_inc(up_done[fc], 1)

            def down(i, r, fc):
                wait_for(pe, h_lo[fc], i + 1)
                if fc == 0:
                    wait_for(pe, w_lo, 2 * i + 2)
                    wait_for(pe, added, i - 1)
                for dc in range(DC):
                    for n, (a, b) in enumerate(TERMS):
                        last = pe.matmul(psZ[r][dc][:, :], wb_s[r][a][:, fc, dc * P:(dc + 1) * P], h_s[fc % 4][b][:, :],
                                         start=(fc == 0 and n == 0), stop=(fc == FC - 1 and n == len(TERMS) - 1))
                last.then_inc(down_done[fc], 1)

            def step(i, r):
                for fc in range(FC):
                    if is_in(i, 0, TILES - 1):
                        up(i, r, fc)
                        if fc >= 2:
                            down(i, r, fc - 2)
                    if is_in(i, 1, TILES) and fc < 2:
                        down(i - 1, 1 - r, FC - 2 + fc)

            run(pe, step)


def finish(nc, new, m, psum, kept, out):
    sb, sem = new.sb, new.sem
    G, BUF = 2, 4
    STEPS = NG // G
    base = [sb(f"base{i}", [P, G * D]) for i in range(BUF)]
    res = [sb(f"res{i}", [P, G * D]) for i in range(BUF)]
    loaded = [sem(f"f_loaded{i}") for i in range(BUF)]
    stored = [sem(f"f_stored{i}") for i in range(BUF)]
    turned, added = sem("f_turned"), sem("f_added")
    kept_v = kept.rearrange("(g p) d -> p g d", p=P)
    out_v = out.rearrange("(g p) d -> p g d", p=P)
    split = lambda t: t[:, :].rearrange("p (g d) -> p g d", d=D)

    def rounds(eng, step):
        for r in range(BUF):
            step(r, r)
        with eng.Fori(1, STEPS // BUF) as k:
            for r in range(BUF):
                step(k * BUF + r, r)

    with nc.Block() as block:

        @block.sync
        def _(sp):
            def step(i, r):
                wait_for(sp, added, i - (BUF - 1))
                sp.dma_start(split(base[r]), kept_v[:, ds(i * G, G), :]).then_inc(loaded[r], 16)

            rounds(sp, step)

        @block.tensor
        def _(pe):
            for i in range(STEPS):
                if i >= BUF:
                    pe.wait_ge(added, i - (BUF - 1))
                for g in range(G):
                    for dc in range(DC):
                        o = g * D + dc * P
                        last = pe.transpose(psum[i % BUF][:, o:o + P],
                                            m.acc[:, dc, (i * G + g) * P:(i * G + g + 1) * P], m.ident[:, :])
                last.then_inc(turned, 1)

        @block.vector
        def _(dve):
            def step(i, r):
                wait_for(dve, loaded[r], (i - r) * (16 // BUF) + 16)
                wait_for(dve, stored[r], (i - r) * (16 // BUF))
                wait_for(dve, turned, i + 1)
                dve.tensor_tensor(res[r][:, :], psum[r][:, :], base[r][:, :], ALU.add).then_inc(added, 1)

            rounds(dve, step)

        @block.scalar
        def _(act):
            def step(i, r):
                wait_for(act, added, i + 1)
                act.dma_start(out_v[:, ds(i * G, G), :], split(res[r])).then_inc(stored[r], 16)

            rounds(act, step)
            for r in range(BUF):
                act.wait_ge(stored[r], 16 * (STEPS // BUF))


class Room:

    def __init__(self, nc, stack, sems):
        self.nc, self.stack, self.sems = nc, stack, sems

    def sb(self, name, shape, dt=F32):
        return self.stack.enter_context(self.nc.sbuf_tensor(name, shape, dt))

    def sem(self, name):
        return self.sems.enter_context(self.nc.semaphore(name))


class Shared:
    pass


def program(nc, x, context, x_wq, x_wkv, a_wq, a_wk, a_wv, w1, b1, w2, b2, wa, wb, out):
    m = Shared()
    kept = nc.dram_tensor("kept", [B * T, D], F32, kind="Internal").ap()
    with ExitStack() as whole:
        new = Room(nc, whole, whole)
        psum = [whole.enter_context(nc.psum_tensor(f"bank{i}", [P, 512], F32)) for i in range(8)]
        constants(nc, new, m)
        m.xnT = new.sb("xnT", [P, DC, B * T + PAD])
        with ExitStack() as rows:
            held = Room(nc, rows, whole)
            m.x_all, m.ret_q = held.sb("x_all", [P, NG * D]), held.sb("ret_q", [P, NG * D])
            m.a_wk = held.sb("a_wk", [P, DC, D])
            with ExitStack() as own:
                attention(nc, Room(nc, own, whole), m, psum, x.rearrange("b t d -> (b t) d"), context,
                          dict(x_wq=x_wq, x_wkv=x_wkv, a_wq=a_wq, a_wk=a_wk, a_wv=a_wv))
            with ExitStack() as own:
                retention(nc, Room(nc, own, whole), m, psum, kept)
        m.tile_expert = new.sb("tile_expert", [1, TILES], I32)
        m.slot_col = new.sb("slot_col", [1, NSLOT], I32)
        m.slot_w = new.sb("slot_w", [P, NSLOT])
        m.acc = new.sb("acc", [P, DC, B * T + PAD])
        with ExitStack() as own:
            router(nc, Room(nc, own, whole), m, psum, w1, b1, w2, b2)
        with ExitStack() as own:
            experts(nc, Room(nc, own, whole), m, psum, wa, wb)
        with ExitStack() as own:
            finish(nc, Room(nc, own, whole), m, psum, kept, out.rearrange("b t d -> (b t) d"))


_INS = ["x", "ctx_1024", "L0_xattn_Wq", "L0_xattn_Wkv", "L0_attn_Wq", "L0_attn_Wk", "L0_attn_Wv", "L0_ffn_W1",
        "L0_ffn_b1", "L0_ffn_W2", "L0_ffn_b2", "L0_ffn_Wa", "L0_ffn_Wb"]
_OUTS = [((128, 32, 256), "float32")]


def kernel(**inputs):
    import numpy as _np
    import concourse.bacc as _bacc
    from concourse import mybir as _mybir
    from concourse.bass_utils import run_bass_kernel_spmd as _run

    nc = _bacc.Bacc("TRN2", target_bir_lowering=False, num_devices=1)
    arrays, args = {}, []
    for name in _INS:
        a = _np.ascontiguousarray(inputs[name])
        arrays[f"in_{name}_dram"] = a
        args.append(nc.dram_tensor(f"in_{name}_dram", a.shape, _mybir.dt.from_np(a.dtype), kind="ExternalInput").ap())
    for i, (shape, dtype) in enumerate(_OUTS):
        dt = _mybir.dt.from_np(_np.dtype(dtype))
        args.append(nc.dram_tensor(f"out_{i}_dram", shape, dt, kind="ExternalOutput").ap())
    program(nc, *args)
    r = _run(nc, [arrays], core_ids=[0])
    return r.results[0]["out_0_dram"]
```

```python
from contextlib import ExitStack

import concourse.bass as bass
from concourse import mybir

F32 = mybir.dt.float32
I32 = mybir.dt.int32
ALU = mybir.AluOpType
ACT = mybir.ActivationFunctionType
AX = mybir.AxisListType
ds = bass.ds

P = 128
B, T, D = 128, 32, 256
KEYS = 257
DC = D // P
GB = P // T
NG = B // GB
NR = 4
EPS = 1e-5
SCALE = 1.0 / 16.0
GAMMA = 0.96875
E, TOP, HID, FF = 8, 3, 64, 1024
FC = FF // P
UNIT, SLOTS = 8, 16
UNITS = (TOP * B + E * (UNIT - 1)) // UNIT
SMALL = 9
BIG = (UNITS - SMALL) // 2
TILES = BIG + SMALL
NSLOT = UNITS * UNIT
assert 2 * BIG + SMALL == UNITS
assert all(odd + 2 * max(0, (UNITS - odd) // 2 - BIG) <= SMALL for odd in range(E + 1))
PAD = SLOTS * T


def wait_for(eng, sem, count):
    if isinstance(count, int) and count <= 0:
        return
    eng.wait_ge(sem, count)


def wait_alone(eng, sem, count, seen):
    if isinstance(count, int) and count <= 0:
        return
    eng.wait_ge(sem, count)
    eng.sem_inc(seen, 1)


def constants(nc, new, m):
    m.ident = new.sb("ident", [P, P])
    m.ones = new.sb("ones", [P, P])
    m.batch_mask = new.sb("batch_mask", [P, GB])
    m.time_mask = new.sb("time_mask", [P, T])
    m.minus_half = new.sb("minus_half", [P, 1])
    m.made = new.sem("made")
    m.seen, m.pool_seen = new.sem("seen"), new.sem("pool_seen")

    m.const_step = new.sem("const_step")
    n = [0]

    def build(pool):
        step = m.const_step

        def done(ins):
            n[0] += 1
            ins.then_inc(step, 1)
            pool.wait_ge(step, n[0])

        done(pool.memset(m.ident[:, :], 0.0))
        pool.affine_select(out=m.ident[:, :], in_=m.ident[:, :], compare_op=ALU.not_equal, fill=1.0,
                           base=0, pattern=[[-1, P]], channel_multiplier=1).then_inc(m.made, 1)
        pool.memset(m.ones[:, :], 1.0).then_inc(m.made, 1)
        done(pool.memset(m.minus_half[:, :], -0.5))
        done(pool.memset(m.batch_mask[:, :], 1.0))
        done(pool.affine_select(out=m.batch_mask[:, :], in_=m.batch_mask[:, :], compare_op=ALU.is_ge,
                                fill=0.0, base=0, pattern=[[-T, GB]], channel_multiplier=1))
        pool.affine_select(out=m.batch_mask[:, :], in_=m.batch_mask[:, :], compare_op=ALU.is_ge,
                           fill=0.0, base=T - 1, pattern=[[T, GB]], channel_multiplier=-1).then_inc(m.made, 1)
        done(pool.memset(m.time_mask[:, :], 0.0))
        for j in range(GB):
            last = pool.affine_select(out=m.time_mask[:, :], in_=m.time_mask[:, :], compare_op=ALU.not_equal,
                                      fill=1.0, base=-T * j, pattern=[[-1, T]], channel_multiplier=1)
            if j < GB - 1:
                done(last)
        last.then_inc(m.made, 1)

    m.build_constants = build
    m.const_steps = n
    m.all_made = 4


def attention(nc, new, m, psum, x, context, w):
    sb, sem = new.sb, new.sem
    ring = lambda name, shape, n=2: [sb(f"{name}{i}", shape) for i in range(n)]
    ident, x_all, ret_q = m.ident, m.x_all, m.ret_q

    ctx_rows = ring("ctx_rows", [P, GB, 2, D], NR)
    ctx_last = ring("ctx_last", [GB, D], NR)
    last_rows = ring("last_rows", [P, D], NR)
    ctxT = ring("ctxT", [P, GB, DC, KEYS])
    xn = ring("xn", [P, D])
    xnT = ring("xnT_a", [P, DC, P])
    qT = ring("qT", [P, DC, P])
    probs = ring("probs", [P, KEYS])
    pT = ring("pT", [P, 2, P])
    pv = ring("pv", [P, D])
    pvT = ring("pvT", [P, DC, P])
    xn2 = ring("xn2", [P, D])
    xn2T = ring("xn2T", [P, DC, P])
    vprod, var_eps = sb("vprod", [P, D]), sb("var_eps", [P, 1])
    bn6a, bn2a, rstd_a = ring("bn6a", [P, 6]), ring("bn2a", [P, 2]), ring("rstd_a", [P, 1])
    bn6b, bn2b, rstd_b = ring("bn6b", [P, 6]), ring("bn2b", [P, 2]), ring("rstd_b", [P, 1])
    mx, nmx, rowsum, rinv, vs = (ring(n, [P, 1]) for n in ("mx", "nmx", "rowsum", "rinv", "vs"))
    x_wq, x_wkv = sb("x_wq", [P, DC, D]), sb("x_wkv", [P, DC, 2 * D])
    a_wq, a_wv = sb("a_wq", [P, DC, D]), sb("a_wv", [P, DC, D])
    w_T = ring("w_T", [P, 2, D], 3)
    qk = sb("qk", [P, DC, D])
    wv_sum = sb("wv_sum", [P, D])

    chunked = lambda bank, n: bank[:, 0:DC * n].rearrange("p (c n) -> p c n", c=DC)
    psC = psum[0:2]
    psT = chunked(psum[2], P)
    psX = chunked(psum[3], P)
    psS = psum[4][:, 0:KEYS]
    psP = psum[5]
    psL = psum[5][:, 3 * P:3 * P + DC * GB].rearrange("p (c b) -> p c b", c=DC)
    psY = psR = psum[6][:, 0:D]
    psPV = psum[7][:, 0:D]

    w_in, x_first, x_rest = sem("w_in"), sem("x_first"), sem("x_rest")
    ctx_in = [sem(f"ctx_in{r}") for r in range(NR)]
    wT_done, wT_copied, w_product, w_product_copied = (
        sem(n) for n in ("wT_done", "wT_copied", "w_product", "w_product_copied"))
    seen, pool_seen = m.seen, m.pool_seen
    eps_a, eps_b = sem("eps_a"), sem("eps_b")
    st_a, ag_a, rs_a, st_b, ag_b, rs_b, mx_done, rinv_done, vs_done = (
        sem(n) for n in ("st_a", "ag_a", "rs_a", "st_b", "ag_b", "rs_b", "mx_done", "rinv_done", "vs_done"))
    xn_ready, xn_turned, xnT_ready, q_done, qT_ready = (
        sem(n) for n in ("xn_ready", "xn_turned", "xnT_ready", "q_done", "qT_ready"))
    ctx_turned = [sem(f"ctx_turned{j}") for j in range(GB)]
    ctxT_ready = [sem(f"ctxT_ready{j}") for j in range(GB)]
    last_turned, lastT_ready = sem("last_turned"), sem("lastT_ready")
    s_done, nmx_ready, p_ready, p_turned, pT_ready = (
        sem(n) for n in ("s_done", "nmx_ready", "p_ready", "p_turned", "pT_ready"))
    pv_done, pv_ready, pv_turned, pvT_ready, y_done, x2_ready = (
        sem(n) for n in ("pv_done", "pv_ready", "pv_turned", "pvT_ready", "y_done", "x2_ready"))
    xn2_ready, xn2_turned, xn2T_ready, r_done, r_copied, u_added = (
        sem(n) for n in ("xn2_ready", "xn2_turned", "xn2T_ready", "r_done", "r_copied", "u_added"))

    W_LOADS = 5
    X_CHUNKS = 8
    XC = NG // X_CHUNKS
    x_v = x.rearrange("(g p) d -> p g d", p=P)
    rows_v = context[:, 0:2 * P, :].rearrange("b (p c) d -> p b c d", c=2)
    last_v = context[:, 2 * P, :]

    def iterations(eng, step):
        for i in range(NR):
            step(i, i, True, i >= 1, i >= 2, i >= 3)
        with eng.Fori(1, NG // NR) as k:
            for r in range(NR):
                step(k * NR + r, r, True, True, True, True)
        for i in range(NG, NG + 3):
            step(i, i % NR, False, i < NG + 1, i < NG + 2, True)

    with nc.Block() as block:

        @block.gpsimd
        def _(pool):
            m.build_constants(pool)
            pool.memset(m.u_rows[:, :], 0.0).then_inc(m.made, 1)

            def rstd_of(g, ag, rs, eps_added, bn2, rstd, ready):
                wait_for(pool, ready, g - 1)
                wait_alone(pool, ag, g + 1, pool_seen)
                pool.tensor_scalar(var_eps[:, :], bn2[:, 1:2], EPS, None, ALU.add).then_inc(eps_added, 1)
                wait_for(pool, eps_added, g + 1)
                pool.tensor_tensor(rstd[:, :], var_eps[:, :], m.minus_half[:, :], ALU.pow).then_inc(rs, 1)

            def step(i, r, front, mid, back, last_one):
                if front:
                    rstd_of(i, ag_a, rs_a, eps_a, bn2a[r % 2], rstd_a[r % 2], xn_ready)
                if back:
                    rstd_of(i - 2, ag_b, rs_b, eps_b, bn2b[r % 2], rstd_b[r % 2], xn2_ready)

            iterations(pool, step)

        @block.sync
        def _(sp):
            sp.dma_start(x_all[:, 0:XC * D].rearrange("p (g d) -> p g d", d=D), x_v[:, 0:XC, :]).then_inc(x_first, 16)
            for t, v in ((x_wq, w["x_wq"]), (x_wkv, w["x_wkv"]), (a_wv, w["a_wv"]), (a_wq, w["a_wq"]), (m.a_wk, w["a_wk"])):
                sp.dma_start(t[:, :, :], v.rearrange("(c p) n -> p c n", p=P)).then_inc(w_in, 16)

            def load(g, r):
                wait_for(sp, pv_ready, g - (NR - 1))
                sp.dma_start(ctx_rows[r][:, :, :, :], rows_v[:, ds(g * GB, GB), :, :]).then_inc(ctx_in[r], 16)
                sp.dma_start(ctx_last[r][:, :], last_v[ds(g * GB, GB), :]).then_inc(ctx_in[r], 16)
                sp.dma_start(last_rows[r][:, :],
                             last_v[ds(g * GB, GB), :].unsqueeze(1).to_broadcast([GB, T, D])).then_inc(ctx_in[r], 16)

            for g in range(NR):
                load(g, g)
            for j in range(1, X_CHUNKS):
                sp.dma_start(x_all[:, j * XC * D:(j + 1) * XC * D].rearrange("p (g d) -> p g d", d=D),
                             x_v[:, j * XC:(j + 1) * XC, :]).then_inc(x_rest, 16)
            with sp.Fori(1, NG // NR) as k:
                for r in range(NR):
                    load(k * NR + r, r)

        @block.tensor
        def _(pe):
            pe.wait_ge(m.made, m.all_made)
            pe.wait_ge(w_in, 16 * W_LOADS)
            for i, src in enumerate((x_wq, x_wkv, a_wv)):
                for kc in range(2):
                    for dc in range(DC):
                        o = kc * D + dc * P
                        last = pe.transpose(psum[i][:, o:o + P], src[:, dc, kc * P:kc * P + P], ident[:, :])
                last.then_inc(wT_done, 1)
            pe.wait_ge(wT_copied, 3)
            for dc in range(DC):
                for kc in range(2):
                    last = pe.matmul(psum[3][:, dc * D:(dc + 1) * D], w_T[0][:, kc, dc * P:(dc + 1) * P],
                                     w_T[1][:, kc, :], start=(kc == 0), stop=(kc == 1))
            last.then_inc(w_product, 1)
            for kc in range(2):
                last = pe.matmul(psum[4][:, 0:D], m.ones[:, :], w_T[2][:, kc, :], start=(kc == 0), stop=(kc == 1))
            last.then_inc(w_product, 1)
            pe.wait_ge(w_product_copied, 2)

            def turn_context(g, r, js):
                for j in js:
                    wait_for(pe, ctxT_ready[(j + 2) % GB], g + 1 if j >= 2 else g)
                    for dc in range(DC):
                        for c in range(2):
                            o = dc * 2 * P + c * P
                            last = pe.transpose(psC[j % 2][:, o:o + P], ctx_rows[r][:, j, c, dc * P:(dc + 1) * P],
                                                ident[:, :])
                    last.then_inc(ctx_turned[j], 1)

            def step(i, r, front, mid, back, last_one):
                f, c, b, a = i, i - 1, i - 2, i - 3
                even, odd = r % 2, (r + 1) % 2
                rc = (r + NR - 1) % NR
                if mid:
                    for j in range(GB):
                        wait_for(pe, ctxT_ready[j], c + 1)
                    wait_for(pe, lastT_ready, c + 1)
                    wait_for(pe, qT_ready, c + 1)
                    wait_for(pe, p_ready, c)
                    for dc in range(DC):
                        for j in range(GB):
                            last = pe.matmul(psS[j * T:(j + 1) * T, :], qT[odd][:, dc, j * T:(j + 1) * T],
                                             ctxT[odd][:, j, dc, :], start=(dc == 0), stop=(dc == DC - 1))
                    last.then_inc(s_done, 1)
                if front:
                    wait_for(pe, pT_ready, c)
                    wait_for(pe, ctx_in[r], (f - r) * (48 // NR) + 48)
                    wait_for(pe, ctxT_ready[2], f)
                if last_one:
                    wait_for(pe, xn2_ready, a + 1)
                    wait_for(pe, pvT_ready, a + 1)
                    for dc in range(DC):
                        last = pe.transpose(psT[:, dc, :], xn2[odd][:, dc * P:(dc + 1) * P], ident[:, :])
                    last.then_inc(xn2_turned, 1)
                if front:
                    for dc in range(DC):
                        last = pe.transpose(psL[:, dc, :], ctx_last[r][:, dc * P:(dc + 1) * P], ident[0:GB, 0:GB])
                    last.then_inc(last_turned, 1)
                    turn_context(f, r, (0, 1))
                if last_one:
                    wait_for(pe, xn2T_ready, a + 1)
                    wait_for(pe, x2_ready, b)
                    for dc in range(DC):
                        last = pe.matmul(psR, xn2T[odd][:, dc, :], a_wq[:, dc, :], start=(dc == 0), stop=(dc == DC - 1))
                    last.then_inc(r_done, 1)
                if back:
                    wait_for(pe, pv_ready, b + 1)
                    wait_for(pe, xn2T_ready, a + 1)
                    for dc in range(DC):
                        last = pe.transpose(psT[:, dc, :], pv[even][:, dc * P:(dc + 1) * P], ident[:, :])
                    last.then_inc(pv_turned, 1)
                if mid:
                    wait_for(pe, p_ready, c + 1)
                    if front:
                        wait_for(pe, lastT_ready, f + 1)
                    for h in range(2):
                        last = pe.transpose(psP[:, h * P:(h + 1) * P], probs[odd][:, h * P:(h + 1) * P], ident[:, :])
                    last.then_inc(p_turned, 1)
                if front:
                    wait_for(pe, xn_ready, f + 1)
                    wait_for(pe, qT_ready, f)
                    for dc in range(DC):
                        last = pe.transpose(psX[:, dc, :], xn[even][:, dc * P:(dc + 1) * P], ident[:, :])
                    last.then_inc(xn_turned, 1)
                if back:
                    wait_for(pe, pvT_ready, b + 1)
                    wait_for(pe, r_copied, a + 1)
                    for dc in range(DC):
                        last = pe.matmul(psY, pvT[even][:, dc, :], x_wkv[:, dc, D:2 * D], start=(dc == 0),
                                         stop=(dc == DC - 1))
                    last.then_inc(y_done, 1)
                if front:
                    turn_context(f, r, (2, 3))
                    wait_for(pe, xnT_ready, f + 1)
                    for ec in range(DC):
                        for dc in range(DC):
                            last = pe.matmul(psX[:, ec, :], qk[:, dc, ec * P:(ec + 1) * P], xnT[even][:, dc, :],
                                             start=(dc == 0), stop=(dc == DC - 1))
                    last.then_inc(q_done, 1)
                if mid:
                    wait_for(pe, pT_ready, c + 1)
                    wait_for(pe, pv_ready, c)
                    for h in range(2):
                        for j in range(GB):
                            last = pe.matmul(psPV[j * T:(j + 1) * T, :], pT[odd][:, h, j * T:(j + 1) * T],
                                             ctx_rows[rc][:, j, h, :], start=(h == 0), stop=(h == 1))
                    last.then_inc(pv_done, 1)

            iterations(pe, step)

        @block.scalar
        def _(act):
            copy = lambda o, i: act.activation(o, i, ACT.Copy)
            for i in range(3):
                act.wait_ge(wT_done, i + 1)
                copy(w_T[i][:, :, :], psum[i][:, :].rearrange("p (c n) -> p c n", c=2)).then_inc(wT_copied, 1)
            act.wait_ge(w_product, 1)
            copy(qk[:, :, :], psum[3][:, :].rearrange("p (c n) -> p c n", c=DC)).then_inc(w_product_copied, 1)
            act.wait_ge(w_product, 2)
            copy(wv_sum[:, :], psum[4][:, 0:D]).then_inc(w_product_copied, 1)

            def context_copy(f, pf, j):
                wait_for(act, ctx_turned[j], f + 1)
                wait_for(act, s_done, f - 1)
                copy(ctxT[pf][:, j, :, 0:2 * P], psC[j % 2][:, :].rearrange("p (c n) -> p c n", c=DC)) \
                    .then_inc(ctxT_ready[j], 1)

            def step(i, r, front, mid, back, last_one):
                f, c, b, a = i, i - 1, i - 2, i - 3
                even, odd = r % 2, (r + 1) % 2
                if last_one:
                    wait_for(act, xn2_turned, a + 1)
                    wait_for(act, r_done, a)
                    copy(xn2T[odd][:, :, :], psT).then_inc(xn2T_ready, 1)
                if mid:
                    wait_for(act, nmx_ready, c + 1)
                    wait_for(act, p_turned, c - 1)
                    wait_for(act, pv_ready, c - 1)
                    act.activation(probs[odd][:, :], psS, ACT.Exp, bias=nmx[odd][:, :], scale=SCALE,
                                   accum_out=rowsum[odd][:, :]).then_inc(p_ready, 1)
                if front:
                    context_copy(f, even, 1)
                if last_one:
                    wait_for(act, r_done, a + 1)
                    copy(ret_q[:, ds(a * D, D)], psR).then_inc(r_copied, 1)
                if back:
                    wait_for(act, pv_turned, b + 1)
                    wait_for(act, y_done, b - 1)
                    copy(pvT[even][:, :, :], psT).then_inc(pvT_ready, 1)
                if front:
                    wait_for(act, xn_turned, f + 1)
                    wait_for(act, q_done, f - 1)
                    copy(xnT[even][:, :, :], psX).then_inc(xnT_ready, 1)
                    context_copy(f, even, 3)
                    wait_for(act, q_done, f + 1)
                    wait_for(act, s_done, f - 1)
                    copy(qT[even][:, :, :], psX).then_inc(qT_ready, 1)

            iterations(act, step)

        @block.vector
        def _(dve):
            dve.wait_ge(m.made, m.all_made + 1)
            dve.wait_ge(w_product_copied, 2)

            def context_copy(f, pf, j):
                wait_for(dve, ctx_turned[j], f + 1)
                wait_for(dve, s_done, f - 1)
                dve.tensor_copy(ctxT[pf][:, j, :, 0:2 * P], psC[j % 2][:, :].rearrange("p (c n) -> p c n", c=DC)) \
                    .then_inc(ctxT_ready[j], 1)

            def moments(src, g, st, ag, rs, bn6, bn2):
                dve.bn_stats(bn6[:, :], src).then_inc(st, 1)
                wait_for(dve, rs, g - 1)
                wait_alone(dve, st, g + 1, seen)
                dve.bn_aggr(bn2[:, :], bn6[:, :]).then_inc(ag, 1)

            def normalise(src, g, ag, rs, bn2, rstd, dst, free, free_at, ready):
                wait_for(dve, rs, g + 1)
                wait_for(dve, ag, g + 1)
                wait_for(dve, free, free_at)
                dve.tensor_scalar(dst, src, bn2[:, 0:1], rstd[:, :], ALU.subtract, ALU.mult).then_inc(ready, 1)

            def step(i, r, front, mid, back, last_one):
                f, c, b, a = i, i - 1, i - 2, i - 3
                even, odd = r % 2, (r + 1) % 2
                if isinstance(i, int) and i == 0:
                    dve.wait_ge(x_first, 16)
                if isinstance(i, int) and i == NR - 1:
                    dve.wait_ge(x_rest, 16 * (X_CHUNKS - 1))
                if front:
                    moments(x_all[:, ds(f * D, D)], f, st_a, ag_a, rs_a, bn6a[even], bn2a[even])
                if back:
                    wait_for(dve, pv_done, b + 1)
                    wait_for(dve, p_ready, b + 1)
                    wait_for(dve, pv_turned, b - 1)
                    dve.scalar_tensor_tensor(out=pv[even][:, :], in0=last_rows[(r + 2) % NR][:, :],
                                             scalar=probs[even][:, 2 * P:KEYS], in1=psPV, op0=ALU.mult,
                                             op1=ALU.add).then_inc(pv_ready, 1)
                if mid:
                    wait_for(dve, s_done, c + 1)
                    dve.reduce_max(mx[odd][:, :], psS, AX.X).then_inc(mx_done, 1)
                    wait_for(dve, mx_done, c + 1)
                    wait_for(dve, p_ready, c - 1)
                    dve.tensor_scalar(nmx[odd][:, :], mx[odd][:, :], -SCALE, None, ALU.mult).then_inc(nmx_ready, 1)
                if front:
                    wait_for(dve, last_turned, f + 1)
                    wait_for(dve, s_done, f - 1)
                    dve.tensor_copy(ctxT[even][:, :, :, 2 * P:KEYS].rearrange("p b c o -> p c (b o)"), psL) \
                        .then_inc(lastT_ready, 1)
                    context_copy(f, even, 0)
                if last_one:
                    wait_for(dve, xn2_ready, a + 1)
                    dve.tensor_tensor_reduce(out=vprod[:, :], in0=xn2[odd][:, :], in1=wv_sum[:, :], scale=1.0,
                                             scalar=0.0, op0=ALU.mult, op1=ALU.add,
                                             accum_out=vs[odd][:, :]).then_inc(vs_done, 1)
                if mid:
                    wait_for(dve, p_ready, c + 1)
                    dve.reciprocal(rinv[odd][:, :], rowsum[odd][:, :]).then_inc(rinv_done, 1)
                if front:
                    normalise(x_all[:, ds(f * D, D)], f, ag_a, rs_a, bn2a[even], rstd_a[even],
                              xn[even][:, :], xn_turned, f - 1, xn_ready)
                if mid:
                    wait_for(dve, p_turned, c + 1)
                    wait_for(dve, pv_done, c - 1)
                    dve.tensor_copy(pT[odd][:, :, :], psP[:, 0:2 * P].rearrange("p (c n) -> p c n", c=2)) \
                        .then_inc(pT_ready, 1)
                if last_one:
                    wait_for(dve, vs_done, a + 1)
                    wait_for(dve, u_added, a)
                    dve.scalar_tensor_tensor(out=m.u_rows[:, :], in0=xn2[odd][:, :], scalar=vs[odd][:, :],
                                             in1=m.u_rows[:, :], op0=ALU.mult, op1=ALU.add).then_inc(u_added, 1)
                if back:
                    wait_for(dve, y_done, b + 1)
                    wait_for(dve, rinv_done, b + 1)
                    xs = x_all[:, ds(b * D, D)]
                    dve.scalar_tensor_tensor(out=xs, in0=psY, scalar=rinv[even][:, :], in1=xs, op0=ALU.mult,
                                             op1=ALU.add).then_inc(x2_ready, 1)
                    wait_alone(dve, x2_ready, b + 1, seen)
                    moments(x_all[:, ds(b * D, D)], b, st_b, ag_b, rs_b, bn6b[even], bn2b[even])
                if front:
                    context_copy(f, even, 2)
                if back:
                    normalise(x_all[:, ds(b * D, D)], b, ag_b, rs_b, bn2b[even], rstd_b[even],
                              xn2[even][:, :], xn2_turned, b - 1, xn2_ready)

            iterations(dve, step)


def two_deep(eng, steps, tail, step):
    for i in range(4):
        step(i, i % 2)
    pairs = steps // 2
    with eng.Fori(2, pairs) as k:
        for r in range(2):
            step(k * 2 + r, r)
    for i in range(2 * pairs, steps + tail):
        step(i, i % 2)


def retention(nc, new, m, psum, kept):
    sb, sem = new.sb, new.sem
    C = 4
    NCH = NG // C
    W = C * D
    ident, x_all, ret_q, xnT = m.ident, m.x_all, m.ret_q, m.xnT
    u = sb("u", [T, D])
    uT = sb("uT", [P, DC, T])
    state = [sb(f"state{i}", [P, DC, T]) for i in range(2)]
    spread = sb("spread", [P, GB, GB, T])
    s_rows = sb("s_rows", [P, D])
    bn6 = [sb(f"bn6_{i}", [P, C, 6]) for i in range(2)]
    bn2 = [sb(f"bn2_{i}", [P, C, 2]) for i in range(2)]
    veps = sb("veps", [P, C])
    rstd = [sb(f"rstd_{i}", [P, C]) for i in range(2)]
    nmr = [sb(f"nmr_{i}", [P, C]) for i in range(2)]
    half4 = sb("half4", [P, C])
    xn3 = [sb(f"xn3_{i}", [P, C, D]) for i in range(2)]
    SPANS = [1, 2, 4, 8, 16]
    STEPS = len(SPANS) + 2
    final = state[len(SPANS) % 2]
    psT = psum[0:2]
    psU = psum[4][0:T, 0:D]
    psM, psRows, m.psMean = psum[2], psum[3], psum[7]
    m.psMean_v = psum[7][:, 0:DC * B].rearrange("p (c b) -> p c b", c=DC)

    names = ("u_summed", "u_copied", "u_turned", "uT_copied", "m_done", "scan", "consts_made", "rows_done",
             "rows_copied", "q_scaled", "x3_done", "st_done", "ag_done", "veps_done", "rstd_done", "nmr_done",
             "xn_done", "mean_done", "kept_ready", "stored", "pads")
    s = {n: sem("r_" + n) for n in names}
    turned = [sem(f"r_turned{j}") for j in range(2)]
    copied = [sem(f"r_copied{j}") for j in range(2)]
    kept_v = kept.rearrange("(g p) d -> p g d", p=P)

    with nc.Block() as block:

        @block.sync
        def _(sp):
            with sp.Fori(0, NCH) as i:
                sp.wait_ge(s["kept_ready"], i + 1)
                sp.dma_start(kept_v[:, ds(i * C, C), :],
                             x_all[:, ds(i * W, W)].rearrange("p (g d) -> p g d", d=D)).then_inc(s["stored"], 16)
            sp.wait_ge(s["stored"], 16 * NCH)

        @block.gpsimd
        def _(pool):
            for b in range(GB):
                last = pool.tensor_copy(spread[:, :, b, :], ident[:, :].rearrange("p (q i) -> p q i", q=GB))
            last.then_inc(s["consts_made"], 1)
            pool.memset(half4[:, :], -0.5).then_inc(s["consts_made"], 1)
            pool.memset(xnT[:, :, B * T:], 0.0).then_inc(s["pads"], 1)
            pool.wait_ge(s["consts_made"], 2)
            pool.wait_ge(s["rows_copied"], 1)

            def step(i, r):
                if is_in(i, 0, NCH - 1):
                    qs = ret_q[:, ds(i * W, W)].rearrange("p (g d) -> p g d", d=D)
                    pool.tensor_tensor(qs, qs, s_rows[:, :].unsqueeze(1).to_broadcast([P, C, D]), ALU.mult) \
                        .then_inc(s["q_scaled"], 1)
                if is_in(i, 1, NCH):
                    j, rj = i - 1, 1 - r
                    wait_for(pool, s["nmr_done"], i - 2)
                    wait_for(pool, s["xn_done"], i - 2)
                    wait_for(pool, s["rstd_done"], i - 1)
                    wait_alone(pool, s["ag_done"], i, m.pool_seen)
                    pool.tensor_scalar(veps[:, :], bn2[rj][:, :, 1], EPS, None, ALU.add).then_inc(s["veps_done"], 1)
                    wait_for(pool, s["veps_done"], i)
                    pool.tensor_tensor(rstd[rj][:, :], veps[:, :], half4[:, :], ALU.pow).then_inc(s["rstd_done"], 1)
                if is_in(i, 2, NCH + 1):
                    xs = x_all[:, ds((i - 2) * W, W)]
                    wait_for(pool, s["xn_done"], i - 1)
                    pool.tensor_tensor(xs, xs, xn3[r][:, :, :].rearrange("p g d -> p (g d)"), ALU.add).then_inc(s["kept_ready"], 1)

            two_deep(pool, NCH, 2, step)

        @block.vector
        def _(dve):
            dve.wait_ge(s["u_summed"], 1)
            dve.tensor_copy(u[:, :], psU).then_inc(s["u_copied"], 1)
            dve.wait_ge(s["m_done"], 1)
            mT = psM[:, 0:DC * T].rearrange("p (c t) -> p c t", c=DC)
            dve.tensor_copy(state[0][:, :, :], mT).then_inc(s["scan"], 1)
            for n, span in enumerate(SPANS):
                a, b = state[n % 2], state[(n + 1) % 2]
                dve.wait_ge(s["scan"], n + 1)
                dve.tensor_copy(b[:, :, 0:1 + span], a[:, :, 0:1 + span])
                dve.scalar_tensor_tensor(out=b[:, :, 1 + span:], in0=a[:, :, 1:T - span], scalar=GAMMA ** span,
                                         in1=a[:, :, 1 + span:], op0=ALU.mult, op1=ALU.add).then_inc(s["scan"], 1)
            dve.wait_ge(s["scan"], STEPS - 1)
            dve.tensor_copy(final[:, :, 0:1], final[:, :, 1:2]).then_inc(s["scan"], 1)
            dve.wait_ge(s["rows_done"], 1)
            dve.tensor_copy(s_rows[:, :].rearrange("p (t c q) -> p q c t", c=DC, q=GB),
                            psRows[:, 0:D].rearrange("p (q c t) -> p q c t", q=GB, c=DC)).then_inc(s["rows_copied"], 1)

            def step(i, r):
                if is_in(i, 0, NCH - 1):
                    xs = x_all[:, ds(i * W, W)]
                    wait_for(dve, s["q_scaled"], i + 1)
                    dve.tensor_tensor(xs, xs, ret_q[:, ds(i * W, W)], ALU.add).then_inc(s["x3_done"], 1)
                    wait_for(dve, s["nmr_done"], i - 1)
                    wait_for(dve, s["rstd_done"], i - 1)
                    wait_alone(dve, s["x3_done"], i + 1, m.seen)
                    for g in range(C):
                        last = dve.bn_stats(bn6[r][:, g, :], x_all[:, ds(i * W + g * D, D)])
                    last.then_inc(s["st_done"], 1)
                    wait_alone(dve, s["st_done"], i + 1, m.seen)
                    for g in range(C):
                        last = dve.bn_aggr(bn2[r][:, g, :], bn6[r][:, g, :])
                    last.then_inc(s["ag_done"], 1)
                if is_in(i, 1, NCH):
                    rj = 1 - r
                    wait_for(dve, s["rstd_done"], i)
                    wait_for(dve, s["ag_done"], i)
                    wait_for(dve, s["xn_done"], i - 2)
                    dve.scalar_tensor_tensor(out=nmr[rj][:, :], in0=bn2[rj][:, :, 0], scalar=-1.0, in1=rstd[rj][:, :],
                                             op0=ALU.mult, op1=ALU.mult).then_inc(s["nmr_done"], 1)

            two_deep(dve, NCH, 1, step)

        @block.tensor
        def _(pe):
            pe.matmul(psU, m.time_mask[:, :], m.u_rows[:, :], start=True, stop=True).then_inc(s["u_summed"], 1)
            pe.wait_ge(s["u_copied"], 1)
            for dc in range(DC):
                last = pe.transpose(psT[0][:, dc * T:(dc + 1) * T], u[:, dc * P:(dc + 1) * P], ident[0:T, 0:T])
            last.then_inc(s["u_turned"], 1)
            pe.wait_ge(s["uT_copied"], 1)
            for ec in range(DC):
                for dc in range(DC):
                    last = pe.matmul(psM[:, ec * T:(ec + 1) * T], m.a_wk[:, dc, ec * P:(ec + 1) * P], uT[:, dc, :],
                                     start=(dc == 0), stop=(dc == DC - 1))
            last.then_inc(s["m_done"], 1)
            pe.wait_ge(s["consts_made"], 1)
            pe.wait_ge(s["scan"], STEPS)
            for q in range(GB):
                last = pe.matmul(psRows[:, q * DC * T:(q + 1) * DC * T], spread[:, q, :, :].rearrange("p b i -> p (b i)"),
                                 final[:, :, :].rearrange("p c t -> p (c t)"), start=True, stop=True)
            last.then_inc(s["rows_done"], 1)

            def step(i, r):
                if is_in(i, 1, NCH):
                    j = 1 - r
                    for h in range(2):
                        wait_for(pe, copied[h], i - 1)
                        wait_for(pe, s["xn_done"], i)
                        for dc in range(DC):
                            for g in range(2):
                                o = (dc * 2 + g) * P
                                last = pe.transpose(psT[h][:, o:o + P], xn3[j][:, 2 * h + g, dc * P:(dc + 1) * P],
                                                    ident[:, :])
                        last.then_inc(turned[h], 1)
                    for dc in range(DC):
                        for g in range(C):
                            last = pe.matmul(m.psMean[:, ds((i - 1) * (C * GB) + dc * B + g * GB, GB)],
                                             xn3[j][:, g, dc * P:(dc + 1) * P], m.batch_mask[:, :],
                                             start=True, stop=True)
                    last.then_inc(s["mean_done"], 1)

            two_deep(pe, NCH, 1, step)

        @block.scalar
        def _(act):
            act.wait_ge(s["u_turned"], 1)
            act.activation(uT[:, :, :], psT[0][:, 0:DC * T].rearrange("p (c t) -> p c t", c=DC), ACT.Copy) \
                .then_inc(s["uT_copied"], 1)

            def step(i, r):
                if is_in(i, 1, NCH):
                    j = 1 - r
                    wait_for(act, s["nmr_done"], i)
                    wait_for(act, s["kept_ready"], i - 2)
                    wait_for(act, s["mean_done"], i - 2)
                    for g in range(C):
                        last = act.activation(xn3[j][:, g, :], x_all[:, ds((i - 1) * W + g * D, D)], ACT.Identity,
                                              bias=nmr[j][:, g:g + 1], scale=rstd[j][:, g:g + 1])
                    last.then_inc(s["xn_done"], 1)
                    for h in range(2):
                        wait_for(act, turned[h], i)
                        act.activation(xnT[:, :, ds((i - 1) * (C * P) + h * 2 * P, 2 * P)],
                                       psT[h][:, :].rearrange("p (c n) -> p c n", c=DC), ACT.Copy).then_inc(copied[h], 1)

            two_deep(act, NCH, 1, step)


def is_in(i, first, last):
    return not isinstance(i, int) or first <= i <= last


def router(nc, new, m, psum, w1, b1, w2, b2):
    sb, sem = new.sb, new.sem
    NSTEP = B // SLOTS
    w1_sb, w2_sb = sb("w1_sb", [P, DC, HID]), sb("w2_sb", [HID, E])
    b1_sb, b2_sb = sb("b1_sb", [HID, 1]), sb("b2_sb", [1, E])
    mean, hid = sb("mean", [P, DC, B]), sb("hid", [HID, B])
    before = sb("before", [P, P])
    lower = sb("lower", [P, E, E])
    slot_no = sb("slot_no", [P, NSLOT])
    pad_plan = sb("pad_plan", [2, NSLOT])
    job = [sb(f"job{k}", [P, 2]) for k in range(TOP)]
    expert_no = sb("expert_no", [P, E])
    steps = [sb(f"steps{n}", [P, NSTEP]) for n in range(2)]
    small = lambda name: sb(name, [P, E])
    mx, nmx, total, inv = (sb(n, [P, 1]) for n in ("r_mx", "r_nmx", "r_total", "r_inv"))
    ex, probs, rank, picked, share, weight = (small("r_" + n) for n in ("ex", "probs", "rank", "picked", "share", "weight"))
    count, pairs, halves, odd, pair0, odd0, place, alone, slot, behind = (
        small("r_" + n) for n in ("count", "pairs", "halves", "odd", "pair0", "odd0", "place", "alone", "slot", "behind"))
    n_pairs, first_odd = sb("n_pairs", [P, 1]), sb("first_odd", [P, 1])
    cnt_cmp = [sb(f"cnt_cmp{n}", [P, E, NSTEP]) for n in range(2)]
    cmp, cmp2 = sb("cmp", [P, E, E]), sb("cmp2", [P, E, E])
    slot_k, weight_k = sb("slot_k", [P, TOP]), sb("weight_k", [P, TOP])
    pick_k = sb("pick_k", [P, E])
    scratch = sb("scratch", [P, E])
    hot = [sb(f"hot{k}", [P, NSLOT]) for k in range(TOP)]
    wide = [sb(f"wide{k}", [P, P]) for k in range(TOP)]
    row, row2 = sb("row", [2, NSLOT]), sb("row2", [2, NSLOT])

    psH, psLg, psPos, psCnt, psW, psCol = psum[0][0:HID, 0:B], psum[1][:, 0:E], psum[2][:, 0:E], psum[3][:, 0:E], \
        psum[4][:, 0:NSLOT], psum[5][0:2, 0:NSLOT]
    loaded, made, mean_copied, h_done, hid_ready, lg_done, nmx_ready, ex_ready, picked_ready, pos_done, \
        hot_ready, wide_ready, w_done, col_done, w_copied, v = (
            sem("o_" + n) for n in ("loaded", "made", "mean_copied", "h_done", "hid_ready", "lg_done", "nmx_ready",
                                    "ex_ready", "picked_ready", "pos_done", "hot_ready", "wide_ready", "w_done",
                                    "col_done", "w_copied", "steps"))

    with nc.Block() as block:

        @block.sync
        def _(sp):
            sp.dma_start(w1_sb[:, :, :], w1.rearrange("(c p) n -> p c n", p=P)).then_inc(loaded, 16)
            sp.dma_start(w2_sb[:, :], w2).then_inc(loaded, 16)
            sp.dma_start(b1_sb[:, :], b1.rearrange("(n a) -> n a", a=1)).then_inc(loaded, 16)
            sp.dma_start(b2_sb[:, :], b2.rearrange("(a n) -> a n", a=1)).then_inc(loaded, 16)

        @block.gpsimd
        def _(pool):
            n, step = m.const_steps, m.const_step

            def done(ins):
                n[0] += 1
                ins.then_inc(step, 1)
                pool.wait_ge(step, n[0])

            done(pool.memset(before[:, :], 1.0))
            done(pool.affine_select(out=before[:, :], in_=before[:, :], compare_op=ALU.is_ge, fill=0.0, base=-1,
                                    pattern=[[1, P]], channel_multiplier=-1))
            done(pool.memset(lower[:, :, :], 1.0))
            done(pool.affine_select(out=lower[:, :, :], in_=lower[:, :, :], compare_op=ALU.is_ge, fill=0.0, base=-1,
                                    pattern=[[1, E], [-1, E]], channel_multiplier=0))
            whole = dict(allow_small_or_imprecise_dtypes=True)
            pool.iota(slot_no[:, :], pattern=[[1, NSLOT]], base=0, channel_multiplier=0, **whole)
            done(pool.iota(pad_plan[:, :].rearrange("p (i s) -> p i s", s=UNIT), pattern=[[0, UNITS], [T, UNIT]],
                           base=B * T + 1, channel_multiplier=0, **whole))
            pool.affine_select(out=pad_plan[:, :], in_=pad_plan[:, :], compare_op=ALU.is_ge, fill=1.0, base=0,
                               pattern=[[0, NSLOT]], channel_multiplier=-1)
            for k in range(TOP):
                pool.iota(job[k][:, 0:1], pattern=[[0, 1]], base=1, channel_multiplier=T, **whole)
            pool.iota(expert_no[:, :], pattern=[[1, E]], base=1, channel_multiplier=0, **whole)
            pool.iota(steps[0][:, :], pattern=[[SLOTS, NSTEP]], base=SLOTS, channel_multiplier=0, **whole)
            done(pool.iota(steps[1][:, :], pattern=[[SLOTS, NSTEP]], base=UNIT, channel_multiplier=0, **whole))
            pool.sem_inc(made, 1)

        @block.tensor
        def _(pe):
            pe.wait_ge(loaded, 64)
            pe.wait_ge(mean_copied, 1)
            for dc in range(DC):
                last = pe.matmul(psH, w1_sb[:, dc, :], mean[:, dc, :], start=(dc == 0), stop=(dc == DC - 1))
            last.then_inc(h_done, 1)
            pe.wait_ge(hid_ready, 1)
            pe.matmul(psLg, hid[:, :], w2_sb[:, :], start=True, stop=False)
            pe.matmul(psLg, m.ones[0:1, :], b2_sb[:, :], start=False, stop=True).then_inc(lg_done, 1)
            pe.wait_ge(picked_ready, 1)
            pe.wait_ge(made, 1)
            pe.matmul(psPos, before[:, :], picked[:, :], start=True, stop=True)
            pe.matmul(psCnt, m.ones[:, :], picked[:, :], start=True, stop=True).then_inc(pos_done, 1)
            for k in range(TOP):
                pe.wait_ge(hot_ready, k + 1)
                pe.matmul(psCol, job[k][:, :], hot[k][:, :], start=(k == 0), stop=(k == TOP - 1)) \
                    .then_inc(col_done, 1)
            for k in range(TOP):
                pe.wait_ge(wide_ready, k + 1)
                pe.matmul(psW, wide[k][:, :], hot[k][:, :], start=(k == 0), stop=(k == TOP - 1)).then_inc(w_done, 1)

        @block.scalar
        def _(act):
            act.activation(mean[:, :, :], m.psMean_v, ACT.Copy, scale=1.0 / T).then_inc(mean_copied, 1)
            act.wait_ge(loaded, 64)
            act.wait_ge(h_done, 1)
            act.activation(hid[:, :], psH, ACT.Tanh, bias=b1_sb[:, :]).then_inc(hid_ready, 1)
            act.wait_ge(nmx_ready, 1)
            act.activation(ex[:, :], psLg, ACT.Exp, bias=nmx[:, :], accum_out=total[:, :]).then_inc(ex_ready, 1)
            act.wait_ge(w_done, TOP)
            act.activation(m.slot_w[:, :], psW, ACT.Copy).then_inc(w_copied, 1)

        @block.vector
        def _(dve):
            n = [0]

            def done(ins):
                n[0] += 1
                ins.then_inc(v, 1)
                dve.wait_ge(v, n[0])

            by_j = lambda t: t[:, :].unsqueeze(1).to_broadcast([P, E, E])
            by_e = lambda t: t[:, :].unsqueeze(2).to_broadcast([P, E, E])
            dve.wait_ge(lg_done, 1)
            done(dve.reduce_max(mx[:, :], psLg, AX.X))
            dve.tensor_scalar(nmx[:, :], mx[:, :], -1.0, None, ALU.mult).then_inc(nmx_ready, 1)
            dve.wait_ge(ex_ready, 1)
            dve.wait_ge(made, 1)
            done(dve.reciprocal(inv[:, :], total[:, :]))
            done(dve.tensor_scalar(probs[:, :], ex[:, :], inv[:, :], None, ALU.mult))
            dve.tensor_tensor(cmp[:, :, :], by_j(probs), by_e(probs), ALU.is_gt)
            done(dve.tensor_tensor(cmp2[:, :, :], by_j(probs), by_e(probs), ALU.is_equal))
            done(dve.tensor_tensor(cmp2[:, :, :], cmp2[:, :, :], lower[:, :, :], ALU.mult))
            done(dve.tensor_tensor(cmp[:, :, :], cmp[:, :, :], cmp2[:, :, :], ALU.add))
            done(dve.reduce_sum(rank[:, :], cmp[:, :, :], AX.X))
            dve.tensor_scalar(picked[:, :], rank[:, :], float(TOP), None, ALU.is_lt).then_inc(picked_ready, 1)
            dve.wait_ge(picked_ready, 1)
            done(dve.tensor_tensor(share[:, :], probs[:, :], picked[:, :], ALU.mult))
            done(dve.reduce_sum(total[:, :], share[:, :], AX.X))
            done(dve.reciprocal(inv[:, :], total[:, :]))
            done(dve.tensor_scalar(weight[:, :], share[:, :], inv[:, :], None, ALU.mult))
            dve.wait_ge(pos_done, 1)
            done(dve.tensor_copy(count[:, :], psCnt))
            by_k = lambda t, n: t[:, :].unsqueeze(2).to_broadcast([P, E, n])
            over_e = lambda t, n: t[:, :].unsqueeze(1).to_broadcast([P, E, n])
            dve.tensor_tensor(cnt_cmp[0][:, :, :], by_k(count, NSTEP), over_e(steps[1], NSTEP), ALU.is_gt)
            done(dve.tensor_scalar(halves[:, :], count[:, :], 0.0, None, ALU.is_gt))
            done(dve.reduce_sum(pairs[:, :], cnt_cmp[0][:, :, :], AX.X))
            done(dve.tensor_tensor(cnt_cmp[1][:, :, :], by_k(count, NSTEP), over_e(steps[0], NSTEP), ALU.is_gt))
            done(dve.reduce_sum(odd[:, :], cnt_cmp[1][:, :, :], AX.X))
            done(dve.tensor_tensor(odd[:, :], odd[:, :], halves[:, :], ALU.add))
            done(dve.tensor_tensor(odd[:, :], odd[:, :], pairs[:, :], ALU.subtract))
            dve.tensor_tensor(cmp[:, :, :], by_j(pairs), lower[:, :, :], ALU.mult)
            dve.tensor_tensor(cmp2[:, :, :], by_j(odd), lower[:, :, :], ALU.mult)
            done(dve.reduce_sum(n_pairs[:, :], pairs[:, :], AX.X))
            dve.reduce_sum(pair0[:, :], cmp[:, :, :], AX.X)
            dve.tensor_scalar(first_odd[:, :], n_pairs[:, :], float(BIG), float(SLOTS), ALU.max, ALU.mult)
            done(dve.reduce_sum(odd0[:, :], cmp2[:, :, :], AX.X))
            dve.tensor_copy(place[:, :], psPos)
            done(dve.tensor_scalar(behind[:, :], pairs[:, :], float(SLOTS), None, ALU.mult))
            dve.scalar_tensor_tensor(out=slot[:, :], in0=pair0[:, :], scalar=float(SLOTS), in1=place[:, :],
                                     op0=ALU.mult, op1=ALU.add)
            done(dve.tensor_tensor(place[:, :], place[:, :], behind[:, :], ALU.subtract))
            done(dve.scalar_tensor_tensor(out=alone[:, :], in0=odd0[:, :], scalar=float(UNIT), in1=place[:, :],
                                          op0=ALU.mult, op1=ALU.add))
            done(dve.tensor_scalar(alone[:, :], alone[:, :], first_odd[:, :], None, ALU.add))
            done(dve.tensor_tensor(alone[:, :], alone[:, :], slot[:, :], ALU.subtract))
            done(dve.scalar_tensor_tensor(out=alone[:, :], in0=place[:, :], scalar=0.0, in1=alone[:, :],
                                          op0=ALU.is_ge, op1=ALU.mult))
            done(dve.tensor_tensor(slot[:, :], slot[:, :], alone[:, :], ALU.add))
            for k in range(TOP):
                done(dve.tensor_scalar(pick_k[:, :], rank[:, :], float(k), None, ALU.is_equal))
                dve.tensor_tensor(scratch[:, :], pick_k[:, :], slot[:, :], ALU.mult)
                dve.tensor_tensor(count[:, :], pick_k[:, :], expert_no[:, :], ALU.mult)
                done(dve.tensor_tensor(share[:, :], pick_k[:, :], weight[:, :], ALU.mult))
                dve.reduce_sum(slot_k[:, k:k + 1], scratch[:, :], AX.X)
                dve.reduce_sum(job[k][:, 1:2], count[:, :], AX.X)
                done(dve.reduce_sum(weight_k[:, k:k + 1], share[:, :], AX.X))
                dve.tensor_scalar(hot[k][:, :], slot_no[:, :], slot_k[:, k:k + 1], None, ALU.is_equal) \
                    .then_inc(hot_ready, 1)
                dve.tensor_scalar(wide[k][:, :], m.ones[:, :], weight_k[:, k:k + 1], None, ALU.mult) \
                    .then_inc(wide_ready, 1)
            dve.wait_ge(col_done, TOP)
            done(dve.tensor_copy(row[:, :], psCol))
            done(dve.scalar_tensor_tensor(out=row2[:, :], in0=row[:, :], scalar=0.0, in1=pad_plan[:, :],
                                          op0=ALU.is_equal, op1=ALU.mult))
            done(dve.scalar_tensor_tensor(out=m.plan[:, :], in0=row[:, :], scalar=-1.0, in1=row2[:, :],
                                          op0=ALU.add, op1=ALU.add))


def experts(nc, new, m, psum, wa, wb):
    sb, sem = new.sb, new.sem
    R = mybir.dt.float32r
    N = SLOTS * T
    raw_a, raw_b = sb("raw_a", [P, DC, FF]), sb("raw_b", [P, FC, D])
    pair = lambda name, shape, n: [[sb(f"{name}{h}{i}", shape, R) for h in ("hi", "lo")] for i in range(n)]
    wa_s, wb_s = pair("wa_", [P, DC, FF], 2), pair("wb_", [P, FC, D], 2)
    cols = sb("cols", [P, DC, N])
    x_s = pair("x_", [P, DC, N], 2)
    act_out = [sb(f"act_out{i}", [P, N]) for i in range(2)]
    h_s = pair("h_", [P, N], 4)
    psH = psum[0:4]
    psZ = [psum[4:6], psum[6:8]]
    TERMS = ((0, 0), (0, 1), (1, 0))

    w_in_a, w_in_b, w_hi, w_lo, cols_ready, x_hi, x_lo, added, acc_zero = (
        sem("e_" + n) for n in ("w_in_a", "w_in_b", "w_hi", "w_lo", "cols_ready", "x_hi", "x_lo", "added", "acc_zero"))
    up_done, gelu_done, h_lo, down_done = (
        [sem(f"e_{n}{c}") for c in range(FC)] for n in ("up_done", "gelu_done", "h_lo", "down_done"))
    h_hi = [sem(f"e_h_hi{c}") for c in range(2)]

    def run(eng, step):
        size = lambda i: SLOTS if i < BIG else UNIT
        one = lambda i: step(i, i % 2, (size(i - 1), size(i), size(i + 1)))
        for i in range(-1, 2):
            one(i)
        with eng.Fori(1, (BIG - 1) // 2) as k:
            for r in range(2):
                step(k * 2 + r, r, (SLOTS,) * 3)
        for i in range(BIG - 1, BIG + 2):
            one(i)
        with eng.Fori((BIG + 2) // 2, (TILES - 1) // 2) as k:
            for r in range(2):
                step(k * 2 + 1 + r, 1 - r, (UNIT,) * 3)
        for i in range(BIG + 2 + 2 * ((TILES - 1) // 2 - (BIG + 2) // 2), TILES + 1):
            one(i)

    def slot_of(i, n):
        return i * SLOTS if n == SLOTS else i * UNIT + BIG * (SLOTS - UNIT)

    def registers(eng_type, tile, n):
        _, v = nc.values_load_multi_w_load_instructions(
            m.plan[0:1, ds(slot_of(tile, n), n)], engines=[eng_type], min_val=0, max_val=B * T + PAD - T)
        return v

    with nc.Block() as block:

        @block.sync
        def _(sp):
            def load(i, n):
                e = sp.value_load(m.plan[1:2, ds(slot_of(i, n), 1)], min_val=0, max_val=E - 1)
                wait_for(sp, w_lo, 2 * i - 1)
                sp.dma_start(raw_a[:, :, :], wa[ds(e, 1), :, :].rearrange("e (c p) f -> p (e c) f", p=P)) \
                    .then_inc(w_in_a, 16)
                wait_for(sp, w_lo, 2 * i)
                sp.dma_start(raw_b[:, :, :], wb[ds(e, 1), :, :].rearrange("e (c p) d -> p (e c) d", p=P)) \
                    .then_inc(w_in_b, 16)

            load(0, SLOTS)
            with sp.Fori(1, BIG) as i:
                load(i, SLOTS)
            with sp.Fori(BIG, TILES) as i:
                load(i, UNIT)

        @block.gpsimd
        def _(pool):
            pool.memset(m.acc[:, :, :], 0.0).then_inc(acc_zero, 1)

            def step(i, r, sizes):
                if is_in(i, -1, TILES - 2):
                    t, q, n = i + 1, 1 - r, sizes[2]
                    v = registers(mybir.EngineType.Pool, t, n)
                    wait_for(pool, x_hi, t)
                    wait_for(pool, x_lo, t)
                    for j in range(n):
                        last = pool.tensor_copy(cols[:, :, j * T:(j + 1) * T], m.xnT[:, :, ds(v[j], T)])
                    last.then_inc(cols_ready, 1)
                    wait_for(pool, down_done[FC - 1], t - 1)
                    wait_for(pool, w_hi, 2 * t + 1)
                    pool.tensor_tensor(wa_s[q][1][:, :, :], raw_a[:, :, :], wa_s[q][0][:, :, :].bitcast(F32),
                                       ALU.subtract).then_inc(w_lo, 1)
                    wait_for(pool, w_hi, 2 * t + 2)
                    pool.tensor_tensor(wb_s[q][1][:, :, :], raw_b[:, :, :], wb_s[q][0][:, :, :].bitcast(F32),
                                       ALU.subtract).then_inc(w_lo, 1)

            run(pool, step)

        @block.scalar
        def _(act):
            def ready(t, q, part, n):
                if part == 0:
                    wait_for(act, cols_ready, t + 1)
                    act.activation(x_s[q][0][:, :, 0:n * T], cols[:, :, 0:n * T], ACT.Copy).then_inc(x_hi, 1)
                if part == 1:
                    wait_for(act, w_in_a, 16 * t + 16)
                    wait_for(act, down_done[FC - 1], t - 1)
                if part == 3:
                    wait_for(act, w_in_b, 16 * t + 16)
                for k, (dst, src) in enumerate(((wa_s[q][0], raw_a), (wb_s[q][0], raw_b))):
                    for half in range(2):
                        if part == 1 + 2 * k + half:
                            h = src.shape[1] // 2
                            last = act.activation(dst[:, half * h:(half + 1) * h, :], src[:, half * h:(half + 1) * h, :],
                                                  ACT.Copy)
                            if half == 1:
                                last.then_inc(w_hi, 1)

            def step(i, r, sizes):
                for fc in range(FC):
                    if is_in(i, 0, TILES - 1):
                        w = sizes[1] * T
                        wait_for(act, up_done[fc], i + 1)
                        wait_for(act, h_lo[(fc - 2) % FC], i + 1 if fc >= 2 else i)
                        act.activation(act_out[fc % 2][:, 0:w], psH[fc % 4][:, 0:w], ACT.Gelu_apprx_tanh) \
                            .then_inc(gelu_done[fc], 1)
                    if is_in(i, -1, TILES - 2) and 2 <= fc:
                        ready(i + 1, 1 - r, fc - 2, sizes[2])

            run(act, step)

        @block.vector
        def _(dve):
            def combine(i, n, r, v, js):
                for j in js:
                    for dc in range(DC):
                        last = dve.scalar_tensor_tensor(
                            out=m.acc[:, dc, ds(v[j], T)], in0=psZ[r][dc][:, j * T:(j + 1) * T],
                            scalar=m.slot_w[:, ds(slot_of(i, n) + j, 1)], in1=m.acc[:, dc, ds(v[j], T)],
                            op0=ALU.mult, op1=ALU.add)
                return last

            def step(i, r, sizes):
                v = None
                for fc in range(FC):
                    if is_in(i, 0, TILES - 1):
                        w = sizes[1] * T
                        g = act_out[fc % 2][:, 0:w]
                        hi, lo = (h[:, 0:w] for h in h_s[fc % 4])
                        wait_for(dve, gelu_done[fc], i + 1)
                        wait_for(dve, down_done[(fc - 4) % FC], i + 1 if fc >= 4 else i)
                        dve.tensor_copy(hi, g).then_inc(h_hi[fc % 2], 1)
                        wait_for(dve, h_hi[fc % 2], i * (FC // 2) + fc // 2 + 1)
                        dve.tensor_tensor(lo, g, hi.bitcast(F32), ALU.subtract).then_inc(h_lo[fc], 1)
                    if is_in(i, 1, TILES) and fc == 2:
                        v = registers(mybir.EngineType.DVE, i - 1, sizes[0])
                        if isinstance(i, int) and i == 1:
                            dve.wait_ge(acc_zero, 1)
                        wait_for(dve, down_done[FC - 1], i)
                        wait_for(dve, added, i - 1)
                    if is_in(i, 1, TILES) and 3 <= fc < 7:
                        q = sizes[0] // 4
                        last = combine(i - 1, sizes[0], 1 - r, v, range((fc - 3) * q, (fc - 2) * q))
                        if fc == 6:
                            last.then_inc(added, 1)
                    if is_in(i, -1, TILES - 2) and fc == 3:
                        q, w = 1 - r, sizes[2] * T
                        wait_for(dve, x_hi, i + 2)
                        dve.tensor_tensor(x_s[q][1][:, :, 0:w], cols[:, :, 0:w], x_s[q][0][:, :, 0:w].bitcast(F32),
                                          ALU.subtract).then_inc(x_lo, 1)

            run(dve, step)

        @block.tensor
        def _(pe):
            def up(i, r, fc, w):
                if fc == 0:
                    wait_for(pe, x_hi, i + 1)
                    wait_for(pe, x_lo, i + 1)
                    wait_for(pe, w_lo, 2 * i + 1)
                wait_for(pe, gelu_done[(fc - 4) % FC], i + 1 if fc >= 4 else i)
                n = 0
                for dc in range(DC):
                    for a, b in TERMS:
                        last = pe.matmul(psH[fc % 4][:, 0:w], wa_s[r][a][:, dc, fc * P:(fc + 1) * P], x_s[r][b][:, dc, 0:w],
                                         start=(n == 0), stop=(n == 2 * len(TERMS) - 1))
                        n += 1
                last.then_inc(up_done[fc], 1)

            def down(i, r, fc, w):
                wait_for(pe, h_lo[fc], i + 1)
                if fc == 0:
                    wait_for(pe, w_lo, 2 * i + 2)
                    wait_for(pe, added, i - 1)
                for dc in range(DC):
                    for n, (a, b) in enumerate(TERMS):
                        last = pe.matmul(psZ[r][dc][:, 0:w], wb_s[r][a][:, fc, dc * P:(dc + 1) * P], h_s[fc % 4][b][:, 0:w],
                                         start=(fc == 0 and n == 0), stop=(fc == FC - 1 and n == len(TERMS) - 1))
                last.then_inc(down_done[fc], 1)

            def step(i, r, sizes):
                for fc in range(FC):
                    if is_in(i, 0, TILES - 1):
                        up(i, r, fc, sizes[1] * T)
                        if fc >= 2:
                            down(i, r, fc - 2, sizes[1] * T)
                    if is_in(i, 1, TILES) and fc < 2:
                        down(i - 1, 1 - r, FC - 2 + fc, sizes[0] * T)

            run(pe, step)


def finish(nc, new, m, psum, kept, out):
    sb, sem = new.sb, new.sem
    G, BUF = 2, 4
    STEPS = NG // G
    base = [sb(f"base{i}", [P, G * D]) for i in range(BUF)]
    res = [sb(f"res{i}", [P, G * D]) for i in range(BUF)]
    loaded = [sem(f"f_loaded{i}") for i in range(BUF)]
    stored = [sem(f"f_stored{i}") for i in range(BUF)]
    turned, added = sem("f_turned"), sem("f_added")
    kept_v = kept.rearrange("(g p) d -> p g d", p=P)
    out_v = out.rearrange("(g p) d -> p g d", p=P)
    split = lambda t: t[:, :].rearrange("p (g d) -> p g d", d=D)

    def rounds(eng, step):
        for r in range(BUF):
            step(r, r)
        with eng.Fori(1, STEPS // BUF) as k:
            for r in range(BUF):
                step(k * BUF + r, r)

    with nc.Block() as block:

        @block.sync
        def _(sp):
            def step(i, r):
                wait_for(sp, added, i - (BUF - 1))
                sp.dma_start(split(base[r]), kept_v[:, ds(i * G, G), :]).then_inc(loaded[r], 16)

            rounds(sp, step)

        @block.tensor
        def _(pe):
            for i in range(STEPS):
                if i >= BUF:
                    pe.wait_ge(added, i - (BUF - 1))
                for g in range(G):
                    for dc in range(DC):
                        o = g * D + dc * P
                        last = pe.transpose(psum[i % BUF][:, o:o + P],
                                            m.acc[:, dc, (i * G + g) * P:(i * G + g + 1) * P], m.ident[:, :])
                last.then_inc(turned, 1)

        @block.vector
        def _(dve):
            def step(i, r):
                wait_for(dve, loaded[r], (i - r) * (16 // BUF) + 16)
                wait_for(dve, stored[r], (i - r) * (16 // BUF))
                wait_for(dve, turned, i + 1)
                dve.tensor_tensor(res[r][:, :], psum[r][:, :], base[r][:, :], ALU.add).then_inc(added, 1)

            rounds(dve, step)

        @block.scalar
        def _(act):
            def step(i, r):
                wait_for(act, added, i + 1)
                act.dma_start(out_v[:, ds(i * G, G), :], split(res[r])).then_inc(stored[r], 16)

            rounds(act, step)
            for r in range(BUF):
                act.wait_ge(stored[r], 16 * (STEPS // BUF))


class Room:

    def __init__(self, nc, stack, sems):
        self.nc, self.stack, self.sems = nc, stack, sems

    def sb(self, name, shape, dt=F32):
        return self.stack.enter_context(self.nc.sbuf_tensor(name, shape, dt))

    def sem(self, name):
        return self.sems.enter_context(self.nc.semaphore(name))


class Shared:
    pass


def program(nc, x, context, x_wq, x_wkv, a_wq, a_wk, a_wv, w1, b1, w2, b2, wa, wb, out):
    m = Shared()
    kept = nc.dram_tensor("kept", [B * T, D], F32, kind="Internal").ap()
    with ExitStack() as whole:
        new = Room(nc, whole, whole)
        psum = [whole.enter_context(nc.psum_tensor(f"bank{i}", [P, 512], F32)) for i in range(8)]
        constants(nc, new, m)
        m.xnT = new.sb("xnT", [P, DC, B * T + PAD])
        with ExitStack() as rows:
            held = Room(nc, rows, whole)
            m.x_all, m.ret_q = held.sb("x_all", [P, NG * D]), held.sb("ret_q", [P, NG * D])
            m.a_wk, m.u_rows = held.sb("a_wk", [P, DC, D]), held.sb("u_rows", [P, D])
            with ExitStack() as own:
                attention(nc, Room(nc, own, whole), m, psum, x.rearrange("b t d -> (b t) d"), context,
                          dict(x_wq=x_wq, x_wkv=x_wkv, a_wq=a_wq, a_wk=a_wk, a_wv=a_wv))
            with ExitStack() as own:
                retention(nc, Room(nc, own, whole), m, psum, kept)
        m.plan = new.sb("plan", [2, NSLOT], I32)
        m.slot_w = new.sb("slot_w", [P, NSLOT])
        m.acc = new.sb("acc", [P, DC, B * T + PAD])
        with ExitStack() as own:
            router(nc, Room(nc, own, whole), m, psum, w1, b1, w2, b2)
        with ExitStack() as own:
            experts(nc, Room(nc, own, whole), m, psum, wa, wb)
        with ExitStack() as own:
            finish(nc, Room(nc, own, whole), m, psum, kept, out.rearrange("b t d -> (b t) d"))


_INS = ["x", "ctx_1024", "L0_xattn_Wq", "L0_xattn_Wkv", "L0_attn_Wq", "L0_attn_Wk", "L0_attn_Wv", "L0_ffn_W1",
        "L0_ffn_b1", "L0_ffn_W2", "L0_ffn_b2", "L0_ffn_Wa", "L0_ffn_Wb"]
_OUTS = [((128, 32, 256), "float32")]


def kernel(**inputs):
    import numpy as _np
    import concourse.bacc as _bacc
    from concourse import mybir as _mybir
    from concourse.bass_utils import run_bass_kernel_spmd as _run

    nc = _bacc.Bacc("TRN2", target_bir_lowering=False, num_devices=1)
    arrays, args = {}, []
    for name in _INS:
        a = _np.ascontiguousarray(inputs[name])
        arrays[f"in_{name}_dram"] = a
        args.append(nc.dram_tensor(f"in_{name}_dram", a.shape, _mybir.dt.from_np(a.dtype), kind="ExternalInput").ap())
    for i, (shape, dtype) in enumerate(_OUTS):
        dt = _mybir.dt.from_np(_np.dtype(dtype))
        args.append(nc.dram_tensor(f"out_{i}_dram", shape, dt, kind="ExternalOutput").ap())
    program(nc, *args)
    r = _run(nc, [arrays], core_ids=[0])
    return r.results[0]["out_0_dram"]
```

```python
from contextlib import ExitStack

import concourse.bass as bass
from concourse import mybir

F32 = mybir.dt.float32
I32 = mybir.dt.int32
F32R = mybir.dt.float32r
ALU = mybir.AluOpType
ACT = mybir.ActivationFunctionType
AX = mybir.AxisListType
ds = bass.ds

P = 128
B, T, D = 128, 32, 256
KEYS = 257
DC = D // P
GB = P // T
NG = B // GB
NR = 4
EPS = 1e-5
SCALE = 1.0 / 16.0
GAMMA = 0.96875
E, TOP, HID, FF = 8, 3, 64, 1024
FC = FF // P
UNIT, SLOTS = 8, 16
UNITS = (TOP * B + E * (UNIT - 1)) // UNIT
SMALL = 9
BIG = (UNITS - SMALL) // 2
TILES = BIG + SMALL
NSLOT = UNITS * UNIT
NSTEP = B // SLOTS
assert 2 * BIG + SMALL == UNITS
assert all(odd + 2 * max(0, (UNITS - odd) // 2 - BIG) <= SMALL for odd in range(E + 1))
GCOLS = P + GB
COLS = NG * GCOLS
PAD = SLOTS * T


def wait_for(eng, sem, count):
    if isinstance(count, int) and count <= 0:
        return
    eng.wait_ge(sem, count)


def wait_alone(eng, sem, count, seen):
    if isinstance(count, int) and count <= 0:
        return
    eng.wait_ge(sem, count)
    eng.sem_inc(seen, 1)


def turn(pe, out, rows, identity):
    return pe.transpose(out, rows, identity)


def constants(nc, new, m):
    m.ident_mask = new.sb("ident_mask", [P, GCOLS])
    m.ident = m.ident_mask[:, 0:P]
    m.batch_mask = m.ident_mask[:, P:GCOLS]
    m.ones = new.sb("ones", [P, P])
    m.time_mask = new.sb("time_mask", [P, T])
    m.minus_half = new.sb("minus_half", [P, 1])
    m.made = new.sem("made")
    m.seen, m.pool_seen, m.sp_seen = (new.sem(n) for n in ("seen", "pool_seen", "sp_seen"))

    m.const_step = new.sem("const_step")
    n = [0]

    def build(pool):
        step = m.const_step

        def done(ins):
            n[0] += 1
            ins.then_inc(step, 1)
            pool.wait_ge(step, n[0])

        done(pool.memset(m.ident[:, :], 0.0))
        pool.affine_select(out=m.ident[:, :], in_=m.ident[:, :], compare_op=ALU.not_equal, fill=1.0,
                           base=0, pattern=[[-1, P]], channel_multiplier=1).then_inc(m.made, 1)
        pool.memset(m.ones[:, :], 1.0).then_inc(m.made, 1)
        done(pool.memset(m.minus_half[:, :], -0.5))
        done(pool.memset(m.batch_mask[:, :], 1.0))
        done(pool.affine_select(out=m.batch_mask[:, :], in_=m.batch_mask[:, :], compare_op=ALU.is_ge,
                                fill=0.0, base=0, pattern=[[-T, GB]], channel_multiplier=1))
        pool.affine_select(out=m.batch_mask[:, :], in_=m.batch_mask[:, :], compare_op=ALU.is_ge,
                           fill=0.0, base=T - 1, pattern=[[T, GB]], channel_multiplier=-1).then_inc(m.made, 1)
        done(pool.memset(m.time_mask[:, :], 0.0))
        for j in range(GB):
            last = pool.affine_select(out=m.time_mask[:, :], in_=m.time_mask[:, :], compare_op=ALU.not_equal,
                                      fill=1.0, base=-T * j, pattern=[[-1, T]], channel_multiplier=1)
            if j < GB - 1:
                done(last)
        last.then_inc(m.made, 1)

    m.build_constants = build
    m.const_steps = n
    m.all_made = 4


def attention(nc, new, m, psum, x, context, w):
    sb, sem = new.sb, new.sem
    ring = lambda name, shape, n=2: [sb(f"{name}{i}", shape) for i in range(n)]
    ident, x_all, ret_q = m.ident, m.x_all, m.ret_q

    lent_xnT, lent_acc = (t[:, :, :].rearrange("p c n -> p (c n)") for t in (m.xnT, m.acc))
    CR, CT = GB * 2 * D, GB * DC * KEYS
    ctx_rows = [lent_acc[:, i * CR:(i + 1) * CR].rearrange("p (b c d) -> p b c d", b=GB, c=2) for i in range(NR)]
    ctxT = [lent_xnT[:, i * CT:(i + 1) * CT].rearrange("p (b c n) -> p b c n", b=GB, c=DC) for i in range(2)]
    last_rows = [lent_xnT[:, 2 * CT + i * D:2 * CT + (i + 1) * D] for i in range(NR)]
    ctx_last = ring("ctx_last", [GB, D], NR)
    xn = ring("xn", [P, D])
    xnT = ring("xnT_a", [P, DC, P])
    qT = ring("qT", [P, DC, P])
    probs = ring("probs", [P, KEYS])
    pT = ring("pT", [P, 2, P])
    pv = ring("pv", [P, D])
    pvT = ring("pvT", [P, DC, P])
    xn2 = ring("xn2", [P, D])
    xn2T = ring("xn2T", [P, DC, P])
    vprod, var_eps_a, var_eps_b = sb("vprod", [P, D]), sb("var_eps_a", [P, 1]), sb("var_eps_b", [P, 1])
    bn6a, bn2a, rstd_a = ring("bn6a", [P, 6]), ring("bn2a", [P, 2]), ring("rstd_a", [P, 1])
    bn6b, bn2b, rstd_b = ring("bn6b", [P, 6]), ring("bn2b", [P, 2]), ring("rstd_b", [P, 1])
    nmr_a = ring("nmr_a", [P, 1])
    mx, nmx, rowsum, rinv, vs = (ring(n, [P, 1]) for n in ("mx", "nmx", "rowsum", "rinv", "vs"))
    x_wq, x_wkv = sb("x_wq", [P, DC, D]), sb("x_wkv", [P, DC, 2 * D])
    a_wq, a_wv = sb("a_wq", [P, DC, D]), sb("a_wv", [P, DC, D])
    w_T = ring("w_T", [P, 2, D], 3)
    qk = sb("qk", [P, DC, D])
    wv_sum = sb("wv_sum", [P, D])

    chunked = lambda bank, n: bank[:, 0:DC * n].rearrange("p (c n) -> p c n", c=DC)
    psC = psum[0:2]
    psT = chunked(psum[2], P)
    psX = chunked(psum[3], P)
    psS = psum[4][:, 0:KEYS]
    psP = psum[5]
    psL = psum[5][:, 3 * P:3 * P + DC * GB].rearrange("p (c b) -> p c b", c=DC)
    psY = psR = psum[6][:, 0:D]
    psPV = psum[7][:, 0:D]

    xw_in, w_in, x_first, x_rest = sem("xw_in"), sem("w_in"), sem("x_first"), sem("x_rest")
    ctx_in = [sem(f"ctx_in{r}") for r in range(NR)]
    wT_done, wT_copied, w_product, w_product_copied = (
        sem(n) for n in ("wT_done", "wT_copied", "w_product", "w_product_copied"))
    seen, pool_seen = m.seen, m.pool_seen
    eps_a, eps_b, nmr_ready = sem("eps_a"), sem("eps_b"), sem("nmr_ready")
    st_a, ag_a, rs_a, st_b, ag_b, rs_b, mx_done, rinv_done, vs_done = (
        sem(n) for n in ("st_a", "ag_a", "rs_a", "st_b", "ag_b", "rs_b", "mx_done", "rinv_done", "vs_done"))
    xn_ready, xn_turned, xnT_ready, q_done, qT_ready = (
        sem(n) for n in ("xn_ready", "xn_turned", "xnT_ready", "q_done", "qT_ready"))
    ctx_turned = [sem(f"ctx_turned{j}") for j in range(GB)]
    ctxT_ready = [sem(f"ctxT_ready{j}") for j in range(GB)]
    last_turned, lastT_ready = sem("last_turned"), sem("lastT_ready")
    s_done, nmx_ready, p_ready, p_turned, pT_ready = (
        sem(n) for n in ("s_done", "nmx_ready", "p_ready", "p_turned", "pT_ready"))
    pv_done, pv_ready, pv_turned, pvT_ready, y_done, x2_ready = (
        sem(n) for n in ("pv_done", "pv_ready", "pv_turned", "pvT_ready", "y_done", "x2_ready"))
    xn2_ready, xn2_turned, xn2T_ready, r_done, r_copied, u_added = (
        sem(n) for n in ("xn2_ready", "xn2_turned", "xn2T_ready", "r_done", "r_copied", "u_added"))

    W_LOADS = 3
    X_CHUNKS = 8
    XC = NG // X_CHUNKS
    assert XC == NR
    x_v = x.rearrange("(g p) d -> p g d", p=P)
    rows_v = context[:, 0:2 * P, :].rearrange("b (p c) d -> p b c d", c=2)
    last_v = context[:, 2 * P, :]

    def iterations(eng, step):
        def one(i):
            step(i, i % NR, i + 1 < NG, 0 <= i < NG, 0 <= i - 1 < NG, 0 <= i - 2 < NG, i >= 3)

        for i in range(-1, NR):
            one(i)
        with eng.Fori(1, NG // NR - 1) as k:
            for r in range(NR):
                step(k * NR + r, r, True, True, True, True, True)
        for i in range(NG - NR, NG + 3):
            one(i)

    with nc.Block() as block:

        @block.gpsimd
        def _(pool):
            m.build_constants(pool)
            m.build_tables(pool)
            pool.memset(m.u_rows[:, :], 0.0).then_inc(m.made, 1)

            def rstd_of(g, ag, rs, eps_added, var_eps, bn2, rstd, ready):
                wait_for(pool, ready, g - 1)
                wait_alone(pool, ag, g + 1, pool_seen)
                pool.tensor_scalar(var_eps[:, :], bn2[:, 1:2], EPS, None, ALU.add).then_inc(eps_added, 1)
                wait_for(pool, eps_added, g + 1)
                pool.tensor_tensor(rstd[:, :], var_eps[:, :], m.minus_half[:, :], ALU.pow).then_inc(rs, 1)

            def step(i, r, ahead, front, mid, back, last_one):
                if back:
                    rstd_of(i - 2, ag_b, rs_b, eps_b, var_eps_b, bn2b[r % 2], rstd_b[r % 2], xn2_ready)
                if ahead:
                    e, q = i + 1, (r + 1) % 2
                    rstd_of(e, ag_a, rs_a, eps_a, var_eps_a, bn2a[q], rstd_a[q], xn_ready)
                    wait_alone(pool, rs_a, e + 1, pool_seen)
                    pool.tensor_scalar(nmr_a[q][:, :], bn2a[q][:, 0:1], rstd_a[q][:, :], -1.0, ALU.mult, ALU.mult) \
                        .then_inc(nmr_ready, 1)

            iterations(pool, step)

        @block.sync
        def _(sp):
            by_chunk = lambda v: v.rearrange("(c p) n -> p c n", p=P)
            for t, v in ((x_wq, w["x_wq"]), (x_wkv, w["x_wkv"])):
                sp.dma_start(t[:, :, :], by_chunk(v)).then_inc(xw_in, 16)
            sp.dma_start(x_all[:, 0:XC * D].rearrange("p (g d) -> p g d", d=D), x_v[:, 0:XC, :]).then_inc(x_first, 16)
            def load(g, r):
                wait_for(sp, pv_ready, g - (NR - 1))
                sp.dma_start(ctx_rows[r][:, :, :, :], rows_v[:, ds(g * GB, GB), :, :]).then_inc(ctx_in[r], 16)
                sp.dma_start(ctx_last[r][:, :], last_v[ds(g * GB, GB), :]).then_inc(ctx_in[r], 16)
                sp.dma_start(last_rows[r][:, :],
                             last_v[ds(g * GB, GB), :].unsqueeze(1).to_broadcast([GB, T, D])).then_inc(ctx_in[r], 16)

            load(0, 0)
            for t, v in ((a_wv, w["a_wv"]), (a_wq, w["a_wq"]), (m.a_wk, w["a_wk"])):
                sp.dma_start(t[:, :, :], by_chunk(v)).then_inc(w_in, 16)
            for g in range(1, NR):
                load(g, g)
            m.load_router(sp)
            for j in range(1, X_CHUNKS):
                sp.dma_start(x_all[:, j * XC * D:(j + 1) * XC * D].rearrange("p (g d) -> p g d", d=D),
                             x_v[:, j * XC:(j + 1) * XC, :]).then_inc(x_rest, 16)
            with sp.Fori(1, NG // NR) as k:
                for r in range(NR):
                    load(k * NR + r, r)

        @block.tensor
        def _(pe):
            pe.wait_ge(m.made, m.all_made)
            pe.wait_ge(xw_in, 32)
            def turn_weight(i, src):
                for kc in range(2):
                    for dc in range(DC):
                        o = kc * D + dc * P
                        last = turn(pe, psum[i][:, o:o + P], src[:, dc, kc * P:kc * P + P], ident[:, :])
                last.then_inc(wT_done, 1)

            turn_weight(0, x_wq)
            turn_weight(1, x_wkv)
            pe.wait_ge(wT_copied, 2)
            for dc in range(DC):
                for kc in range(2):
                    last = pe.matmul(psum[3][:, dc * D:(dc + 1) * D], w_T[0][:, kc, dc * P:(dc + 1) * P],
                                     w_T[1][:, kc, :], start=(kc == 0), stop=(kc == 1))
            last.then_inc(w_product, 1)
            pe.wait_ge(w_product_copied, 1)

            def retention_weights(i):
                if i == 0:
                    pe.wait_ge(w_in, 16 * W_LOADS)
                    turn_weight(2, a_wv)
                if i == 1:
                    pe.wait_ge(wT_copied, 3)
                    for kc in range(2):
                        last = pe.matmul(psum[6][:, 0:D], m.ones[:, :], w_T[2][:, kc, :], start=(kc == 0), stop=(kc == 1))
                    last.then_inc(w_product, 1)
                if i == 2:
                    pe.wait_ge(w_product_copied, 2)

            def turn_context(g, r, js):
                for j in js:
                    wait_for(pe, ctxT_ready[(j + 2) % GB], g + 1 if j >= 2 else g)
                    for dc in range(DC):
                        for c in range(2):
                            o = dc * 2 * P + c * P
                            last = turn(pe, psC[j % 2][:, o:o + P], ctx_rows[r][:, j, c, dc * P:(dc + 1) * P],
                                                ident[:, :])
                    last.then_inc(ctx_turned[j], 1)

            def step(i, r, ahead, front, mid, back, last_one):
                f, c, b, a = i, i - 1, i - 2, i - 3
                even, odd = r % 2, (r + 1) % 2
                rc = (r + NR - 1) % NR
                if isinstance(i, int) and i == 2:
                    retention_weights(i)
                if mid:
                    for j in range(GB):
                        wait_for(pe, ctxT_ready[j], c + 1)
                    wait_for(pe, lastT_ready, c + 1)
                    wait_for(pe, qT_ready, c + 1)
                    wait_for(pe, p_ready, c)
                    for dc in range(DC):
                        for j in range(GB):
                            last = pe.matmul(psS[j * T:(j + 1) * T, :], qT[odd][:, dc, j * T:(j + 1) * T],
                                             ctxT[odd][:, j, dc, :], start=(dc == 0), stop=(dc == DC - 1))
                    last.then_inc(s_done, 1)
                if back:
                    wait_for(pe, pv_ready, b + 1)
                    wait_for(pe, xn2T_ready, a)
                    for dc in range(DC):
                        last = turn(pe, psT[:, dc, :], pv[even][:, dc * P:(dc + 1) * P], ident[:, :])
                    last.then_inc(pv_turned, 1)
                if front:
                    wait_for(pe, pT_ready, c)
                    wait_for(pe, ctx_in[r], (f - r) * (48 // NR) + 48)
                    wait_for(pe, ctxT_ready[2], f)
                    turn_context(f, r, (0, 1))
                    for dc in range(DC):
                        last = turn(pe, psL[:, dc, :], ctx_last[r][:, dc * P:(dc + 1) * P], ident[0:GB, 0:GB])
                    last.then_inc(last_turned, 1)
                    wait_for(pe, xn_ready, f + 1)
                    wait_for(pe, qT_ready, f)
                    for dc in range(DC):
                        last = turn(pe, psX[:, dc, :], xn[even][:, dc * P:(dc + 1) * P], ident[:, :])
                    last.then_inc(xn_turned, 1)
                if back:
                    wait_for(pe, pvT_ready, b + 1)
                    wait_for(pe, r_copied, a)
                    for dc in range(DC):
                        last = pe.matmul(psY, pvT[even][:, dc, :], x_wkv[:, dc, D:2 * D], start=(dc == 0),
                                         stop=(dc == DC - 1))
                    last.then_inc(y_done, 1)
                if last_one:
                    wait_for(pe, xn2_ready, a + 1)
                    wait_for(pe, pvT_ready, b + 1 if back else NG)
                    for dc in range(DC):
                        last = turn(pe, psT[:, dc, :], xn2[odd][:, dc * P:(dc + 1) * P], ident[:, :])
                    last.then_inc(xn2_turned, 1)
                if mid:
                    wait_for(pe, p_ready, c + 1)
                    if front:
                        wait_for(pe, lastT_ready, f + 1)
                    for h in range(2):
                        last = turn(pe, psP[:, h * P:(h + 1) * P], probs[odd][:, h * P:(h + 1) * P], ident[:, :])
                    last.then_inc(p_turned, 1)
                if front:
                    turn_context(f, r, (2, 3))
                if last_one:
                    wait_for(pe, xn2T_ready, a + 1)
                    wait_for(pe, x2_ready, b + 1 if back else NG)
                    for dc in range(DC):
                        last = pe.matmul(psR, xn2T[odd][:, dc, :], a_wq[:, dc, :], start=(dc == 0), stop=(dc == DC - 1))
                    last.then_inc(r_done, 1)
                if front:
                    wait_for(pe, xnT_ready, f + 1)
                    for ec in range(DC):
                        for dc in range(DC):
                            last = pe.matmul(psX[:, ec, :], qk[:, dc, ec * P:(ec + 1) * P], xnT[even][:, dc, :],
                                             start=(dc == 0), stop=(dc == DC - 1))
                    last.then_inc(q_done, 1)
                if mid:
                    wait_for(pe, pT_ready, c + 1)
                    wait_for(pe, pv_ready, c)
                    for h in range(2):
                        for j in range(GB):
                            last = pe.matmul(psPV[j * T:(j + 1) * T, :], pT[odd][:, h, j * T:(j + 1) * T],
                                             ctx_rows[rc][:, j, h, :], start=(h == 0), stop=(h == 1))
                    last.then_inc(pv_done, 1)
                if isinstance(i, int) and i < 2:
                    retention_weights(i)

            iterations(pe, step)

        @block.scalar
        def _(act):
            copy = lambda o, i: act.activation(o, i, ACT.Copy)
            def copy_weight(i):
                act.wait_ge(wT_done, i + 1)
                copy(w_T[i][:, :, :], psum[i][:, :].rearrange("p (c n) -> p c n", c=2)).then_inc(wT_copied, 1)

            copy_weight(0)
            copy_weight(1)
            act.wait_ge(w_product, 1)
            copy(qk[:, :, :], psum[3][:, :].rearrange("p (c n) -> p c n", c=DC)).then_inc(w_product_copied, 1)

            def context_copy(f, pf, j):
                wait_for(act, ctx_turned[j], f + 1)
                wait_for(act, s_done, f - 1)
                copy(ctxT[pf][:, j, :, 0:2 * P], psC[j % 2][:, :].rearrange("p (c n) -> p c n", c=DC)) \
                    .then_inc(ctxT_ready[j], 1)

            def step(i, r, ahead, front, mid, back, last_one):
                f, c, b, a = i, i - 1, i - 2, i - 3
                even, odd = r % 2, (r + 1) % 2
                if front:
                    wait_for(act, nmr_ready, f + 1)
                    wait_for(act, xn_turned, f - 1)
                    act.activation(xn[even][:, :], x_all[:, ds(f * D, D)], ACT.Identity,
                                   bias=nmr_a[even][:, :], scale=rstd_a[even][:, :]).then_inc(xn_ready, 1)
                if back:
                    wait_for(act, pv_turned, b + 1)
                    wait_for(act, y_done, b - 1)
                    copy(pvT[even][:, :, :], psT).then_inc(pvT_ready, 1)
                if front:
                    context_copy(f, even, 1)
                    wait_for(act, xn_turned, f + 1)
                    wait_for(act, q_done, f - 1)
                    copy(xnT[even][:, :, :], psX).then_inc(xnT_ready, 1)
                if mid:
                    wait_for(act, nmx_ready, c + 1)
                    wait_for(act, p_turned, c - 1)
                    wait_for(act, pv_ready, c - 1)
                    act.activation(probs[odd][:, :], psS, ACT.Exp, bias=nmx[odd][:, :], scale=SCALE,
                                   accum_out=rowsum[odd][:, :]).then_inc(p_ready, 1)
                if last_one:
                    wait_for(act, xn2_turned, a + 1)
                    wait_for(act, r_done, a - 1)
                    copy(xn2T[odd][:, :, :], psT).then_inc(xn2T_ready, 1)
                if front:
                    context_copy(f, even, 2)
                    context_copy(f, even, 3)
                if last_one:
                    wait_for(act, r_done, a + 1)
                    copy(ret_q[:, ds(a * D, D)], psR).then_inc(r_copied, 1)
                if front:
                    wait_for(act, q_done, f + 1)
                    wait_for(act, s_done, f - 1)
                    copy(qT[even][:, :, :], psX).then_inc(qT_ready, 1)
                if isinstance(i, int) and i == 0:
                    copy_weight(2)
                if isinstance(i, int) and i == 1:
                    act.wait_ge(w_product, 2)
                    copy(wv_sum[:, :], psum[6][:, 0:D]).then_inc(w_product_copied, 1)

            iterations(act, step)

        @block.vector
        def _(dve):
            dve.wait_ge(m.made, m.all_made + 1)

            def context_copy(f, pf, j):
                wait_for(dve, ctx_turned[j], f + 1)
                wait_for(dve, s_done, f - 1)
                dve.tensor_copy(ctxT[pf][:, j, :, 0:2 * P], psC[j % 2][:, :].rearrange("p (c n) -> p c n", c=DC)) \
                    .then_inc(ctxT_ready[j], 1)

            def moments(src, g, st, ag, rs, bn6, bn2):
                dve.bn_stats(bn6[:, :], src).then_inc(st, 1)
                wait_for(dve, rs, g - 1)
                wait_alone(dve, st, g + 1, seen)
                dve.bn_aggr(bn2[:, :], bn6[:, :]).then_inc(ag, 1)

            def normalise(src, g, ag, rs, bn2, rstd, dst, free, free_at, ready):
                wait_for(dve, rs, g + 1)
                wait_for(dve, ag, g + 1)
                wait_for(dve, free, free_at)
                dve.tensor_scalar(dst, src, bn2[:, 0:1], rstd[:, :], ALU.subtract, ALU.mult).then_inc(ready, 1)

            def step(i, r, ahead, front, mid, back, last_one):
                f, c, b, a = i, i - 1, i - 2, i - 3
                even, odd = r % 2, (r + 1) % 2
                if isinstance(i, int) and i == -1:
                    dve.wait_ge(x_first, 16)
                if isinstance(i, int) and i == NR - 1:
                    dve.wait_ge(x_rest, 16 * (X_CHUNKS - 1))
                    dve.wait_ge(w_product_copied, 2)
                if back:
                    wait_for(dve, pv_done, b + 1)
                    wait_for(dve, p_ready, b + 1)
                    wait_for(dve, pv_turned, b - 1)
                    dve.scalar_tensor_tensor(out=pv[even][:, :], in0=last_rows[(r + 2) % NR][:, :],
                                             scalar=probs[even][:, 2 * P:KEYS], in1=psPV, op0=ALU.mult,
                                             op1=ALU.add).then_inc(pv_ready, 1)
                if last_one:
                    wait_for(dve, xn2_ready, a + 1)
                    dve.tensor_tensor_reduce(out=vprod[:, :], in0=xn2[odd][:, :], in1=wv_sum[:, :], scale=1.0,
                                             scalar=0.0, op0=ALU.mult, op1=ALU.add,
                                             accum_out=vs[odd][:, :]).then_inc(vs_done, 1)
                    wait_for(dve, vs_done, a + 1)
                    wait_for(dve, u_added, a)
                    dve.scalar_tensor_tensor(out=m.u_rows[:, :], in0=xn2[odd][:, :], scalar=vs[odd][:, :],
                                             in1=m.u_rows[:, :], op0=ALU.mult, op1=ALU.add).then_inc(u_added, 1)
                if mid:
                    wait_for(dve, s_done, c + 1)
                    dve.reduce_max(mx[odd][:, :], psS, AX.X).then_inc(mx_done, 1)
                    wait_for(dve, mx_done, c + 1)
                    wait_for(dve, p_ready, c - 1)
                    dve.tensor_scalar(nmx[odd][:, :], mx[odd][:, :], -SCALE, None, ALU.mult).then_inc(nmx_ready, 1)
                if front:
                    context_copy(f, even, 0)
                    wait_for(dve, last_turned, f + 1)
                    wait_for(dve, s_done, f - 1)
                    dve.tensor_copy(ctxT[even][:, :, :, 2 * P:KEYS].rearrange("p b c o -> p c (b o)"), psL) \
                        .then_inc(lastT_ready, 1)
                if back:
                    wait_for(dve, y_done, b + 1)
                    wait_for(dve, rinv_done, b + 1)
                    xs = x_all[:, ds(b * D, D)]
                    dve.scalar_tensor_tensor(out=xs, in0=psY, scalar=rinv[even][:, :], in1=xs, op0=ALU.mult,
                                             op1=ALU.add).then_inc(x2_ready, 1)
                    wait_alone(dve, x2_ready, b + 1, seen)
                    moments(x_all[:, ds(b * D, D)], b, st_b, ag_b, rs_b, bn6b[even], bn2b[even])
                if mid:
                    wait_for(dve, p_ready, c + 1)
                    dve.reciprocal(rinv[odd][:, :], rowsum[odd][:, :]).then_inc(rinv_done, 1)
                    wait_for(dve, p_turned, c + 1)
                    wait_for(dve, pv_done, c - 1)
                    dve.tensor_copy(pT[odd][:, :, :], psP[:, 0:2 * P].rearrange("p (c n) -> p c n", c=2)) \
                        .then_inc(pT_ready, 1)
                if ahead:
                    moments(x_all[:, ds((i + 1) * D, D)], i + 1, st_a, ag_a, xn_ready, bn6a[odd], bn2a[odd])
                if back:
                    normalise(x_all[:, ds(b * D, D)], b, ag_b, rs_b, bn2b[even], rstd_b[even],
                              xn2[even][:, :], xn2_turned, b - 1, xn2_ready)

            iterations(dve, step)


def two_deep(eng, steps, tail, step):
    for i in range(4):
        step(i, i % 2)
    pairs = steps // 2
    with eng.Fori(2, pairs) as k:
        for r in range(2):
            step(k * 2 + r, r)
    for i in range(2 * pairs, steps + tail):
        step(i, i % 2)


def retention(nc, new, m, psum):
    sb, sem = new.sb, new.sem
    C = 4
    NCH = NG // C
    W = C * D
    ident, x_all, ret_q, xnT = m.ident, m.x_all, m.ret_q, m.xnT
    u = sb("u", [T, D])
    uT = sb("uT", [P, DC, T])
    state = [sb(f"state{i}", [P, DC, T]) for i in range(2)]
    spread = sb("spread", [P, GB, GB, T])
    s_rows = sb("s_rows", [P, D])
    bn6 = [sb(f"bn6_{i}", [P, C, 6]) for i in range(2)]
    bn2 = [sb(f"bn2_{i}", [P, C, 2]) for i in range(2)]
    veps = sb("veps", [P, C])
    rstd = [sb(f"rstd_{i}", [P, C]) for i in range(2)]
    nmr = [sb(f"nmr_{i}", [P, C]) for i in range(2)]
    half4 = sb("half4", [P, C])
    x3 = [sb(f"x3_{i}", [P, W]) for i in range(2)]
    xn3 = [sb(f"xn3_{i}", [P, C, D]) for i in range(2)]
    SPANS = [1, 2, 4, 8, 16]
    STEPS = len(SPANS) + 2
    final = state[len(SPANS) % 2]
    ps_xnT = [psum[b] for b in (0, 1, 5, 6)]
    ps_x3T = [psum[b] for b in (4, 7)]
    psT = psum[0:2]
    psU = psum[4][0:T, 0:D]
    psM, psRows = psum[2], psum[3]

    names = ("u_summed", "u_copied", "u_turned", "uT_copied", "m_done", "scan", "consts_made", "rows_done",
             "rows_copied", "q_scaled", "x3_done", "st_done", "ag_done", "veps_done", "rstd_done", "nmr_done",
             "xn_done", "x3_turned", "acc_done", "xn_turned", "xn_copied")
    s = {n: sem("r_" + n) for n in names}
    in_groups = lambda t: t[:, :, 0:COLS].rearrange("p c (g n) -> p c g n", n=GCOLS)
    xnT_g, accT_g = in_groups(xnT), in_groups(m.acc)

    with nc.Block() as block:

        @block.gpsimd
        def _(pool):
            for b in range(GB):
                last = pool.tensor_copy(spread[:, :, b, :], ident[:, :].rearrange("p (q i) -> p q i", q=GB))
            last.then_inc(s["consts_made"], 1)
            pool.memset(half4[:, :], -0.5).then_inc(s["consts_made"], 1)
            pool.memset(xnT[:, :, COLS:], 0.0)
            pool.memset(m.acc[:, :, COLS:], 0.0)
            pool.wait_ge(s["consts_made"], 2)
            pool.wait_ge(s["rows_copied"], 1)

            def step(i, r):
                if is_in(i, 0, NCH - 1):
                    qs = ret_q[:, ds(i * W, W)].rearrange("p (g d) -> p g d", d=D)
                    pool.tensor_tensor(qs, qs, s_rows[:, :].unsqueeze(1).to_broadcast([P, C, D]), ALU.mult) \
                        .then_inc(s["q_scaled"], 1)
                if is_in(i, 1, NCH):
                    j, rj = i - 1, 1 - r
                    wait_for(pool, s["nmr_done"], i - 2)
                    wait_for(pool, s["xn_done"], C * (i - 2))
                    wait_for(pool, s["rstd_done"], i - 1)
                    wait_alone(pool, s["ag_done"], i, m.pool_seen)
                    pool.tensor_scalar(veps[:, :], bn2[rj][:, :, 1], EPS, None, ALU.add).then_inc(s["veps_done"], 1)
                    wait_for(pool, s["veps_done"], i)
                    pool.tensor_tensor(rstd[rj][:, :], veps[:, :], half4[:, :], ALU.pow).then_inc(s["rstd_done"], 1)

            two_deep(pool, NCH, 1, step)

        @block.vector
        def _(dve):
            dve.wait_ge(s["u_summed"], 1)
            dve.tensor_copy(u[:, :], psU).then_inc(s["u_copied"], 1)
            dve.wait_ge(s["m_done"], 1)
            mT = psM[:, 0:DC * T].rearrange("p (c t) -> p c t", c=DC)
            dve.tensor_copy(state[0][:, :, :], mT).then_inc(s["scan"], 1)
            for n, span in enumerate(SPANS):
                a, b = state[n % 2], state[(n + 1) % 2]
                dve.wait_ge(s["scan"], n + 1)
                dve.tensor_copy(b[:, :, 0:1 + span], a[:, :, 0:1 + span])
                dve.scalar_tensor_tensor(out=b[:, :, 1 + span:], in0=a[:, :, 1:T - span], scalar=GAMMA ** span,
                                         in1=a[:, :, 1 + span:], op0=ALU.mult, op1=ALU.add).then_inc(s["scan"], 1)
            dve.wait_ge(s["scan"], STEPS - 1)
            dve.tensor_copy(final[:, :, 0:1], final[:, :, 1:2]).then_inc(s["scan"], 1)
            dve.wait_ge(s["rows_done"], 1)
            dve.tensor_copy(s_rows[:, :].rearrange("p (t c q) -> p q c t", c=DC, q=GB),
                            psRows[:, 0:D].rearrange("p (q c t) -> p q c t", q=GB, c=DC)).then_inc(s["rows_copied"], 1)

            def step(i, r):
                if is_in(i, 0, NCH - 1):
                    wait_for(dve, s["q_scaled"], i + 1)
                    wait_for(dve, s["x3_turned"], 2 * (i - 1))
                    wait_for(dve, s["xn_done"], C * (i - 1))
                    dve.tensor_tensor(x3[r][:, :], x_all[:, ds(i * W, W)], ret_q[:, ds(i * W, W)], ALU.add).then_inc(s["x3_done"], 1)
                    wait_for(dve, s["nmr_done"], i - 1)
                    wait_for(dve, s["rstd_done"], i - 1)
                    wait_alone(dve, s["x3_done"], i + 1, m.seen)
                    for g in range(C):
                        last = dve.bn_stats(bn6[r][:, g, :], x3[r][:, g * D:(g + 1) * D])
                    last.then_inc(s["st_done"], 1)
                    wait_alone(dve, s["st_done"], i + 1, m.seen)
                    for g in range(C):
                        last = dve.bn_aggr(bn2[r][:, g, :], bn6[r][:, g, :])
                    last.then_inc(s["ag_done"], 1)
                if is_in(i, 2, NCH + 1):
                    for h in range(2):
                        g0 = (i - 2) * C + 2 * h
                        wait_for(dve, s["x3_turned"], 2 * (i - 2) + h + 1)
                        wait_for(dve, s["xn_copied"], g0 + 2)
                        dve.tensor_tensor(accT_g[:, :, ds(g0, 2), 0:P],
                                          ps_x3T[h][:, :].rearrange("p (c g n) -> p c g n", c=DC, g=2),
                                          xnT_g[:, :, ds(g0, 2), 0:P], ALU.add).then_inc(s["acc_done"], 1)
                if is_in(i, 0, NCH - 1):
                    wait_for(dve, s["xn_done"], C * (i - 1))
                    wait_for(dve, s["ag_done"], i + 1)
                    wait_for(dve, s["rstd_done"], i + 1)
                    dve.scalar_tensor_tensor(out=nmr[r][:, :], in0=bn2[r][:, :, 0], scalar=-1.0, in1=rstd[r][:, :],
                                             op0=ALU.mult, op1=ALU.mult).then_inc(s["nmr_done"], 1)

            two_deep(dve, NCH, 2, step)

        @block.tensor
        def _(pe):
            pe.matmul(psU, m.time_mask[:, :], m.u_rows[:, :], start=True, stop=True).then_inc(s["u_summed"], 1)
            pe.wait_ge(s["u_copied"], 1)
            for dc in range(DC):
                last = turn(pe, psT[0][:, dc * T:(dc + 1) * T], u[:, dc * P:(dc + 1) * P], ident[0:T, 0:T])
            last.then_inc(s["u_turned"], 1)
            pe.wait_ge(s["uT_copied"], 1)
            for ec in range(DC):
                for dc in range(DC):
                    last = pe.matmul(psM[:, ec * T:(ec + 1) * T], m.a_wk[:, dc, ec * P:(ec + 1) * P], uT[:, dc, :],
                                     start=(dc == 0), stop=(dc == DC - 1))
            last.then_inc(s["m_done"], 1)
            pe.wait_ge(s["consts_made"], 1)
            pe.wait_ge(s["scan"], STEPS)
            for q in range(GB):
                last = pe.matmul(psRows[:, q * DC * T:(q + 1) * DC * T], spread[:, q, :, :].rearrange("p b i -> p (b i)"),
                                 final[:, :, :].rearrange("p c t -> p (c t)"), start=True, stop=True)
            last.then_inc(s["rows_done"], 1)

            def step(i, r):
                if is_in(i, 1, NCH):
                    j = 1 - r
                    for g in range(C):
                        wait_for(pe, s["xn_done"], C * (i - 1) + g + 1)
                        wait_for(pe, s["xn_copied"], C * (i - 2) + g + 1)
                        for dc in range(DC):
                            last = pe.matmul(ps_xnT[g][:, dc * GCOLS:(dc + 1) * GCOLS], xn3[j][:, g, dc * P:(dc + 1) * P],
                                             m.ident_mask[:, :], start=True, stop=True)
                        last.then_inc(s["xn_turned"], 1)
                    for h in range(2):
                        wait_for(pe, s["acc_done"], 2 * (i - 2) + h + 1)
                        wait_for(pe, s["x3_done"], i)
                        for dc in range(DC):
                            for g in range(2):
                                o, c = (dc * 2 + g) * P, (2 * h + g) * D + dc * P
                                last = turn(pe, ps_x3T[h][:, o:o + P], x3[j][:, c:c + P], ident[:, :])
                        last.then_inc(s["x3_turned"], 1)

            two_deep(pe, NCH, 1, step)

        @block.scalar
        def _(act):
            act.wait_ge(s["u_turned"], 1)
            act.activation(uT[:, :, :], psT[0][:, 0:DC * T].rearrange("p (c t) -> p c t", c=DC), ACT.Copy) \
                .then_inc(s["uT_copied"], 1)

            def step(i, r):
                if is_in(i, 1, NCH):
                    j = 1 - r
                    wait_for(act, s["nmr_done"], i)
                    wait_for(act, s["xn_turned"], C * (i - 2))
                    for g in range(C):
                        act.activation(xn3[j][:, g, :], x3[j][:, g * D:(g + 1) * D], ACT.Identity,
                                       bias=nmr[j][:, g:g + 1], scale=rstd[j][:, g:g + 1]).then_inc(s["xn_done"], 1)
                    for g in range(C):
                        wait_for(act, s["xn_turned"], C * (i - 1) + g + 1)
                        act.activation(xnT_g[:, :, ds((i - 1) * C + g, 1), :].rearrange("p c g n -> p c (g n)"),
                                       ps_xnT[g][:, 0:DC * GCOLS].rearrange("p (c n) -> p c n", c=DC), ACT.Copy) \
                            .then_inc(s["xn_copied"], 1)

            two_deep(act, NCH, 1, step)


def is_in(i, first, last):
    return not isinstance(i, int) or first <= i <= last


def tables(nc, new, m, w1, b1, w2, b2):
    m.w1_sb, m.w2_sb = new.sb("w1_sb", [P, DC, HID]), new.sb("w2_sb", [HID, E])
    m.b1_sb, m.b2_sb = new.sb("b1_sb", [HID, 1]), new.sb("b2_sb", [1, E])
    m.before = new.sb("before", [P, P])
    m.lower = new.sb("lower", [P, E, E])
    m.slot_no = new.sb("slot_no", [P, NSLOT])
    m.pad_plan = new.sb("pad_plan", [2, NSLOT])
    m.job = new.sb("job", [P, TOP, 2])
    m.rank_no = new.sb("rank_no", [P, TOP, E])
    m.batches_past = new.sb("batches_past", [P, NG])
    m.row_no = new.sb("row_no", [P, 1])
    m.expert_no = new.sb("expert_no", [P, E])
    m.steps = [new.sb(f"steps{n}", [P, NSTEP]) for n in range(2)]
    m.router_loaded = new.sem("router_loaded")

    def load(sp):
        sp.dma_start(m.w1_sb[:, :, :], w1.rearrange("(c p) n -> p c n", p=P)).then_inc(m.router_loaded, 16)
        sp.dma_start(m.w2_sb[:, :], w2).then_inc(m.router_loaded, 16)
        sp.dma_start(m.b1_sb[:, :], b1.rearrange("(n a) -> n a", a=1)).then_inc(m.router_loaded, 16)
        sp.dma_start(m.b2_sb[:, :], b2.rearrange("(a n) -> a n", a=1)).then_inc(m.router_loaded, 16)

    def build(pool):
        n, step = m.const_steps, m.const_step

        def done(ins):
            n[0] += 1
            ins.then_inc(step, 1)
            pool.wait_ge(step, n[0])

        done(pool.memset(m.before[:, :], 1.0))
        pool.affine_select(out=m.before[:, :], in_=m.before[:, :], compare_op=ALU.is_ge, fill=0.0, base=-1,
                           pattern=[[1, P]], channel_multiplier=-1)
        done(pool.memset(m.lower[:, :, :], 1.0))
        pool.affine_select(out=m.lower[:, :, :], in_=m.lower[:, :, :], compare_op=ALU.is_ge, fill=0.0, base=-1,
                           pattern=[[1, E], [-1, E]], channel_multiplier=0)
        whole = dict(allow_small_or_imprecise_dtypes=True)
        pool.iota(m.slot_no[:, :], pattern=[[1, NSLOT]], base=0, channel_multiplier=0, **whole)
        done(pool.iota(m.pad_plan[:, :].rearrange("p (i s) -> p i s", s=UNIT), pattern=[[0, UNITS], [T, UNIT]],
                       base=COLS + 1, channel_multiplier=0, **whole))
        pool.affine_select(out=m.pad_plan[:, :], in_=m.pad_plan[:, :], compare_op=ALU.is_ge, fill=1.0, base=0,
                           pattern=[[0, NSLOT]], channel_multiplier=-1)
        pool.iota(m.batches_past[:, :], pattern=[[-GB, NG]], base=0, channel_multiplier=1, **whole)
        pool.iota(m.row_no[:, :], pattern=[[0, 1]], base=1 - GB, channel_multiplier=T, **whole)
        pool.iota(m.rank_no[:, :, :], pattern=[[1, TOP], [0, E]], base=0, channel_multiplier=0, **whole)
        pool.iota(m.expert_no[:, :], pattern=[[1, E]], base=1, channel_multiplier=0, **whole)
        pool.iota(m.steps[0][:, :], pattern=[[SLOTS, NSTEP]], base=SLOTS, channel_multiplier=0, **whole)
        pool.iota(m.steps[1][:, :], pattern=[[SLOTS, NSTEP]], base=UNIT, channel_multiplier=0, **whole)

    m.load_router, m.build_tables = load, build



def router(nc, new, m, psum):
    sb, sem = new.sb, new.sem
    w1_sb, w2_sb, b1_sb, b2_sb, before, lower, slot_no, pad_plan, job, expert_no, steps = (
        m.w1_sb, m.w2_sb, m.b1_sb, m.b2_sb, m.before, m.lower, m.slot_no, m.pad_plan, m.job, m.expert_no, m.steps)
    mean, hid = sb("mean", [P, DC, B]), sb("hid", [HID, B])
    group_of, column = sb("group_of", [P, NG]), sb("column", [P, 1])
    small = lambda name: sb(name, [P, E])
    mx, nmx, total, inv = (sb(n, [P, 1]) for n in ("r_mx", "r_nmx", "r_total", "r_inv"))
    ex, probs, rank, picked, share, weight = (small("r_" + n) for n in ("ex", "probs", "rank", "picked", "share", "weight"))
    count, pairs, halves, odd, pair0, odd0, place, alone, slot, behind = (
        small("r_" + n) for n in ("count", "pairs", "halves", "odd", "pair0", "odd0", "place", "alone", "slot", "behind"))
    n_pairs, first_odd = sb("n_pairs", [P, 1]), sb("first_odd", [P, 1])
    cnt_cmp = [sb(f"cnt_cmp{n}", [P, E, NSTEP]) for n in range(2)]
    cmp, cmp2 = sb("cmp", [P, E, E]), sb("cmp2", [P, E, E])
    slot_k, weight_k = sb("slot_k", [P, TOP]), sb("weight_k", [P, TOP])
    pick, pick_slot, pick_expert, pick_weight = (
        sb(n, [P, TOP, E]) for n in ("pick", "pick_slot", "pick_expert", "pick_weight"))
    hot = [sb(f"hot{k}", [P, NSLOT], F32R) for k in range(TOP)]
    wide = [[sb(f"wide{k}_{h}", [P, P], F32R) for h in range(2)] for k in range(TOP)]
    job_s = [sb(f"job_s{h}", [P, TOP, 2], F32R) for h in range(2)]
    row2 = sb("row2", [2, NSLOT])

    psH, psLg, psPos, psCnt, psW, psCol = psum[0][0:HID, 0:B], psum[1][:, 0:E], psum[2][:, 0:E], psum[3][:, 0:E], \
        psum[4][:, 0:NSLOT], psum[5][0:2, 0:NSLOT]
    job_ready, mean_copied, h_done, hid_ready, lg_done, nmx_ready, ex_ready, picked_ready, pos_done, \
        hot_ready, wide_ready, w_done, col_done, w_copied, v = (
            sem("o_" + n) for n in ("job_ready", "mean_copied", "h_done", "hid_ready", "lg_done", "nmx_ready", "ex_ready",
                                    "picked_ready", "pos_done", "hot_ready", "wide_ready", "w_done", "col_done",
                                    "w_copied", "steps"))

    with nc.Block() as block:

        @block.tensor
        def _(pe):
            pe.wait_ge(m.router_loaded, 64)
            pe.wait_ge(mean_copied, 1)
            for dc in range(DC):
                last = pe.matmul(psH, w1_sb[:, dc, :], mean[:, dc, :], start=(dc == 0), stop=(dc == DC - 1))
            last.then_inc(h_done, 1)
            pe.wait_ge(hid_ready, 1)
            pe.matmul(psLg, hid[:, :], w2_sb[:, :], start=True, stop=False)
            pe.matmul(psLg, m.ones[0:1, :], b2_sb[:, :], start=False, stop=True).then_inc(lg_done, 1)
            pe.wait_ge(picked_ready, 1)
            pe.matmul(psPos, before[:, :], picked[:, :], start=True, stop=True)
            pe.matmul(psCnt, m.ones[:, :], picked[:, :], start=True, stop=True).then_inc(pos_done, 1)
            pe.wait_ge(job_ready, 1)
            for k in range(TOP):
                pe.wait_ge(hot_ready, k + 1)
                for h in range(2):
                    last = pe.matmul(psCol, job_s[h][:, k, :], hot[k][:, :], start=(k + h == 0), stop=(k + h == TOP))
            last.then_inc(col_done, 1)
            for k in range(TOP):
                pe.wait_ge(wide_ready, k + 1)
                for h in range(2):
                    last = pe.matmul(psW, wide[k][h][:, :], hot[k][:, :], start=(k + h == 0), stop=(k + h == TOP))
            last.then_inc(w_done, 1)

        @block.scalar
        def _(act):
            sums = m.xnT[:, :, 0:COLS].rearrange("p c (g n) -> p c g n", n=GCOLS)[:, :, :, P:]
            act.activation(mean[:, :, :].rearrange("p c (g b) -> p c g b", b=GB), sums, ACT.Copy, scale=1.0 / T) \
                .then_inc(mean_copied, 1)
            act.wait_ge(m.router_loaded, 64)
            act.wait_ge(h_done, 1)
            act.activation(hid[:, :], psH, ACT.Tanh, bias=b1_sb[:, :]).then_inc(hid_ready, 1)
            act.wait_ge(nmx_ready, 1)
            act.activation(ex[:, :], psLg, ACT.Exp, bias=nmx[:, :], accum_out=total[:, :]).then_inc(ex_ready, 1)
            act.wait_ge(w_done, 1)
            act.activation(m.slot_w[:, :], psW, ACT.Copy).then_inc(w_copied, 1)

        @block.vector
        def _(dve):
            n = [0]

            def done(ins):
                n[0] += 1
                ins.then_inc(v, 1)
                dve.wait_ge(v, n[0])

            by_j = lambda t: t[:, :].unsqueeze(1).to_broadcast([P, E, E])
            by_e = lambda t: t[:, :].unsqueeze(2).to_broadcast([P, E, E])
            done(dve.tensor_scalar(group_of[:, :], m.batches_past[:, :], 0.0, float(GB), ALU.is_ge, ALU.mult))
            done(dve.reduce_sum(column[:, :], group_of[:, :], AX.X))
            dve.tensor_tensor(job[:, :, 0], m.row_no[:, :].to_broadcast([P, TOP]), column[:, :].to_broadcast([P, TOP]),
                              ALU.add)
            dve.wait_ge(lg_done, 1)
            done(dve.reduce_max(mx[:, :], psLg, AX.X))
            dve.tensor_scalar(nmx[:, :], mx[:, :], -1.0, None, ALU.mult).then_inc(nmx_ready, 1)
            dve.wait_ge(ex_ready, 1)
            done(dve.reciprocal(inv[:, :], total[:, :]))
            done(dve.tensor_scalar(probs[:, :], ex[:, :], inv[:, :], None, ALU.mult))
            dve.tensor_tensor(cmp[:, :, :], by_j(probs), by_e(probs), ALU.is_gt)
            done(dve.tensor_tensor(cmp2[:, :, :], by_j(probs), by_e(probs), ALU.is_equal))
            done(dve.tensor_tensor(cmp2[:, :, :], cmp2[:, :, :], lower[:, :, :], ALU.mult))
            done(dve.tensor_tensor(cmp[:, :, :], cmp[:, :, :], cmp2[:, :, :], ALU.add))
            done(dve.reduce_sum(rank[:, :], cmp[:, :, :], AX.X))
            dve.tensor_scalar(picked[:, :], rank[:, :], float(TOP), None, ALU.is_lt).then_inc(picked_ready, 1)
            dve.wait_ge(picked_ready, 1)
            done(dve.tensor_tensor(share[:, :], probs[:, :], picked[:, :], ALU.mult))
            done(dve.reduce_sum(total[:, :], share[:, :], AX.X))
            done(dve.reciprocal(inv[:, :], total[:, :]))
            done(dve.tensor_scalar(weight[:, :], share[:, :], inv[:, :], None, ALU.mult))
            by_rank = lambda t: t[:, :].unsqueeze(1).to_broadcast([P, TOP, E])
            done(dve.tensor_tensor(pick[:, :, :], by_rank(rank), m.rank_no[:, :, :], ALU.is_equal))
            done(dve.tensor_tensor(pick_expert[:, :, :], pick[:, :, :], by_rank(expert_no), ALU.mult))
            done(dve.reduce_sum(job[:, :, 1], pick_expert[:, :, :], AX.X))
            done(dve.tensor_copy(job_s[0][:, :, :], job[:, :, :]))
            dve.tensor_tensor(job_s[1][:, :, :], job[:, :, :], job_s[0][:, :, :].bitcast(F32), ALU.subtract) \
                .then_inc(job_ready, 1)
            dve.wait_ge(pos_done, 1)
            done(dve.tensor_copy(count[:, :], psCnt))
            by_k = lambda t, n: t[:, :].unsqueeze(2).to_broadcast([P, E, n])
            over_e = lambda t, n: t[:, :].unsqueeze(1).to_broadcast([P, E, n])
            dve.tensor_tensor(cnt_cmp[0][:, :, :], by_k(count, NSTEP), over_e(steps[1], NSTEP), ALU.is_gt)
            done(dve.tensor_scalar(halves[:, :], count[:, :], 0.0, None, ALU.is_gt))
            done(dve.reduce_sum(pairs[:, :], cnt_cmp[0][:, :, :], AX.X))
            done(dve.tensor_tensor(cnt_cmp[1][:, :, :], by_k(count, NSTEP), over_e(steps[0], NSTEP), ALU.is_gt))
            done(dve.reduce_sum(odd[:, :], cnt_cmp[1][:, :, :], AX.X))
            done(dve.tensor_tensor(odd[:, :], odd[:, :], halves[:, :], ALU.add))
            done(dve.tensor_tensor(odd[:, :], odd[:, :], pairs[:, :], ALU.subtract))
            dve.tensor_tensor(cmp[:, :, :], by_j(pairs), lower[:, :, :], ALU.mult)
            dve.tensor_tensor(cmp2[:, :, :], by_j(odd), lower[:, :, :], ALU.mult)
            done(dve.reduce_sum(n_pairs[:, :], pairs[:, :], AX.X))
            dve.reduce_sum(pair0[:, :], cmp[:, :, :], AX.X)
            dve.tensor_scalar(first_odd[:, :], n_pairs[:, :], float(BIG), float(SLOTS), ALU.max, ALU.mult)
            done(dve.reduce_sum(odd0[:, :], cmp2[:, :, :], AX.X))
            dve.tensor_copy(place[:, :], psPos)
            done(dve.tensor_scalar(behind[:, :], pairs[:, :], float(SLOTS), None, ALU.mult))
            dve.scalar_tensor_tensor(out=slot[:, :], in0=pair0[:, :], scalar=float(SLOTS), in1=place[:, :],
                                     op0=ALU.mult, op1=ALU.add)
            done(dve.tensor_tensor(place[:, :], place[:, :], behind[:, :], ALU.subtract))
            done(dve.scalar_tensor_tensor(out=alone[:, :], in0=odd0[:, :], scalar=float(UNIT), in1=place[:, :],
                                          op0=ALU.mult, op1=ALU.add))
            done(dve.tensor_scalar(alone[:, :], alone[:, :], first_odd[:, :], None, ALU.add))
            done(dve.tensor_tensor(alone[:, :], alone[:, :], slot[:, :], ALU.subtract))
            done(dve.scalar_tensor_tensor(out=alone[:, :], in0=place[:, :], scalar=0.0, in1=alone[:, :],
                                          op0=ALU.is_ge, op1=ALU.mult))
            done(dve.tensor_tensor(slot[:, :], slot[:, :], alone[:, :], ALU.add))
            done(dve.tensor_tensor(pick_slot[:, :, :], pick[:, :, :], by_rank(slot), ALU.mult))
            done(dve.reduce_sum(slot_k[:, :], pick_slot[:, :, :], AX.X))
            for k in range(TOP):
                dve.tensor_scalar(hot[k][:, :], slot_no[:, :], slot_k[:, k:k + 1], None, ALU.is_equal) \
                    .then_inc(hot_ready, 1)
            done(dve.tensor_tensor(pick_weight[:, :, :], pick[:, :, :], by_rank(weight), ALU.mult))
            done(dve.reduce_sum(weight_k[:, :], pick_weight[:, :, :], AX.X))
            for k in range(TOP):
                done(dve.tensor_scalar(wide[k][0][:, :], m.ones[:, :], weight_k[:, k:k + 1], None, ALU.mult))
                dve.scalar_tensor_tensor(out=wide[k][1][:, :], in0=m.ones[:, :], scalar=weight_k[:, k:k + 1],
                                         in1=wide[k][0][:, :].bitcast(F32), op0=ALU.mult, op1=ALU.subtract) \
                    .then_inc(wide_ready, 1)
            dve.wait_ge(col_done, 1)
            done(dve.scalar_tensor_tensor(out=row2[:, :], in0=psCol, scalar=0.0, in1=m.pad_plan[:, :],
                                          op0=ALU.is_equal, op1=ALU.mult))
            done(dve.scalar_tensor_tensor(out=m.plan[:, :], in0=psCol, scalar=-1.0, in1=row2[:, :],
                                          op0=ALU.add, op1=ALU.add))


def experts(nc, new, m, psum, wa, wb):
    sb, sem = new.sb, new.sem
    N = SLOTS * T
    raw_a, raw_b = sb("raw_a", [P, DC, FF]), sb("raw_b", [P, FC, D])
    pair = lambda name, shape, n: [[sb(f"{name}{h}{i}", shape, F32R) for h in ("hi", "lo")] for i in range(n)]
    wa_s, wb_s = pair("wa_", [P, DC, FF], 2), pair("wb_", [P, FC, D], 2)
    cols = sb("cols", [P, DC, N])
    x_s = pair("x_", [P, DC, N], 2)
    act_out = [sb(f"act_out{i}", [P, N]) for i in range(2)]
    h_s = pair("h_", [P, N], 4)
    psH = psum[0:4]
    psZ = [psum[4:6], psum[6:8]]
    TERMS = ((0, 0), (0, 1), (1, 0))
    X_PART, X_LO_FC = {SLOTS: 0, UNIT: 2}, 4
    COMBINE = 5

    w_in, w_lo = ([sem(f"e_{n}{quarter}") for quarter in range(4)] for n in ("w_in", "w_lo"))
    w_hi, cols_ready, cols_rest, x_hi, x_lo, added = (
        sem("e_" + n) for n in ("w_hi", "cols_ready", "cols_rest", "x_hi", "x_lo", "added"))
    up_done, gelu_done, h_lo, down_done = (
        [sem(f"e_{n}{c}") for c in range(FC)] for n in ("up_done", "gelu_done", "h_lo", "down_done"))
    h_hi = [sem(f"e_h_hi{c}") for c in range(2)]

    def run(eng, step):
        size = lambda i: SLOTS if i < BIG else UNIT
        one = lambda i: step(i, i % 2, (size(i - 1), size(i), size(i + 1)))
        for i in range(-1, 2):
            one(i)
        with eng.Fori(1, (BIG - 1) // 2) as k:
            for r in range(2):
                step(k * 2 + r, r, (SLOTS,) * 3)
        for i in range(BIG - 1, BIG + 2):
            one(i)
        with eng.Fori((BIG + 2) // 2, (TILES - 1) // 2) as k:
            for r in range(2):
                step(k * 2 + 1 + r, 1 - r, (UNIT,) * 3)
        for i in range(BIG + 2 + 2 * ((TILES - 1) // 2 - (BIG + 2) // 2), TILES + 1):
            one(i)

    def part_of(k, a, b):
        t = (a, b)[k // 2]
        half = t.shape[1] // 2
        return t[:, k % 2 * half:(k % 2 + 1) * half, :]

    def low_part(eng, q, t, k):
        wait_for(eng, w_hi, 4 * t + k + 1)
        eng.tensor_tensor(part_of(k, wa_s[q][1], wb_s[q][1]), part_of(k, raw_a, raw_b),
                          part_of(k, wa_s[q][0], wb_s[q][0]).bitcast(F32), ALU.subtract).then_inc(w_lo[k], 1)

    def slot_of(i, n):
        return i * SLOTS if n == SLOTS else i * UNIT + BIG * (SLOTS - UNIT)

    def registers(eng_type, tile, count, n, first=0):
        _, v = nc.values_load_multi_w_load_instructions(
            m.plan[0:1, ds(slot_of(tile, n) + first, count)], engines=[eng_type], min_val=0, max_val=COLS + PAD - T)
        return v

    with nc.Block() as block:

        @block.sync
        def _(sp):
            def load(i, n):
                e = sp.value_load(m.plan[1:2, ds(slot_of(i, n), 1)], min_val=0, max_val=E - 1)
                for k in range(4):
                    w, chunks = ((wa, DC), (wb, FC))[k // 2]
                    rows = slice(k % 2 * chunks // 2 * P, (k % 2 + 1) * chunks // 2 * P)
                    wait_for(sp, w_lo[k], i)
                    sp.dma_start(part_of(k, raw_a, raw_b), w[ds(e, 1), rows, :].rearrange("e (c p) f -> p (e c) f", p=P)) \
                        .then_inc(w_in[k], 16)

            load(0, SLOTS)
            with sp.Fori(1, BIG) as i:
                load(i, SLOTS)
            with sp.Fori(BIG, TILES) as i:
                load(i, UNIT)

        @block.gpsimd
        def _(pool):
            def step(i, r, sizes):
                if is_in(i, -1, TILES - 2):
                    t, q, n = i + 1, 1 - r, sizes[2]
                    mine = n if is_in(i, 0, TILES) else n // 2
                    v = registers(mybir.EngineType.Pool, t, mine, n)
                    wait_for(pool, x_hi, t)
                    wait_for(pool, x_lo, t)
                    for j in range(mine):
                        last = pool.tensor_copy(cols[:, :, j * T:(j + 1) * T], m.xnT[:, :, ds(v[j], T)])
                    last.then_inc(cols_ready, 1)
                    wait_for(pool, down_done[FC - 1], t - 1)
                    for k in range(0 if is_in(i, 0, TILES) else 2, 4 if n == SLOTS else 3):
                        low_part(pool, q, t, k)

            run(pool, step)

        @block.scalar
        def _(act):
            def ready(t, q, part, n, x_part):
                if part == x_part:
                    wait_for(act, cols_ready, t + 1)
                    if isinstance(t, int) and t == 0:
                        act.wait_ge(cols_rest, 1)
                    act.activation(x_s[q][0][:, :, 0:n * T], cols[:, :, 0:n * T], ACT.Copy).then_inc(x_hi, 1)
                    return
                k = part - (part > x_part)
                wait_for(act, w_in[k], 16 * t + 16)
                if k == 0:
                    wait_for(act, down_done[FC - 1], t - 1)
                act.activation(part_of(k, wa_s[q][0], wb_s[q][0]), part_of(k, raw_a, raw_b), ACT.Copy).then_inc(w_hi, 1)

            def step(i, r, sizes):
                for fc in range(FC):
                    if is_in(i, 0, TILES - 1):
                        w = sizes[1] * T
                        wait_for(act, up_done[fc], i + 1)
                        wait_for(act, h_lo[(fc - 2) % FC], i + 1 if fc >= 2 else i)
                        act.activation(act_out[fc % 2][:, 0:w], psH[fc % 4][:, 0:w], ACT.Gelu_apprx_tanh) \
                            .then_inc(gelu_done[fc], 1)
                    if is_in(i, -1, TILES - 2) and 2 <= fc < 7:
                        ready(i + 1, 1 - r, fc - 2, sizes[2], X_PART[sizes[2]] if is_in(i, 0, TILES) else 2)

            run(act, step)

        @block.vector
        def _(dve):
            def combine(i, n, r, v, js):
                for j in js:
                    for dc in range(DC):
                        last = dve.scalar_tensor_tensor(
                            out=m.acc[:, dc, ds(v[j], T)], in0=psZ[r][dc][:, j * T:(j + 1) * T],
                            scalar=m.slot_w[:, ds(slot_of(i, n) + j, 1)], in1=m.acc[:, dc, ds(v[j], T)],
                            op0=ALU.mult, op1=ALU.add)
                return last

            def step(i, r, sizes):
                v = registers(mybir.EngineType.DVE, i - 1, sizes[0], sizes[0]) if is_in(i, 1, TILES) else None
                if not is_in(i, 0, TILES):
                    half = SLOTS // 2
                    late = registers(mybir.EngineType.DVE, 0, half, SLOTS, half)
                    for j in range(half):
                        last = dve.tensor_copy(cols[:, :, (half + j) * T:(half + j + 1) * T], m.xnT[:, :, ds(late[j], T)])
                    last.then_inc(cols_rest, 1)
                for fc in range(FC):
                    if is_in(i, 0, TILES - 1):
                        w = sizes[1] * T
                        g = act_out[fc % 2][:, 0:w]
                        hi, lo = (h[:, 0:w] for h in h_s[fc % 4])
                        wait_for(dve, gelu_done[fc], i + 1)
                        wait_for(dve, down_done[(fc - 4) % FC], i + 1 if fc >= 4 else i)
                        dve.tensor_copy(hi, g).then_inc(h_hi[fc % 2], 1)
                        wait_for(dve, h_hi[fc % 2], i * (FC // 2) + fc // 2 + 1)
                        dve.tensor_tensor(lo, g, hi.bitcast(F32), ALU.subtract).then_inc(h_lo[fc], 1)
                    if is_in(i, 1, TILES) and fc == 2:
                        wait_for(dve, down_done[FC - 1], i)
                        wait_for(dve, added, i - 1)
                    if is_in(i, 1, TILES) and 2 <= fc < 2 + COMBINE:
                        last = combine(i - 1, sizes[0], 1 - r, v, range(*((fc - 2 + k) * sizes[0] // COMBINE for k in range(2))))
                        if fc == 1 + COMBINE:
                            last.then_inc(added, 1)
                    if is_in(i, -1, -1) and not is_in(i, 0, TILES) and fc == 3:
                        for k in range(2):
                            low_part(dve, 0, 0, k)
                    if is_in(i, -1, TILES - 2) and fc == X_LO_FC:
                        q, w = 1 - r, sizes[2] * T
                        wait_for(dve, x_hi, i + 2)
                        dve.tensor_tensor(x_s[q][1][:, :, 0:w], cols[:, :, 0:w], x_s[q][0][:, :, 0:w].bitcast(F32),
                                          ALU.subtract).then_inc(x_lo, 1)
                    if is_in(i, -1, TILES - 2) and fc == 7 and sizes[2] == UNIT:
                        low_part(dve, 1 - r, i + 1, 3)

            run(dve, step)

        @block.tensor
        def _(pe):
            def up(i, r, fc, w):
                if fc == 0:
                    wait_for(pe, x_hi, i + 1)
                    wait_for(pe, x_lo, i + 1)
                    for k in range(2):
                        wait_for(pe, w_lo[k], i + 1)
                wait_for(pe, gelu_done[(fc - 4) % FC], i + 1 if fc >= 4 else i)
                n = 0
                for dc in range(DC):
                    for a, b in TERMS:
                        last = pe.matmul(psH[fc % 4][:, 0:w], wa_s[r][a][:, dc, fc * P:(fc + 1) * P], x_s[r][b][:, dc, 0:w],
                                         start=(n == 0), stop=(n == 2 * len(TERMS) - 1))
                        n += 1
                last.then_inc(up_done[fc], 1)

            def down(i, r, fc, w):
                wait_for(pe, h_lo[fc], i + 1)
                if fc % (FC // 2) == 0:
                    wait_for(pe, w_lo[2 + fc // (FC // 2)], i + 1)
                if fc == 0:
                    wait_for(pe, added, i - 1)
                for dc in range(DC):
                    for n, (a, b) in enumerate(TERMS):
                        last = pe.matmul(psZ[r][dc][:, 0:w], wb_s[r][a][:, fc, dc * P:(dc + 1) * P], h_s[fc % 4][b][:, 0:w],
                                         start=(fc == 0 and n == 0), stop=(fc == FC - 1 and n == len(TERMS) - 1))
                last.then_inc(down_done[fc], 1)

            def step(i, r, sizes):
                for fc in range(FC):
                    if is_in(i, 0, TILES - 1):
                        up(i, r, fc, sizes[1] * T)
                        if fc >= 2:
                            down(i, r, fc - 2, sizes[1] * T)
                    if is_in(i, 1, TILES) and fc < 2:
                        down(i - 1, 1 - r, FC - 2 + fc, sizes[0] * T)

            run(pe, step)


def finish(nc, new, m, psum, out):
    sb, sem = new.sb, new.sem
    G, BUF = 4, 4
    STEPS = NG // G
    res = [sb(f"res{i}", [P, G * D]) for i in range(BUF)]
    stored = [sem(f"f_stored{i}") for i in range(BUF)]
    turned, copied = ([sem(f"f_{n}{h}") for h in range(2)] for n in ("turned", "copied"))
    out_v = out.rearrange("(g p) d -> p g d", p=P)

    def rounds(eng, step):
        for r in range(BUF):
            step(r, r)
        with eng.Fori(1, STEPS // BUF) as k:
            for r in range(BUF):
                step(k * BUF + r, r)

    with nc.Block() as block:

        @block.tensor
        def _(pe):
            for i in range(STEPS):
                for h in range(2):
                    if i >= BUF:
                        pe.wait_ge(copied[h], i - (BUF - 1))
                    for g in range(2):
                        for dc in range(DC):
                            o, c = g * D + dc * P, (i * G + 2 * h + g) * GCOLS
                            last = turn(pe, psum[2 * (i % BUF) + h][:, o:o + P], m.acc[:, dc, c:c + P], m.ident[:, :])
                    last.then_inc(turned[h], 1)

        @block.vector
        def _(dve):
            def step(i, r):
                wait_for(dve, turned[0], i + 1)
                wait_for(dve, stored[r], (i - r) * (16 // BUF))
                dve.tensor_copy(res[r][:, 0:2 * D], psum[2 * r][:, :]).then_inc(copied[0], 1)

            rounds(dve, step)

        @block.scalar
        def _(act):
            def step(i, r):
                wait_for(act, turned[1], i + 1)
                wait_for(act, stored[r], (i - r) * (16 // BUF))
                act.activation(res[r][:, 2 * D:], psum[2 * r + 1][:, :], ACT.Copy).then_inc(copied[1], 1)

            rounds(act, step)

        @block.sync
        def _(sp):
            def step(i, r):
                for h in range(2):
                    wait_for(sp, copied[h], i + 1)
                sp.dma_start(out_v[:, ds(i * G, G), :], res[r][:, :].rearrange("p (g d) -> p g d", d=D)) \
                    .then_inc(stored[r], 16)

            rounds(sp, step)
            for r in range(BUF):
                sp.wait_ge(stored[r], 16 * (STEPS // BUF))



class Room:

    def __init__(self, nc, stack, sems):
        self.nc, self.stack, self.sems = nc, stack, sems

    def sb(self, name, shape, dt=F32):
        return self.stack.enter_context(self.nc.sbuf_tensor(name, shape, dt))

    def sem(self, name):
        return self.sems.enter_context(self.nc.semaphore(name))


class Shared:
    pass


def program(nc, x, context, x_wq, x_wkv, a_wq, a_wk, a_wv, w1, b1, w2, b2, wa, wb, out):
    m = Shared()
    with ExitStack() as whole:
        new = Room(nc, whole, whole)
        psum = [whole.enter_context(nc.psum_tensor(f"bank{i}", [P, 512], F32)) for i in range(8)]
        constants(nc, new, m)
        tables(nc, new, m, w1, b1, w2, b2)
        m.plan = new.sb("plan", [2, NSLOT], I32)
        m.slot_w = new.sb("slot_w", [P, NSLOT])
        m.xnT = new.sb("xnT", [P, DC, COLS + PAD])
        m.acc = new.sb("acc", [P, DC, COLS + PAD])
        with ExitStack() as rows:
            held = Room(nc, rows, whole)
            m.x_all, m.ret_q = held.sb("x_all", [P, NG * D]), held.sb("ret_q", [P, NG * D])
            m.a_wk, m.u_rows = held.sb("a_wk", [P, DC, D]), held.sb("u_rows", [P, D])
            with ExitStack() as own:
                attention(nc, Room(nc, own, whole), m, psum, x.rearrange("b t d -> (b t) d"), context,
                          dict(x_wq=x_wq, x_wkv=x_wkv, a_wq=a_wq, a_wk=a_wk, a_wv=a_wv))
            with ExitStack() as own:
                retention(nc, Room(nc, own, whole), m, psum)
        with ExitStack() as own:
            router(nc, Room(nc, own, whole), m, psum)
        with ExitStack() as own:
            experts(nc, Room(nc, own, whole), m, psum, wa, wb)
        with ExitStack() as own:
            finish(nc, Room(nc, own, whole), m, psum, out.rearrange("b t d -> (b t) d"))


_INS = ["x", "ctx_1024", "L0_xattn_Wq", "L0_xattn_Wkv", "L0_attn_Wq", "L0_attn_Wk", "L0_attn_Wv", "L0_ffn_W1",
        "L0_ffn_b1", "L0_ffn_W2", "L0_ffn_b2", "L0_ffn_Wa", "L0_ffn_Wb"]
_OUTS = [((128, 32, 256), "float32")]


def kernel(**inputs):
    import numpy as _np
    import concourse.bacc as _bacc
    from concourse import mybir as _mybir
    from concourse.bass_utils import run_bass_kernel_spmd as _run

    nc = _bacc.Bacc("TRN2", target_bir_lowering=False, num_devices=1)
    arrays, args = {}, []
    for name in _INS:
        a = _np.ascontiguousarray(inputs[name])
        arrays[f"in_{name}_dram"] = a
        args.append(nc.dram_tensor(f"in_{name}_dram", a.shape, _mybir.dt.from_np(a.dtype), kind="ExternalInput").ap())
    for i, (shape, dtype) in enumerate(_OUTS):
        dt = _mybir.dt.from_np(_np.dtype(dtype))
        args.append(nc.dram_tensor(f"out_{i}_dram", shape, dt, kind="ExternalOutput").ap())
    program(nc, *args)
    r = _run(nc, [arrays], core_ids=[0])
    return r.results[0]["out_0_dram"]
```
